# Optimizing a Trainium2 kernel written in Bass

```python
import numpy as np
import jax
import jax.numpy as jnp

def _softmax(x, axis=-1):
    return jax.nn.softmax(x, axis=axis)

def _gelu(x):
    return jax.nn.gelu(x, approximate=True)

def _silu(x):
    return jax.nn.silu(x)

def _sigmoid(x):
    return jax.nn.sigmoid(x)

def _layernorm(x, axis=-1, eps=1e-05):
    m = jnp.mean(x, axis=axis, keepdims=True)
    v = jnp.var(x, axis=axis, keepdims=True)
    return (x - m) / jnp.sqrt(v + eps)

def _scatter_add(tgt, idx, src, axis=0):
    return tgt.at[idx].add(src)

def _segment_sum(src, seg, n):
    return jax.ops.segment_sum(src, seg, n)
kernel_name = 'mk_decoder_preln_d1_seqx_r4_a3d8ae'

def setup_inputs(seed: int=0):
    np.random.seed(seed)
    _w = jnp.asarray

    def _rec_inputs():
        import jax
        import jax.numpy as jnp
        _rk = jax.random.key(seed)
        x = 2.818e-05 + 1 * jax.random.normal(jax.random.fold_in(_rk, 1), (4, 512, 512), jnp.float32)
        _lenS = 512 - jax.random.randint(jax.random.fold_in(_rk, 7), (4,), 0, max(1, 512 // 4) + 1, jnp.int32)
        _lenS2 = 512 - jax.random.randint(jax.random.fold_in(_rk, 8), (4,), 0, max(1, 512 // 4) + 1, jnp.int32)
        _ctx_1024P = jax.random.normal(jax.random.fold_in(_rk, 11), (4, 16, 256), jnp.float32)
        _ctx_1024c = jax.random.dirichlet(jax.random.fold_in(_rk, 511), 0.3 * jnp.ones((16,), jnp.float32), (4, 512))
        _ctx_1024t = jnp.einsum('bsk,bkd->bsd', _ctx_1024c, _ctx_1024P)
        _ctx_1024t = _ctx_1024t * jax.lax.rsqrt(jnp.mean(jnp.square(_ctx_1024t)) + 1e-12) * 0.953939
        ctx_1024 = 7.22013e-05 + 1.00017 * (_ctx_1024t + 0.3 * jax.random.normal(jax.random.fold_in(_rk, 611), (4, 512, 256), jnp.float32))
        return (x, ctx_1024)
    x, ctx_1024 = _rec_inputs()

    def _L0_attn_setup():
        import jax, jax.numpy as jnp
        import numpy as np
        HIDDEN = 512
        HEAD_DIM = 128
        NUM_HEADS = 8
        NUM_HH = 2
        CONV = 4
        EPS = 1e-05
        KEY_DIM = NUM_HEADS * HEAD_DIM

        def _causal_conv_silu(x, w):
            y = jax.lax.conv_general_dilated(jnp.swapaxes(x, 1, 2), w, window_strides=(1,), padding=[(w.shape[-1] - 1, 0)], feature_group_count=w.shape[0], dimension_numbers=('NCH', 'OIH', 'NCH'))
            return jnp.swapaxes(jax.nn.silu(y), 1, 2)

        def _l2norm(x):
            n = jnp.sqrt(jnp.sum(x * x, axis=-1, keepdims=True))
            return x / jnp.maximum(n, 1e-12)

        def _reference_tuple_inner(x, Wq, Wk, Wv, Wb, Wa, A_log, dt_bias, conv_q_w, conv_k_w, conv_v_w, Wg, norm_w, Wo):
            B, L, _ = x.shape
            H, Dh, nh = (NUM_HEADS, HEAD_DIM, NUM_HH)
            q = _causal_conv_silu(x @ Wq, conv_q_w).reshape(B, L, H, Dh)
            k = _causal_conv_silu(x @ Wk, conv_k_w).reshape(B, L, nh, H, Dh)
            v = _causal_conv_silu(x @ Wv, conv_v_w).reshape(B, L, nh, H, Dh)
            q = _l2norm(q) / np.float32(np.sqrt(Dh))
            k = _l2norm(k)
            beta = 2.0 * jax.nn.sigmoid(x @ Wb).reshape(B, L, nh, H)
            g = -jnp.exp(A_log) * jax.nn.softplus(x @ Wa + dt_bias)

            def step(state, inp):
                q_t, k_t, v_t, b_t, g_t = inp
                state = state * jnp.exp(g_t)[..., None, None]
                for j in range(nh):
                    kj = k_t[:, j]
                    corr = jnp.einsum('bhk,bhkv->bhv', kj, state)
                    u = (v_t[:, j] - corr) * b_t[:, j][..., None]
                    state = state + jnp.einsum('bhk,bhv->bhkv', kj, u)
                o_t = jnp.einsum('bhk,bhkv->bhv', q_t, state)
                return (state, o_t)
            state0 = jnp.zeros((B, H, Dh, Dh), x.dtype)
            xs = (jnp.moveaxis(q, 1, 0), jnp.moveaxis(k, 1, 0), jnp.moveaxis(v, 1, 0), jnp.moveaxis(beta, 1, 0), jnp.moveaxis(g, 1, 0))
            state, o = jax.lax.scan(step, state0, xs)
            o = jnp.moveaxis(o, 0, 1)
            gate = (x @ Wg).reshape(B, L, H, Dh)
            o = o * jax.lax.rsqrt(jnp.mean(o * o, axis=-1, keepdims=True) + EPS)
            o = o * norm_w * jax.nn.silu(gate)
            out = o.reshape(B, L, H * Dh) @ Wo
            return (out, state)
        key = jax.random.key(seed)
        ks = jax.random.split(key, 14)
        B, L = (2, 128)
        s = 0.02
        x = jax.random.normal(ks[0], (B, L, HIDDEN), jnp.float32)
        Wq = jax.random.normal(ks[1], (HIDDEN, KEY_DIM), jnp.float32) * s
        Wk = jax.random.normal(ks[2], (HIDDEN, KEY_DIM * NUM_HH), jnp.float32) * s
        Wv = jax.random.normal(ks[3], (HIDDEN, KEY_DIM * NUM_HH), jnp.float32) * s
        Wb = jax.random.normal(ks[4], (HIDDEN, NUM_HEADS * NUM_HH), jnp.float32) * s
        Wa = jax.random.normal(ks[5], (HIDDEN, NUM_HEADS), jnp.float32) * s
        A_log = jnp.log(jax.random.uniform(ks[6], (NUM_HEADS,), jnp.float32, 0.001, 16.0))
        dt = jnp.exp(jax.random.uniform(ks[7], (NUM_HEADS,), jnp.float32) * (np.float32(np.log(0.1)) - np.float32(np.log(0.001))) + np.float32(np.log(0.001)))
        dt = jnp.maximum(dt, 0.0001)
        dt_bias = dt + jnp.log(-jnp.expm1(-dt))
        conv_q_w = jax.random.normal(ks[8], (KEY_DIM, 1, CONV), jnp.float32) * 0.1
        conv_k_w = jax.random.normal(ks[9], (KEY_DIM * NUM_HH, 1, CONV), jnp.float32) * 0.1
        conv_v_w = jax.random.normal(ks[10], (KEY_DIM * NUM_HH, 1, CONV), jnp.float32) * 0.1
        Wg = jax.random.normal(ks[11], (HIDDEN, KEY_DIM), jnp.float32) * s
        norm_w = jnp.ones((HEAD_DIM,), jnp.float32)
        Wo = jax.random.normal(ks[12], (KEY_DIM, HIDDEN), jnp.float32) * s
        return dict(x=x, Wq=Wq, Wk=Wk, Wv=Wv, Wb=Wb, Wa=Wa, A_log=A_log, dt_bias=dt_bias, conv_q_w=conv_q_w, conv_k_w=conv_k_w, conv_v_w=conv_v_w, Wg=Wg, norm_w=norm_w, Wo=Wo)
    _L0_attn_all = _L0_attn_setup()
    _L0_attn_in = {k: v for k, v in _L0_attn_all.items() if k in ('Wq', 'Wk', 'Wv', 'Wb', 'Wa', 'A_log', 'dt_bias', 'conv_q_w', 'conv_k_w', 'conv_v_w', 'Wg', 'norm_w', 'Wo')}
    del _L0_attn_all

    def _L0_xattn_setup():
        import jax, jax.numpy as jnp
        import numpy as np
        B_, L_, D_MODEL = (4, 512, 256)
        D_STATE, D_CONV, EXPAND = (16, 4, 2)
        D_INNER = EXPAND * D_MODEL
        DT_RANK = (D_MODEL + 15) // 16

        def silu(x):
            return x * jax.nn.sigmoid(x)
        key = jax.random.key(seed)
        ks = jax.random.split(key, 10)
        f32 = jnp.float32
        hidden_states = jax.random.normal(ks[0], (B_, L_, D_MODEL), dtype=f32)
        z = jax.random.normal(ks[1], (B_, D_INNER, L_), dtype=f32)
        in_proj_w = jax.random.normal(ks[2], (D_INNER, D_MODEL), dtype=f32) * 0.02
        conv_w = jax.random.normal(ks[3], (D_INNER, 1, D_CONV), dtype=f32) * 0.1
        conv_b = jax.random.normal(ks[4], (D_INNER,), dtype=f32) * 0.02
        x_proj_w = jax.random.normal(ks[5], (DT_RANK + 2 * D_STATE, D_INNER), dtype=f32) * 0.02
        dt_proj_w = jax.random.uniform(ks[6], (D_INNER, DT_RANK), dtype=f32, minval=-DT_RANK ** (-0.5), maxval=DT_RANK ** (-0.5))
        dt = jnp.exp(jax.random.uniform(ks[7], (D_INNER,), dtype=f32, minval=np.log(0.001), maxval=np.log(0.1)))
        dt_proj_b = jnp.log(jnp.expm1(dt))
        A_log = jnp.log(jnp.broadcast_to(jnp.arange(1, D_STATE + 1, dtype=f32), (D_INNER, D_STATE)))
        D = jnp.ones((D_INNER,), f32)
        return {'hidden_states': hidden_states, 'z': z, 'in_proj_w': in_proj_w, 'conv_w': conv_w, 'conv_b': conv_b, 'x_proj_w': x_proj_w, 'dt_proj_w': dt_proj_w, 'dt_proj_b': dt_proj_b, 'A_log': A_log, 'D': D}
    _L0_xattn_all = _L0_xattn_setup()
    _L0_xattn_in = {k: v for k, v in _L0_xattn_all.items() if k in ('in_proj_w', 'conv_w', 'conv_b', 'x_proj_w', 'dt_proj_w', 'dt_proj_b', 'A_log', 'D')}
    del _L0_xattn_all

    def _L0_ffn_setup():
        import jax, jax.numpy as jnp
        import numpy as np
        D_MODEL = 512
        D_FF = 352
        N_EXPERTS = 6
        TOP_K = 2
        B, S = (8, 1024)
        key = jax.random.key(seed)
        ks = jax.random.split(key, 6)
        x = jax.random.normal(ks[0], (B, S, D_MODEL), dtype=jnp.float32)
        W1 = jax.random.normal(ks[1], (N_EXPERTS, D_MODEL, D_FF), dtype=jnp.float32) * 0.02
        b1 = jax.random.normal(ks[2], (N_EXPERTS, D_FF), dtype=jnp.float32) * 0.02
        W2 = jax.random.normal(ks[3], (N_EXPERTS, D_FF, D_MODEL), dtype=jnp.float32) * 0.02
        b2 = jax.random.normal(ks[4], (N_EXPERTS, D_MODEL), dtype=jnp.float32) * 0.02
        gate_W = jax.random.normal(ks[5], (N_EXPERTS, D_MODEL), dtype=jnp.float32) * 0.02
        return {'x': x, 'gate_W': gate_W, 'W1': W1, 'b1': b1, 'W2': W2, 'b2': b2}
    _L0_ffn_all = _L0_ffn_setup()
    _L0_ffn_in = {k: v for k, v in _L0_ffn_all.items() if k in ('gate_W', 'W1', 'b1', 'W2', 'b2')}
    del _L0_ffn_all
    return {'x': x, 'ctx_1024': ctx_1024, 'L0_attn_Wq': _L0_attn_in['Wq'], 'L0_attn_Wk': _L0_attn_in['Wk'], 'L0_attn_Wv': _L0_attn_in['Wv'], 'L0_attn_Wb': _L0_attn_in['Wb'], 'L0_attn_Wa': _L0_attn_in['Wa'], 'L0_attn_A_log': _L0_attn_in['A_log'], 'L0_attn_dt_bias': _L0_attn_in['dt_bias'], 'L0_attn_conv_q_w': _L0_attn_in['conv_q_w'], 'L0_attn_conv_k_w': _L0_attn_in['conv_k_w'], 'L0_attn_conv_v_w': _L0_attn_in['conv_v_w'], 'L0_attn_Wg': _L0_attn_in['Wg'], 'L0_attn_norm_w': _L0_attn_in['norm_w'], 'L0_attn_Wo': _L0_attn_in['Wo'], 'L0_xattn_in_proj_w': _L0_xattn_in['in_proj_w'], 'L0_xattn_conv_w': _L0_xattn_in['conv_w'], 'L0_xattn_conv_b': _L0_xattn_in['conv_b'], 'L0_xattn_x_proj_w': _L0_xattn_in['x_proj_w'], 'L0_xattn_dt_proj_w': _L0_xattn_in['dt_proj_w'], 'L0_xattn_dt_proj_b': _L0_xattn_in['dt_proj_b'], 'L0_xattn_A_log': _L0_xattn_in['A_log'], 'L0_xattn_D': _L0_xattn_in['D'], 'L0_ffn_gate_W': _L0_ffn_in['gate_W'], 'L0_ffn_W1': _L0_ffn_in['W1'], 'L0_ffn_b1': _L0_ffn_in['b1'], 'L0_ffn_W2': _L0_ffn_in['W2'], 'L0_ffn_b2': _L0_ffn_in['b2']}

def reference(x, ctx_1024, L0_attn_Wq, L0_attn_Wk, L0_attn_Wv, L0_attn_Wb, L0_attn_Wa, L0_attn_A_log, L0_attn_dt_bias, L0_attn_conv_q_w, L0_attn_conv_k_w, L0_attn_conv_v_w, L0_attn_Wg, L0_attn_norm_w, L0_attn_Wo, L0_xattn_in_proj_w, L0_xattn_conv_w, L0_xattn_conv_b, L0_xattn_x_proj_w, L0_xattn_dt_proj_w, L0_xattn_dt_proj_b, L0_xattn_A_log, L0_xattn_D, L0_ffn_gate_W, L0_ffn_W1, L0_ffn_b1, L0_ffn_W2, L0_ffn_b2):
    import jax
    import jax.numpy as jnp

    def _L0_attn_ref(x, Wq, Wk, Wv, Wb, Wa, A_log, dt_bias, conv_q_w, conv_k_w, conv_v_w, Wg, norm_w, Wo):
        import jax, jax.numpy as jnp
        import numpy as np
        HIDDEN = 512
        HEAD_DIM = 128
        NUM_HEADS = 8
        NUM_HH = 2
        CONV = 4
        EPS = 1e-05
        KEY_DIM = NUM_HEADS * HEAD_DIM

        def _causal_conv_silu(x, w):
            y = jax.lax.conv_general_dilated(jnp.swapaxes(x, 1, 2), w, window_strides=(1,), padding=[(w.shape[-1] - 1, 0)], feature_group_count=w.shape[0], dimension_numbers=('NCH', 'OIH', 'NCH'))
            return jnp.swapaxes(jax.nn.silu(y), 1, 2)

        def _l2norm(x):
            n = jnp.sqrt(jnp.sum(x * x, axis=-1, keepdims=True))
            return x / jnp.maximum(n, 1e-12)

        def _reference_tuple_inner(x, Wq, Wk, Wv, Wb, Wa, A_log, dt_bias, conv_q_w, conv_k_w, conv_v_w, Wg, norm_w, Wo):
            B, L, _ = x.shape
            H, Dh, nh = (NUM_HEADS, HEAD_DIM, NUM_HH)
            q = _causal_conv_silu(x @ Wq, conv_q_w).reshape(B, L, H, Dh)
            k = _causal_conv_silu(x @ Wk, conv_k_w).reshape(B, L, nh, H, Dh)
            v = _causal_conv_silu(x @ Wv, conv_v_w).reshape(B, L, nh, H, Dh)
            q = _l2norm(q) / np.float32(np.sqrt(Dh))
            k = _l2norm(k)
            beta = 2.0 * jax.nn.sigmoid(x @ Wb).reshape(B, L, nh, H)
            g = -jnp.exp(A_log) * jax.nn.softplus(x @ Wa + dt_bias)

            def step(state, inp):
                q_t, k_t, v_t, b_t, g_t = inp
                state = state * jnp.exp(g_t)[..., None, None]
                for j in range(nh):
                    kj = k_t[:, j]
                    corr = jnp.einsum('bhk,bhkv->bhv', kj, state)
                    u = (v_t[:, j] - corr) * b_t[:, j][..., None]
                    state = state + jnp.einsum('bhk,bhv->bhkv', kj, u)
                o_t = jnp.einsum('bhk,bhkv->bhv', q_t, state)
                return (state, o_t)
            state0 = jnp.zeros((B, H, Dh, Dh), x.dtype)
            xs = (jnp.moveaxis(q, 1, 0), jnp.moveaxis(k, 1, 0), jnp.moveaxis(v, 1, 0), jnp.moveaxis(beta, 1, 0), jnp.moveaxis(g, 1, 0))
            state, o = jax.lax.scan(step, state0, xs)
            o = jnp.moveaxis(o, 0, 1)
            gate = (x @ Wg).reshape(B, L, H, Dh)
            o = o * jax.lax.rsqrt(jnp.mean(o * o, axis=-1, keepdims=True) + EPS)
            o = o * norm_w * jax.nn.silu(gate)
            out = o.reshape(B, L, H * Dh) @ Wo
            return (out, state)
        return _reference_tuple_inner(x, Wq, Wk, Wv, Wb, Wa, A_log, dt_bias, conv_q_w, conv_k_w, conv_v_w, Wg, norm_w, Wo)[0]

    def _L0_xattn_ref(hidden_states, z, in_proj_w, conv_w, conv_b, x_proj_w, dt_proj_w, dt_proj_b, A_log, D):
        import jax, jax.numpy as jnp
        import numpy as np
        B_, L_, D_MODEL = (4, 512, 256)
        D_STATE, D_CONV, EXPAND = (16, 4, 2)
        D_INNER = EXPAND * D_MODEL
        DT_RANK = (D_MODEL + 15) // 16

        def silu(x):
            return x * jax.nn.sigmoid(x)
        Bsz, L, _ = hidden_states.shape
        d_inner, _, d_conv = conv_w.shape
        dt_rank = dt_proj_w.shape[1]
        d_state = A_log.shape[1]
        x = jnp.einsum('bld,ed->bel', hidden_states, in_proj_w)
        xc = jax.lax.conv_general_dilated(x, conv_w, window_strides=(1,), padding=[(d_conv - 1, 0)], feature_group_count=d_inner, dimension_numbers=('NCH', 'OIH', 'NCH'))
        x = silu(xc + conv_b[None, :, None])
        x_dbl = jnp.einsum('bdl,ed->bel', x, x_proj_w)
        dt_low, Bm, Cm = jnp.split(x_dbl, [dt_rank, dt_rank + d_state], axis=1)
        dt = jnp.einsum('brl,dr->bdl', dt_low, dt_proj_w)
        dt = jax.nn.softplus(dt + dt_proj_b[None, :, None])
        A = -jnp.exp(A_log)
        dt_t = jnp.moveaxis(dt, -1, 0)
        B_t = jnp.moveaxis(Bm, -1, 0)
        C_t = jnp.moveaxis(Cm, -1, 0)
        u_t = jnp.moveaxis(x, -1, 0)

        def step(state, inp):
            d, b, c, u = inp
            dA = jnp.exp(d[..., None] * A)
            state = state * dA + (d * u)[..., None] * b[:, None, :]
            y = jnp.einsum('bdn,bn->bd', state, c)
            return (state, y)
        state0 = jnp.zeros((Bsz, d_inner, d_state), x.dtype)
        _, ys = jax.lax.scan(step, state0, (dt_t, B_t, C_t, u_t))
        y = jnp.moveaxis(ys, 0, 2)
        y = y + D[None, :, None] * x
        y = y * silu(z)
        return jnp.swapaxes(y, 1, 2)

    def _L0_ffn_ref(x, gate_W, W1, b1, W2, b2):
        import jax, jax.numpy as jnp
        import numpy as np
        D_MODEL = 512
        D_FF = 352
        N_EXPERTS = 6
        TOP_K = 2
        B, S = (8, 1024)
        gate_logits = jnp.einsum('bd,ed->be', x.mean(axis=1), gate_W)
        gate_probs = jax.nn.softmax(gate_logits, axis=-1)
        topk_vals, topk_idx = jax.lax.top_k(gate_probs, TOP_K)
        topk_vals = topk_vals / topk_vals.sum(axis=-1, keepdims=True)
        W1g = W1[topk_idx]
        b1g = b1[topk_idx]
        W2g = W2[topk_idx]
        b2g = b2[topk_idx]
        h = jnp.einsum('bsd,bkdf->bksf', x, W1g) + b1g[:, :, None, :]
        h = jax.nn.gelu(h, approximate=False)
        eo = jnp.einsum('bksf,bkfd->bksd', h, W2g) + b2g[:, :, None, :]
        return jnp.einsum('bk,bksd->bsd', topk_vals, eo)
    x = x + _L0_attn_ref(_layernorm(x, axis=-1), L0_attn_Wq, L0_attn_Wk, L0_attn_Wv, L0_attn_Wb, L0_attn_Wa, L0_attn_A_log, L0_attn_dt_bias, L0_attn_conv_q_w, L0_attn_conv_k_w, L0_attn_conv_v_w, L0_attn_Wg, L0_attn_norm_w, L0_attn_Wo)
    x = x + _L0_xattn_ref(ctx_1024, _layernorm(x, axis=-1), L0_xattn_in_proj_w, L0_xattn_conv_w, L0_xattn_conv_b, L0_xattn_x_proj_w, L0_xattn_dt_proj_w, L0_xattn_dt_proj_b, L0_xattn_A_log, L0_xattn_D)
    x = x + _L0_ffn_ref(_layernorm(x, axis=-1), L0_ffn_gate_W, L0_ffn_W1, L0_ffn_b1, L0_ffn_W2, L0_ffn_b2)
    return x

_drawn_inputs = setup_inputs


def setup_inputs(seed=0):
    import zlib

    import numpy as np

    out = dict(_drawn_inputs(seed))
    spreads = {'L0_attn_norm_w': (1.0, 0.6), 'L0_xattn_D': (1.0, 0.6)}
    factors = {'ctx_1024': 2.906,
     'L0_attn_Wb': 3.1,
     'L0_attn_Wa': 8.0,
     'L0_xattn_in_proj_w': 2.911,
     'L0_xattn_conv_w': 2.97,
     'L0_xattn_conv_b': 8.0,
     'L0_xattn_x_proj_w': 8.0,
     'L0_xattn_dt_proj_w': 8.0,
     'L0_xattn_dt_proj_b': 8.0,
     'L0_xattn_A_log': 8.0,
     'L0_ffn_b1': 200.0,
     'L0_ffn_b2': 200.0,
     'L0_attn_A_log': 3.675,
     'L0_attn_dt_bias': 2.786,
     'L0_ffn_gate_W': 8.0,
     'L0_ffn_W1': 8.0,
     'L0_ffn_W2': 8.0}
    for name, (base, spread) in spreads.items():
        noise = np.random.default_rng([zlib.crc32(name.encode()), seed]).standard_normal(out[name].shape)
        drawn = base * np.exp(spread * noise) if base else spread * noise
        out[name] = jnp.asarray(drawn.astype(out[name].dtype))
    for name, factor in factors.items():
        out[name] = (out[name] * factor).astype(out[name].dtype)
    return out
```

```python
from contextlib import ExitStack

import concourse.bass as bass
from concourse import mybir
from concourse.bass import ds

F32 = mybir.dt.float32
BF16 = mybir.dt.bfloat16
U32 = mybir.dt.uint32
ALU = mybir.AluOpType
ACT = mybir.ActivationFunctionType
AX = mybir.AxisListType

P = 128
B, L, HID = 4, 512, 512
KT = HID // P
H, DH, NHH = 8, 128, 2
TAPS = 4
CT = 64
CM = CT * NHH
NC = L // CT
NIT = H * NC
LV = 7
PAD = TAPS - 1
TW = L + PAD
EPS = 1e-5
NTT = B * L // P
NG = NHH * H + H
DI, DS, DR = 512, 16, 16
DT = DI // P
CTXT = 2
NE, FF = 6, 352
FT = [(0, 128), (128, 128), (256, 96)]


def log1p_coefficients():
    import numpy as np
    deg = 9
    k = np.arange(400)
    e = (1 + np.cos(np.pi * (k + 0.5) / 400)) / 2
    f = np.log1p(e) / e
    c = np.polynomial.chebyshev.Chebyshev.fit(e, f, deg, domain=[0, 1])
    return [float(v) for v in c.convert(kind=np.polynomial.Polynomial).coef]


def at(n, off):
    def val(per, c):
        return n * per + (off * per + c)
    return val


def wait(eng, sem, value):
    if not (isinstance(value, int) and value <= 0):
        eng.wait_ge(sem, value)


def wait_apart(eng, passed, sem, value):
    if not (isinstance(value, int) and value <= 0):
        eng.wait_ge(sem, value)
        eng.sem_inc(passed, 1)


def state_inputs(nc, g):
    with ExitStack() as ctx:
        sb = lambda name, shape, dt=F32: ctx.enter_context(nc.sbuf_tensor(name, shape, dt))
        pb = lambda name, shape, dt=F32: ctx.enter_context(nc.psum_tensor(name, shape, dt))
        sem = lambda name: ctx.enter_context(nc.semaphore(name))
        ctxT = sb("ctxT", [P, CTXT, B * L])
        inw = sb("inw", [P, CTXT, DI])
        xw = sb("xw", [P, DT, DR + 2 * DS])
        dw = sb("dw", [DR, DI])
        cw = sb("scw", [P, DT, TAPS])
        cb = sb("scb", [P, DT])
        db = sb("sdb", [P, DT])
        dd = sb("sdd", [P, DT])
        acc = sb("acc", [P, DT, L])
        th = sb("sth", [P, DT, L])
        u2 = sb("u2", [P, DT, L])
        xd = sb("xd", [DR + 2 * DS, L])
        y = sb("sy", [P, DT, L])
        ya = sb("sya", [P, DT, L])
        e = sb("se", [P, DT, L])
        dt = sb("sdt", [P, DT, L])
        dtu = sb("sdtu", [P, DT, L])
        ud = sb("sud", [P, DT, L])
        px = pb("px", [P, DT, 512])
        pd = pb("pd", [P, 512])
        pt = pb("pt", [P, 2, 512])
        names = ("s_in", "in_done", "tap_done", "conv_link", "conv_done", "tanh_done", "u_done", "xd_done",
                 "xd_copied", "dt_done", "y_done", "abs_done", "e_done", "poly", "out_ready")
        s = {k: sem("si_" + k) for k in names}
        out_dma = sem("si_out")
        NP = len(g.log1p) + 1

        with nc.Block() as block:
            @block.sync
            def _(sp):
                for dst, src in ((ctxT, g.inputs["ctxT"]), (inw, g.inputs["in_w"]), (cw, g.inputs["s_conv"]), (cb, g.inputs["s_convb"]), (xw, g.inputs["x_w"]),
                                 (dw, g.inputs["dt_w"]), (db, g.inputs["dt_b"]), (dd, g.inputs["s_d"])):
                    sp.dma_start(dst[:], src).then_inc(s["s_in"], 16)
                def batch(b):
                    one = slice(b, b + 1) if isinstance(b, int) else ds(b, 1)
                    sp.wait_ge(s["xd_copied"], b + 1)
                    sp.dma_start(g.bc_dram[one].rearrange("b k l -> (b k) l"), xd[DR:, :]).then_inc(out_dma, 16)
                    sp.wait_ge(s["out_ready"], b + 1)
                    for dst, src in ((g.dts_dram[one, :, 0], dt), (g.dts_dram[one, :, 1], dtu), (g.ud_dram[one], ud)):
                        sp.dma_start(dst.rearrange("b t p l -> p (b t) l"), src[:]).then_inc(out_dma, 16)

                batch(0)
                with sp.Fori(1, B) as b:
                    batch(b)
                sp.wait_ge(out_dma, 16 * 4 * B)

            @block.tensor
            def _(pe):
                pe.wait_ge(s["s_in"], 16 * 8)
                def batch(b):
                    for t in range(DT):
                        wait(pe, s["conv_done"], b * DT)
                        for k in range(CTXT):
                            i = pe.matmul(px[:, t, :], inw[:, k, t * P:(t + 1) * P], ctxT[:, k, b * L:(b + 1) * L] if isinstance(b, int) else ctxT[:, k, ds(b * L, L)],
                                          start=(k == 0), stop=(k == CTXT - 1))
                        i.then_inc(s["in_done"], 1)
                    pe.wait_ge(s["u_done"], b + 1)
                    for t in range(DT):
                        i = pe.matmul(pd[0:DR + 2 * DS, :], xw[:, t, :], u2[:, t, :], start=(t == 0), stop=(t == DT - 1))
                    i.then_inc(s["xd_done"], 1)
                    pe.wait_ge(s["xd_copied"], b + 1)
                    for t in range(DT):
                        if t > 1:
                            pe.wait_ge(s["y_done"], b * DT + (t - 1))
                        pe.matmul(pt[:, t % 2, :], dw[:, t * P:(t + 1) * P], xd[0:DR, :], start=True, stop=True)\
                            .then_inc(s["dt_done"], 1)

                batch(0)
                with pe.Fori(1, B) as b:
                    batch(b)

            @block.scalar
            def _(act):
                act.wait_ge(s["s_in"], 16 * 8)
                def batch(b):
                    for t in range(DT):
                        act.wait_ge(s["in_done"], b * DT + (t + 1))
                        wait(act, s["u_done"], b)
                        act.activation(acc[:, t, :], px[:, t, :], ACT.Identity, bias=cb[:, t:t + 1],
                                       scale=cw[:, t, PAD:TAPS]).then_inc(s["tap_done"], 1)
                    act.wait_ge(s["conv_done"], b * DT + DT)
                    act.activation(th[:], acc[:], ACT.Tanh, scale=0.5).then_inc(s["tanh_done"], 1)
                    act.wait_ge(s["xd_done"], b + 1)
                    wait(act, out_dma, b * 64)
                    act.activation(xd[:, :], pd[0:DR + 2 * DS, :], ACT.Copy, scale=0.5).then_inc(s["xd_copied"], 1)
                    for t in range(DT):
                        act.wait_ge(s["dt_done"], b * DT + (t + 1))
                        wait(act, s["out_ready"], b)
                        act.activation(y[:, t, :], pt[:, t % 2, :], ACT.Identity, bias=db[:, t:t + 1])\
                            .then_inc(s["y_done"], 1)
                    act.wait_ge(s["y_done"], b * DT + DT)
                    act.activation(ya[:], y[:], ACT.Abs).then_inc(s["abs_done"], 1)
                    act.wait_ge(s["abs_done"], b + 1)
                    act.activation(e[:], ya[:], ACT.Exp, scale=-1.0).then_inc(s["e_done"], 1)

                batch(0)
                with act.Fori(1, B) as b:
                    batch(b)

            @block.vector
            def _(dve):
                def batch(b):
                    for t in range(DT):
                        dve.wait_ge(s["tap_done"], b * DT + (t + 1))
                        for k in range(1, TAPS):
                            i = dve.scalar_tensor_tensor(acc[:, t, k:], px[:, t, 0:L - k], cw[:, t, PAD - k:TAPS - k],
                                                         acc[:, t, k:], ALU.mult, ALU.add)
                            if k < PAD:
                                i.then_inc(s["conv_link"], 1)
                                dve.wait_ge(s["conv_link"], b * (2 * DT) + (2 * t + k))
                        i.then_inc(s["conv_done"], 1)
                    dve.wait_ge(s["tanh_done"], b + 1)
                    dve.scalar_tensor_tensor(u2[:], th[:], 1.0, acc[:], ALU.add, ALU.mult).then_inc(s["u_done"], 1)
                    dve.wait_ge(s["e_done"], b + 1)
                    wait(dve, out_dma, b * 64)
                    dve.tensor_scalar(dt[:], e[:], g.log1p[-1], None, ALU.mult).then_inc(s["poly"], 1)
                    for k, c in enumerate(g.log1p[-2::-1]):
                        dve.wait_ge(s["poly"], b * NP + (k + 1))
                        dve.scalar_tensor_tensor(dt[:], dt[:], c, e[:], ALU.add, ALU.mult).then_inc(s["poly"], 1)
                    dve.wait_ge(s["poly"], b * NP + (NP - 1))
                    dve.scalar_tensor_tensor(dt[:], y[:], 0.0, dt[:], ALU.max, ALU.add).then_inc(s["poly"], 1)
                    for t in range(DT):
                        dve.tensor_scalar(ud[:, t, :], u2[:, t, :], dd[:, t:t + 1], 0.5, ALU.mult, ALU.mult)
                    dve.wait_ge(s["poly"], b * NP + NP)
                    dve.scalar_tensor_tensor(dtu[:], u2[:], 0.5, dt[:], ALU.mult, ALU.mult).then_inc(s["out_ready"], 1)

                batch(0)
                with dve.Fori(1, B) as b:
                    batch(b)


def prepare(nc, g):
    with ExitStack() as ctx:
        sb = lambda name, shape, dt=F32: ctx.enter_context(nc.sbuf_tensor(name, shape, dt))
        pb = lambda name, shape, dt=F32: ctx.enter_context(nc.psum_tensor(name, shape, dt))
        sem = lambda name: ctx.enter_context(nc.semaphore(name))
        xin = sb("xin", [P, NTT, HID])
        xhat = sb("xhat", [P, 2, HID])
        stats = sb("stats", [P, 2, 6])
        mv = sb("mv", [P, NTT, 2])
        rstd = sb("rstd", [P, NTT])
        wg = sb("wg", [P, KT, NG])
        logitT = sb("logitT", [NG, B * L, NHH])
        bias_bc = sb("bias_bc", [P, H])
        alog_bc = sb("alog_bc", [P, H])
        expa = sb("expa", [P, H])
        parity = sb("parity", [P, 2])
        first = sb("first", [P, NIT])
        flag = sb("flag", [P, NIT])
        neg = sb("neg32", [P, CM])
        negq = sb("negq32", [P, CT])
        ssa = sb("ssa", [P, DT * DS])
        raw = sb("raw", [P, B * NC, NG])
        y = sb("y", [P, 2, B * NC, H])
        ya = sb("ya", [P, 2, B * NC, H])
        e = sb("e", [P, 2, B * NC, H])
        sp = sb("sp", [P, 2, B * NC, H])
        decay = sb("decay", [P, H, NC, B])
        eG = sb("eG", [P, NIT, B])
        psT = pb("psT", [P, 2, 512])
        psL = pb("psL", [P, 512])
        psR = pb("psR", [P, 2, 512])
        psG = pb("psG", [P, 3, 512])
        x_in, c_in, var_ready, rstd_ready, xhat_ready, t_ready, xT_ready = map(
            sem, ("x_in", "c_in", "var_ready", "rstd_ready", "xhat_ready", "t_ready", "xT_ready"))
        lg_ready, lg_copied, raw_ready, raw_copied, act1, dve1, cum_ready, done_a = map(
            sem, ("lg_ready", "lg_copied", "raw_ready", "raw_copied", "act1", "dve1", "cum_ready", "done_a"))
        chain = sem("prep_chain")
        act_chain = sem("act_chain")
        st_link = sem("st_link")

        with nc.Block() as block:
            @block.sync
            def _(sp_):
                sp_.dma_start(xin[:, :, :], g.inputs["x"].rearrange("(n p) d -> p n d", p=P)).then_inc(x_in, 16)
                for dst, src in ((g.ident, g.inputs["c_ident"]), (g.upto, g.inputs["c_upto"]), (g.after, g.inputs["c_after"]),
                                 (g.ones, g.inputs["c_ones"]), (neg, g.inputs["c_neg"]), (negq, g.inputs["c_negq"]),
                                 (g.levels, g.inputs["c_levels"]), (wg, g.inputs["w_gates"]),
                                 (parity, g.inputs["c_parity"]), (first, g.inputs["c_first"]), (flag, g.inputs["c_flag"]), (ssa, g.inputs["s_alog"]), (g.normw, g.inputs["norm_w"])):
                    sp_.dma_start(dst[:], src).then_inc(c_in, 16)
                sp_.dma_start(bias_bc[:, :], g.inputs["dt_bias"].partition_broadcast(P)).then_inc(c_in, 16)
                sp_.dma_start(alog_bc[:, :], g.inputs["a_log"].partition_broadcast(P)).then_inc(c_in, 16)
            CONSTS = 16 * 15

            @block.vector
            def _(dve):
                dve.wait_ge(x_in, 16)
                for t in range(NTT):
                    dve.bn_stats(stats[:, t % 2, :], xin[:, t, :]).then_inc(st_link, 1)
                    dve.wait_ge(st_link, t + 1)
                    i = dve.bn_aggr(mv[:, t, :], stats[:, t % 2, :])
                i.then_inc(var_ready, 1)
                dve.wait_ge(var_ready, 1)
                dve.tensor_scalar(rstd[:, :], mv[:, :, 1], EPS, None, ALU.add).then_inc(var_ready, 1)
                dve.memset(g.xT[:, :, :, 0:PAD], 0.0)
                dve.wait_ge(rstd_ready, 1)
                for t in range(NTT):
                    wait(dve, t_ready, t - 1)
                    dve.tensor_scalar(xhat[:, t % 2, :], xin[:, t, :], mv[:, t, 0:1], rstd[:, t:t + 1],
                                      ALU.subtract, ALU.mult).then_inc(xhat_ready, 1)
                for k in range(2):
                    dve.wait_ge(raw_ready, k + 1)
                    i = dve.tensor_copy(raw[:, 16 * k:16 * k + 16, :],
                                        psR[:, k, 0:16 * NG].rearrange("p (n c) -> p n c", c=NG))
                i.then_inc(chain, 1)
                dve.wait_ge(chain, 1)
                dve.wait_ge(c_in, CONSTS)
                k = [1]

                def link(ins):
                    k[0] += 1
                    ins.then_inc(chain, 1)
                    dve.wait_ge(chain, k[0])

                bc = lambda a: a.unsqueeze(1).to_broadcast([P, B * NC, H])
                link(dve.tensor_tensor(y[:, 0], raw[:, :, 2 * H:3 * H], bc(bias_bc[:, :]), ALU.add))
                link(dve.tensor_scalar(y[:, 1], raw[:, :, 0:H], parity[:, 0:1], -1.0, ALU.mult, ALU.mult))
                link(dve.tensor_scalar(ya[:, 1], raw[:, :, H:2 * H], parity[:, 1:2], -1.0, ALU.mult, ALU.mult))
                link(dve.tensor_tensor(y[:, 1], y[:, 1], ya[:, 1], ALU.add))
                i = dve.tensor_scalar(ya[:], y[:], -1.0, None, ALU.mult)
                link(i)
                link(dve.tensor_tensor(ya[:], ya[:], y[:], ALU.min))
                dve.nop().then_inc(dve1, 1)
                dve.wait_ge(act1, 2)
                link(dve.tensor_scalar(sp[:], e[:], g.log1p[-1], None, ALU.mult))
                for c in g.log1p[-2::-1]:
                    link(dve.scalar_tensor_tensor(sp[:], sp[:], c, e[:], ALU.add, ALU.mult))
                link(dve.scalar_tensor_tensor(sp[:], y[:], 0.0, sp[:], ALU.max, ALU.add))
                link(dve.tensor_tensor(sp[:, 0], sp[:, 0], bc(expa[:, :]), ALU.mult))
                dv = decay[:, :, :, :].rearrange("p h c b -> p b c h")
                link(dve.tensor_scalar(dv, sp[:, 0].rearrange("p (b c) h -> p b c h", b=B),
                                       parity[:, 0:1], -1.0, ALU.mult, ALU.mult))
                tb = g.tab[:, :, :].rearrange("p (h c) k -> p h c k", h=H)
                for b in range(B):
                    sv = sp[:, 1].rearrange("p (b c) h -> p b h c", b=B)[:, b]
                    dve.tensor_scalar(tb[:, :, :, 4 + b], sv, -1.0, g.ln2, ALU.mult, ALU.add)
                    dve.tensor_scalar(tb[:, :, :, 8 + b], sv, -1.0, None, ALU.mult)
                    i = dve.tensor_copy(tb[:, :, :, b], decay[:, :, :, b])
                link(i)
                dve.nop().then_inc(dve1, 1)
                dve.wait_ge(act1, 3)
                f4 = first[:, :].unsqueeze(2).to_broadcast([P, NIT, B])
                link(dve.scalar_tensor_tensor(eG[:], eG[:], -2.0, f4, ALU.mult, ALU.mult))
                dve.tensor_tensor(g.tab[:, :, 12:16], eG[:], g.tab[:, :, 8:12], ALU.mult)
                dve.tensor_tensor(g.tab[:, :, 20:24], g.tab[:, :, 20:24], f4, ALU.mult)
                dve.tensor_tensor(g.tab[:, :, 24:26], g.tab[:, :, 24:26], f4[:, :, 0:2], ALU.mult)
                dve.tensor_scalar(g.normw[:, :], g.normw[:, :], 0.5, None, ALU.mult)
                dve.tensor_copy(g.tab[:, :, 26:27], flag[:, :].unsqueeze(2))
                dve.tensor_scalar(g.a_neg[:, :], ssa[:, :], -1.0, None, ALU.mult)
                dve.tensor_copy(g.identb[:, :], g.ident[:, :])
                dve.tensor_copy(g.neg[:].rearrange("p (b n) -> p b n", b=B), neg[:, :].unsqueeze(1).to_broadcast([P, B, CM]))
                dve.tensor_copy(g.negq[:].rearrange("p (b n) -> p b n", b=B), negq[:, :].unsqueeze(1).to_broadcast([P, B, CT]))
                for l in range(LV):
                    dve.tensor_copy(g.Xm[:, l], g.ident[:, :].unsqueeze(1).to_broadcast([P, B, P]))
                dve.memset(g.S[:, :, :], 0.0)

            @block.gpsimd
            def _(pool):
                pool.memset(g.mhalf[:, :], -0.5).then_inc(done_a, 1)
                pool.wait_ge(done_a, 1)
                pool.wait_ge(var_ready, 2)
                pool.tensor_tensor(rstd[:, :], rstd[:, :], g.mhalf[:, 0:NTT], ALU.pow).then_inc(rstd_ready, 1)

            @block.tensor
            def _(pe):
                pe.wait_ge(c_in, CONSTS)
                for t in range(NTT):
                    pe.wait_ge(xhat_ready, t + 1)
                    wait(pe, xT_ready, t - 1)
                    for k in range(KT):
                        i = pe.transpose(psT[:, t % 2, k * P:(k + 1) * P], xhat[:, t % 2, k * P:(k + 1) * P],
                                         g.ident[:, :])
                    i.then_inc(t_ready, 1)
                for b in range(B):
                    pe.wait_ge(xT_ready, NTT)
                    wait(pe, lg_copied, b)
                    for k in range(KT):
                        i = pe.matmul(psL[0:NG, :], wg[:, k, :], g.xT[:, k, b, PAD:], start=(k == 0), stop=(k == KT - 1))
                    i.then_inc(lg_ready, 1)
                pe.wait_ge(lg_copied, B)
                for n in range(B * NC):
                    src = logitT[:, n * CT:(n + 1) * CT, :].rearrange("p t j -> p (t j)")
                    i = pe.transpose(psR[:, n // 16, (n % 16) * NG:(n % 16 + 1) * NG], src, g.ident[0:NG, 0:NG])
                    if n % 16 == 15:
                        i.then_inc(raw_ready, 1)
                pe.wait_ge(dve1, 2)
                rhs = decay[:, :, :, :].rearrange("p h c b -> p (h c b)")
                pe.matmul(psG[:, 0, 0:256], g.upto[:, :], rhs, start=True, stop=True)
                pe.matmul(psG[:, 1, 0:256], g.after[:, :], rhs, start=True, stop=True)
                pe.matmul(psG[:, 2, 0:256], g.ones[:, :], rhs, start=True, stop=True)
                uq = g.upto[:, :].rearrange("p (t j) -> p t j", j=2)[:, :, 1]
                for h2 in range(2):
                    i = pe.matmul(psG[h2 * CT:(h2 + 1) * CT, 0, 256:384], uq,
                                  decay[:, :, :, h2::2].rearrange("p h c b -> p (h c) b"),
                                  start=True, stop=True, skip_group_check=True)
                i.then_inc(cum_ready, 1)

            @block.scalar
            def _(act):
                for t in range(NTT):
                    act.wait_ge(t_ready, t + 1)
                    tok = (t % (L // P)) * P
                    act.activation(g.xT[:, :, t // (L // P), PAD + tok:PAD + tok + P],
                                   psT[:, t % 2, :].rearrange("p (k n) -> p k n", k=KT),
                                   ACT.Copy).then_inc(xT_ready, 1)
                for b in range(B):
                    act.wait_ge(lg_ready, b + 1)
                    act.activation(logitT[:, b * L:(b + 1) * L, :],
                                   psL[0:NG, :].unsqueeze(2).to_broadcast([NG, L, NHH]), ACT.Copy).then_inc(lg_copied, 1)
                act.wait_ge(c_in, CONSTS)
                act.activation(ssa[:, :], ssa[:, :], ACT.Exp)
                act.activation(expa[:, :], alog_bc[:, :], ACT.Exp).then_inc(act1, 1)
                act.wait_ge(dve1, 1)
                act.activation(e[:], ya[:], ACT.Exp).then_inc(act1, 1)
                act.wait_ge(cum_ready, 1)
                v = lambda k: psG[:, k, 0:256].rearrange("p (n b) -> p n b", b=B)
                act.activation(eG[:], v(0), ACT.Exp)
                act.activation(g.tab[:, :, 16:20], v(1), ACT.Exp)
                act.activation(g.tab[:, :, 20:24], v(2), ACT.Exp)
                act.activation(g.tab[:, :, 8:12], g.tab[:, :, 8:12], ACT.Exp)
                act.activation(g.tab[:, :, 24:26], psG[:, 0, 256:384].rearrange("p (n b) -> p n b", b=2),
                               ACT.Exp).then_inc(act1, 1)


def delta(nc, g):
    with ExitStack() as ctx:
        sb = lambda name, shape, dt=F32: ctx.enter_context(nc.sbuf_tensor(name, shape, dt))
        pb = lambda name, shape, dt=F32: ctx.enter_context(nc.psum_tensor(name, shape, dt))
        sem = lambda name: ctx.enter_context(nc.semaphore(name))
        K0, V0, Q0, END = 0, B * CM, 2 * B * CM, 2 * B * CM + B * CT
        NO = 6
        W = sb("W", [P, NO, KT, P])
        cw = sb("cw", [P, NO - 1, TAPS])
        cv = sb("cv", [P, END])
        th = sb("th", [P, END])
        kvq = sb("kvq", [P, 2, END])
        gt = sb("gt", [P, B, CT])
        gs = sb("gs", [P, 2, B, CT])
        junk = sb("junk", [P, 8, P])
        sc = sb("sc", [P, 2, 27])
        ss = sb("ss", [P, 6])
        rr = sb("rr", [P, 6])
        rw = sb("rw", [P, B])
        rq = sb("rq", [P, 2, 2])
        Kn = sb("Kn", [P, B, DH])
        Kw = sb("Kw", [P, 2, B, DH])
        Vb = sb("Vb", [P, 2, B, DH])
        Qn = sb("Qn", [P, 2, 2, DH])
        KTr = sb("KTr", [P, 2, B, CM])
        QTr = sb("QTr", [P, 2, 2, 2, P])
        Dr = sb("Dr", [P, B, CM])
        Dt = sb("Dt", [P, B, CM])
        Dq = sb("Dq", [P, B, CT])
        E_ = sb("E_", [P, B, CM])
        Eq = sb("Eq", [P, B, CT])
        At = sb("At", [P, B, CM])
        PT = sb("PT", [P, 2, B, CT])
        Tb = sb("Tb", [P, B, CM])
        Rb = sb("Rb", [P, B, CM])
        Rf = sb("Rf", [P, 2, B, CM])
        F = sb("F", [P, B, DH])
        U = sb("U", [P, B, DH])
        oss = sb("oss", [P, 2])
        orr = sb("orr", [P, 2])
        On = sb("On", [P, 2, DH])
        OT = sb("OT", [P, 2, B, CT])
        dts = sb("dts", [P, 2, 2, L])
        bcq = sb("bcq", [P, 2, 4, L])
        da = sb("da", [P, 4, L])
        hs = sb("hs", [P, 4, L])
        ys = sb("ys", [P, DT, L])
        bank = [pb(f"bank{i}", [P, 512]) for i in range(8)]
        by_batch = lambda a: a[:, 0:512].rearrange("p (b n) -> p b n", b=B)
        pairs = lambda a: a.rearrange("p (b n) -> p b n", b=2)

        names = ("w_in", "proj_done", "tap_done", "conv_done", "gtanh_done", "tanh_done", "act_done",
                 "natural_done", "ss_done", "sc_done", "r_done", "dr_done", "kn_done", "qn_done", "turned",
                 "kt_done", "qt_done", "decay_done", "e_done", "gram_done", "at_done", "pt_done", "x_done",
                 "xm_done", "t_done", "tcopy_done", "rt_done", "rcopy_done", "ks_done", "f_done", "u_done",
                 "ucopy_done", "so_done", "s_done", "oss_done", "orr_done", "on_done", "ot_turned",
                 "ot_done", "conv_link", "pool_link_b", "pool_link_c", "bc_in", "ya_cleared",
                 "da_done", "bx_done", "scan_done", "hc_done", "ys_link", "ys_done")
        passed = {k: sem(f"passed_{k}") for k in ("sp", "pool", "dve")}
        s = {k: sem(k) for k in names}
        out_dma = [sem("out_dma0"), sem("out_dma1")]
        dt_in = [sem("dt_in0"), sem("dt_in1")]
        y_dma = sem("y_dma")
        seq = {0: K0, 1: K0, 2: V0, 3: V0}

        def loops(eng, body):
            body(eng, -2, 0, C=False, B_=False)
            body(eng, -1, 1, C=False)
            body(eng, 0, 0)
            body(eng, 1, 1)
            with eng.Fori(2, NIT - 2, 2) as i:
                for u in range(2):
                    body(eng, i + u, u)
            body(eng, NIT - 2, 0, A=False)
            body(eng, NIT - 1, 1, A=False, B_=False)

        def conv_out(o):
            if o == 4:
                return cv[:, Q0:END].rearrange("p (b t) -> p b t", b=B)
            return cv[:, seq[o]:seq[o] + B * CM].rearrange("p (b t j) -> p j b t", b=B, j=NHH)[:, o % 2]

        def proj_bank(o):
            return bank[o % 2][:, 0:B * (CT + PAD)].rearrange("p (b t) -> p b t", b=B)

        with nc.Block() as block:
            @block.sync
            def _(sp):
                def load(w):
                    one = slice(w, w + 1) if isinstance(w, int) else ds(w, 1)
                    sp.dma_start(W[:, :, :, :], g.inputs["w_heads"][one].rearrange("h p (o k n) -> p (h o) k n", o=NO, k=KT))\
                        .then_inc(s["w_in"], 16)
                    sp.dma_start(cw[:, :, :], g.inputs["conv_heads"][one].rearrange("h p (o k) -> p (h o) k", k=TAPS))\
                        .then_inc(s["w_in"], 16)

                def store(h, c, u):
                    sp.wait_ge(s["ot_done"], h * NC + (c + 1))
                    one = slice(h, h + 1) if isinstance(h, int) else ds(h, 1)
                    sp.dma_start(g.o_dram[one, :, :, c * CT:(c + 1) * CT].rearrange("o v b t -> v (o b) t"),
                                 OT[:, u]).then_inc(out_dma[u], 16)

                def scan_inputs(b, k):
                    n = b * 16 + k
                    wait(sp, s["da_done"], n - 1)
                    wait_apart(sp, passed["sp"], s["bx_done"], n - 1)
                    one = slice(b, b + 1) if isinstance(b, int) else ds(b, 1)
                    if k % 4 == 0:
                        wait(sp, s["hc_done"], n)
                        src = g.bc_dram[one].rearrange("b (i n) l -> (b i) n l", i=2)[:, k // 4 * 4:k // 4 * 4 + 4, :]
                        sp.dma_start(bcq[:], src.partition_broadcast(P)).then_inc(s["bc_in"], 16)
                    sp.dma_start(dts[:, k % 2], g.dts_dram[one, k % 4].rearrange("b i p l -> p (b i) l"))\
                        .then_inc(dt_in[k % 2], 16)

                def flush(b, t):
                    sp.wait_ge(s["ys_done"], b * 16 + (13 + t))
                    one = slice(b, b + 1) if isinstance(b, int) else ds(b, 1)
                    sp.dma_start(g.y_dram[one, t].rearrange("b p l -> p (b l)"), ys[:, t]).then_inc(y_dma, 16)

                def span(b, first):
                    for k in range(16):
                        if not (first and k < 2):
                            scan_inputs(b, k)
                        h, c = b * 2 + k // NC, k % NC
                        if c == NC - 3 and not (isinstance(b, int) and b == B - 1 and k >= NC):
                            sp.wait_ge(s["proj_done"], (h + 1) * (NC * NO))
                            sp.wait_ge(s["conv_done"], (h + 1) * (NC * NO))
                            load(h + 1)
                        store(h, c, c % 2)
                        if k > 12:
                            flush(b, k - 13)
                    flush(b, 3)

                sp.sem_inc(y_dma, 16 * DT)
                load(0)
                scan_inputs(0, 0)
                scan_inputs(0, 1)
                span(0, True)
                with sp.Fori(1, B - 1) as b:
                    span(b, False)
                span(B - 1, False)
                sp.wait_ge(y_dma, 16 * DT * (B + 1))
                for u in range(2):
                    sp.wait_ge(out_dma[u], 16 * NIT // 2)

            @block.gpsimd
            def _(pool):
                def link(sname, per, val, k, ins):
                    ins.then_inc(s[sname], 1)
                    wait_apart(pool, passed["pool"], s[sname], val(per, k))

                def body(pool, n, u, A=True, B_=True, C=True):
                    if B_:
                        b = at(n, 1)
                        v = (u + 1) % 2
                        wait(pool, s["s_done"], at(n, 0)(1, 0))
                        wait(pool, s["ys_done"], at(n, 0)(1, 0))
                        wait(pool, s["kn_done"], b(3, 0))
                        m = n + 1
                        src = g.tab[:, m, :] if isinstance(m, int) else g.tab[:, ds(m, 1), :]
                        dst = sc[:, v, :] if isinstance(m, int) else sc[:, v:v + 1, :]
                        pool.tensor_copy(dst, src).then_inc(s["sc_done"], 1)
                        pool.wait_ge(s["sc_done"], b(1, 1))
                        wait(pool, s["qn_done"], b(1, 0))
                        wait_apart(pool, passed["pool"], s["ss_done"], b(1, 1))
                        L_ = lambda k, ins: link("pool_link_b", 5, b, k, ins)
                        L_(1, pool.tensor_scalar(rr[:, :], ss[:, :], 4e-24, None, ALU.max))
                        L_(2, pool.tensor_tensor(rr[:, :], rr[:, :], g.mhalf[:, 0:6], ALU.pow))
                        pool.tensor_scalar(rq[:, 0, :], rr[:, 4:6], DH ** -0.5, None, ALU.mult)
                        L_(3, pool.tensor_tensor(rw[:, :], rr[:, 0:B], sc[:, v, 16:20], ALU.mult))
                        pool.tensor_tensor(rq[:, 1, :], rq[:, 0, :], sc[:, v, 24:26], ALU.mult).then_inc(s["r_done"], 1)
                        wait(pool, s["decay_done"], b(2, 0))
                        gb = lambda w: sc[:, v, 0:B].unsqueeze(2).to_broadcast([P, B, w])
                        up = g.upto[:, :].unsqueeze(1).to_broadcast([P, B, CM])
                        upq = g.upto[:, :].rearrange("p (t j) -> p t j", j=2)[:, :, 1].unsqueeze(1).to_broadcast([P, B, CT])
                        pool.tensor_tensor(Dr[:], up, gb(CM), ALU.mult)
                        L_(4, pool.tensor_tensor(Dt[:], g.ident[:, :].unsqueeze(1).to_broadcast([P, B, CM]),
                                                 sc[:, v, 4:8].unsqueeze(2).to_broadcast([P, B, CM]), ALU.mult))
                        L_(5, pool.tensor_tensor(Dr[:], Dr[:], Dt[:], ALU.add))
                        pool.tensor_tensor(Dq[:], upq, gb(CT), ALU.mult).then_inc(s["dr_done"], 1)
                    if C:
                        a = at(n, 0)
                        pool.wait_ge(dt_in[u], ((n >> 1) + 1) * 16)
                        pool.wait_ge(s["bc_in"], ((n >> 2) + 1) * 16)
                        pool.wait_ge(s["ys_done"], a(1, 0)) if not (isinstance(n, int) and n == 0) else None
                        pool.tensor_tensor(hs[:], dts[:, u, 1, :].unsqueeze(1).to_broadcast([P, 4, L]), bcq[:, 0],
                                           ALU.mult).then_inc(s["bx_done"], 1)
                        wait(pool, s["on_done"], a(1, 0))
                        wait_apart(pool, passed["pool"], s["oss_done"], a(1, 1))
                        link("pool_link_c", 1, a, 1,
                             pool.tensor_scalar(orr[:, :], oss[:, :], 1.0 / DH, EPS, ALU.mult, ALU.add))
                        pool.tensor_tensor(orr[:, :], orr[:, :], g.mhalf[:, 0:2], ALU.pow).then_inc(s["orr_done"], 1)
                        pool.wait_ge(s["hc_done"], a(1, 1))
                        t = ds((n & 3) * L, L) if not isinstance(n, int) else slice((n & 3) * L, (n & 3) * L + L)
                        yt = ys[:].rearrange("p t l -> p (t l)")[:, t]
                        pool.wait_ge(y_dma, (n >> 4) * (16 * DT) + 16 * DT)
                        link("ys_link", 3, a, 1, pool.tensor_tensor(hs[:, 0:2], hs[:, 0:2], hs[:, 2:4], ALU.add))
                        link("ys_link", 3, a, 2, pool.tensor_tensor(hs[:, 0], hs[:, 0], hs[:, 1], ALU.add))
                        link("ys_link", 3, a, 3, pool.tensor_tensor(yt, yt, sc[:, u, 26:27].to_broadcast([P, L]), ALU.mult))
                        pool.tensor_tensor(yt, yt, hs[:, 0], ALU.add).then_inc(s["ys_done"], 1)

                pool.wait_ge(s["ya_cleared"], 1)
                loops(pool, body)

            @block.tensor
            def _(pe):
                def body(pe, n, u, A=True, B_=True, C=True):
                    a, b, c = at(n, 2), at(n, 1), at(n, 0)
                    v = (u + 1) % 2

                    def proj(o):
                        if not A:
                            return
                        m = n + 2
                        if o == 0:
                            pe.wait_ge(s["w_in"], ((m >> 3) + 1) * 32)
                        wait(pe, s["conv_done"], a(NO, o - 1))
                        off = (m & 7) * CT
                        for k in range(KT):
                            src = g.xT[:, k, :, off:off + CT + PAD] if isinstance(m, int) else g.xT[:, k, :, ds(off, CT + PAD)]
                            i = pe.matmul(proj_bank(o), W[:, o, k, :], src, start=(k == 0), stop=(k == KT - 1))
                        i.then_inc(s["proj_done"], 1)

                    def level(l, x=False, tr=False):
                        if not B_:
                            return
                        X, T, R = by_batch(bank[2]), by_batch(bank[3]), by_batch(bank[4])
                        if x:
                            if l == 0:
                                pe.wait_ge(s["at_done"], b(1, 1))
                            elif l == 1:
                                pe.wait_ge(s["xm_done"], b(LV, 1))
                            else:
                                pe.wait_ge(s["tcopy_done"], b(LV - 2, l - 1))
                            for q in range(B):
                                if l == 0:
                                    i = pe.transpose(X[:, q], At[:, q], g.ident[:, :])
                                else:
                                    i = pe.matmul(X[:, q], At[:, q], (g.Xm[:, 0, q] if l == 1 else Tb[:, q]),
                                                  start=True, stop=True)
                            i.then_inc(s["x_done"], 1)
                        if tr:
                            pe.wait_ge(s["xm_done"], b(LV, l + 1))
                            if l == 0:
                                pe.wait_ge(s["pt_done"], b(1, 1))
                                pe.wait_ge(s["e_done"], b(2, 2))
                            else:
                                pe.wait_ge(s["rcopy_done"], b(LV, l))
                            if 1 <= l < LV - 1:
                                for q in range(B):
                                    i = pe.matmul(T[:, q], Rb[:, q], g.Xm[:, l, q], start=True, stop=True)
                                i.then_inc(s["t_done"], 1)
                            for q in range(B):
                                if l == 0:
                                    i = pe.transpose(R[:, q], g.Xm[:, 0, q], g.ident[:, :])
                                else:
                                    i = pe.matmul(R[:, q], g.Xm[:, l, q], Rb[:, q], start=True, stop=True)
                            i.then_inc(s["rt_done"], 1)

                    if B_:
                        pe.wait_ge(s["act_done"], b(1, 1))
                        wait(pe, s["xm_done"], b(LV, 0))
                        for q in range(B):
                            i = pe.transpose(by_batch(bank[2])[:, q], kvq[:, v, K0 + q * CM:K0 + (q + 1) * CM], g.ident[:, :])
                        i.then_inc(s["natural_done"], 1)
                        wait(pe, s["rcopy_done"], b(LV, 0))
                        for q in range(2):
                            i = pe.transpose(pairs(bank[4][:, 0:256])[:, q], kvq[:, v, Q0 + q * P:Q0 + (q + 1) * P], g.ident[:, :])
                        i.then_inc(s["natural_done"], 1)
                        wait(pe, s["tcopy_done"], b(LV - 2, 0))
                        for q in range(B):
                            i = pe.transpose(by_batch(bank[3])[:, q], kvq[:, v, V0 + q * CM:V0 + (q + 1) * CM], g.ident[:, :])
                        i.then_inc(s["natural_done"], 1)
                    if C:
                        pe.wait_ge(s["kt_done"], c(1, 1))
                        wait(pe, s["s_done"], c(1, 0))
                        for q in range(B):
                            i = pe.matmul(by_batch(bank[5])[:, q], KTr[:, u, q], g.S[:, q], start=True, stop=True)
                        i.then_inc(s["ks_done"], 1)
                    proj(0)
                    if C:
                        pe.wait_ge(s["f_done"], c(1, 1))
                        pe.wait_ge(s["rcopy_done"], c(LV, LV))
                        pe.wait_ge(s["pt_done"], c(1, 1))
                        for q in range(B):
                            i = pe.matmul(by_batch(bank[6])[:, q], Rf[:, u, q], F[:, q], start=True, stop=True)
                        i.then_inc(s["u_done"], 1)
                    if B_:
                        pe.wait_ge(s["kn_done"], b(3, 2))
                        for q in range(B):
                            i = pe.transpose(by_batch(bank[2])[:, q], Kn[:, q], g.ident[:, :])
                        i.then_inc(s["turned"], 1)
                        pe.wait_ge(s["kn_done"], b(3, 3))
                        pe.wait_ge(s["qn_done"], b(1, 1))
                        for q in range(4):
                            i = pe.transpose(by_batch(bank[3])[:, q], Qn[:, q // 2, q % 2], g.ident[:, :])
                        i.then_inc(s["turned"], 1)
                    if C:
                        pe.wait_ge(s["ucopy_done"], c(1, 1))
                        for q in range(B):
                            i = pe.matmul(by_batch(bank[5])[:, q], Kw[:, u, q], U[:, q], start=True, stop=True)
                        i.then_inc(s["so_done"], 1)
                        wait(pe, s["ot_done"], c(1, 0))
                        O = pairs(bank[7][:, 0:256])
                        for q in range(B):
                            rows = slice((q % 2) * CT, (q % 2 + 1) * CT)
                            pe.matmul(O[rows, q // 2], QTr[:, u, 1, q // 2, rows], g.S[:, q], start=True, stop=False)
                            i = pe.matmul(O[rows, q // 2], PT[:, u, q], U[:, q], start=False, stop=True)
                        i.then_inc(s["so_done"], 1)
                    proj(1)
                    if B_:
                        pe.wait_ge(s["kt_done"], b(1, 1))
                        pe.wait_ge(s["dr_done"], b(1, 1))
                        pe.matmul(bank[2][:, :], g.after[:, :], Dr[:].rearrange("p b n -> p (b n)"), start=True, stop=False)
                        pe.matmul(bank[2][:, :], g.identb[:, :], g.neg[:, :], start=False, stop=True)\
                            .then_inc(s["decay_done"], 1)
                        pe.matmul(bank[4][:, 0:256], g.after[:, :], Dq[:].rearrange("p b n -> p (b n)"), start=True, stop=False)
                        pe.matmul(bank[4][:, 0:256], g.identb[:, :], g.negq[:, :], start=False, stop=True)\
                            .then_inc(s["decay_done"], 1)
                        pe.wait_ge(s["qt_done"], b(1, 1))
                        for q in range(B):
                            i = pe.matmul(by_batch(bank[3])[:, q], KTr[:, v, q], KTr[:, v, q], start=True, stop=True)
                        i.then_inc(s["gram_done"], 1)
                        for q in range(B):
                            i = pe.matmul(bank[6][:, q * CT:(q + 1) * CT], KTr[:, v, q],
                                          QTr[:, v, 0, q // 2, (q % 2) * CT:(q % 2 + 1) * CT], start=True, stop=True)
                        i.then_inc(s["gram_done"], 1)
                    level(0, x=True)
                    proj(2)
                    level(0, tr=True)
                    level(1, x=True)
                    proj(3)
                    if C:
                        pe.wait_ge(s["on_done"], c(1, 1))
                        wait(pe, s["ot_done"], c(1, 0))
                        for q in range(2):
                            i = pe.transpose(bank[7][:, 256 + q * P:256 + (q + 1) * P], On[:, q], g.ident[:, :])
                        i.then_inc(s["ot_turned"], 1)
                    level(1, tr=True)
                    level(2, x=True)
                    proj(4)
                    level(2, tr=True)
                    level(3, x=True)
                    proj(5)
                    level(3, tr=True)
                    for l in range(4, LV):
                        level(l, x=True)
                        level(l, tr=True)

                loops(pe, body)

            @block.scalar
            def _(act):
                act.wait_ge(s["ya_cleared"], 1)

                def body(act, n, u, A=True, B_=True, C=True):
                    a, b, c = at(n, 2), at(n, 1), at(n, 0)
                    v = (u + 1) % 2

                    def tap(o):
                        if A:
                            act.wait_ge(s["proj_done"], a(NO, o + 1))
                            if o == 0:
                                wait(act, s["act_done"], a(1, 0))
                            act.activation(conv_out(o), proj_bank(o)[:, :, PAD:], ACT.Copy,
                                           scale=cw[:, o, PAD:TAPS]).then_inc(s["tap_done"], 1)

                    def decay_of_state(j):
                        if not C:
                            return
                        if j == 0:
                            act.wait_ge(dt_in[u], ((n >> 1) + 1) * 16)
                            wait(act, s["scan_done"], c(1, 0))
                        k = (n & 15) * 4 + j
                        i = act.activation(da[:, j, 1:], dts[:, u, 0, 1:], ACT.Exp,
                                           scale=g.a_neg[:, k:k + 1] if isinstance(k, int) else g.a_neg[:, ds(k, 1)])
                        if j == 3:
                            i.then_inc(s["da_done"], 1)

                    def copies(l):
                        if not B_:
                            return
                        if 1 <= l < LV - 1:
                            act.wait_ge(s["t_done"], b(LV - 2, l))
                            act.activation(Tb[:], by_batch(bank[3]), ACT.Copy).then_inc(s["tcopy_done"], 1)
                        act.wait_ge(s["rt_done"], b(LV, l + 1))
                        if l == LV - 1:
                            wait(act, s["u_done"], c(1, 0))
                        act.activation(Rb[:] if l < LV - 1 else Rf[:, v], by_batch(bank[4]), ACT.Copy)\
                            .then_inc(s["rcopy_done"], 1)

                    if B_:
                        wait(act, s["r_done"], b(1, 0))
                        act.wait_ge(s["natural_done"], b(3, 1))
                        for q in range(B):
                            act.activation(junk[:, q], by_batch(bank[2])[:, q], ACT.Square, accum_out=ss[:, q:q + 1])
                        act.wait_ge(s["natural_done"], b(3, 2))
                        for q in range(2):
                            i = act.activation(junk[:, 4 + q], pairs(bank[4][:, 0:256])[:, q], ACT.Square,
                                               accum_out=ss[:, 4 + q:5 + q])
                        i.then_inc(s["ss_done"], 1)
                    tap(0)
                    if B_:
                        act.wait_ge(s["r_done"], b(1, 1))
                        wait(act, s["turned"], b(2, 0))
                        for k in range(2):
                            for q in range(2):
                                i = act.activation(Qn[:, k, q], pairs(bank[4][:, 0:256])[:, q], ACT.Copy,
                                                   scale=rq[:, k, q:q + 1])
                        i.then_inc(s["qn_done"], 1)
                    if C:
                        act.wait_ge(s["u_done"], c(1, 1))
                        wait(act, s["so_done"], c(2, 0))
                        act.activation(U[:], by_batch(bank[6]), ACT.Copy).then_inc(s["ucopy_done"], 1)
                    if B_:
                        act.wait_ge(s["turned"], b(2, 1))
                        wait(act, s["ks_done"], c(1, 0))
                        act.activation(KTr[:, v], by_batch(bank[2]), ACT.Copy).then_inc(s["kt_done"], 1)
                    tap(1)
                    if B_:
                        act.wait_ge(s["decay_done"], b(2, 1))
                        wait(act, s["at_done"], b(1, 0))
                        act.activation(E_[:], by_batch(bank[2]), ACT.Exp).then_inc(s["e_done"], 1)
                        act.wait_ge(s["decay_done"], b(2, 2))
                        wait(act, s["pt_done"], b(1, 0))
                        act.activation(Eq[:], bank[4][:, 0:256].rearrange("p (b t) -> p b t", b=B), ACT.Exp)\
                            .then_inc(s["e_done"], 1)
                    if C:
                        act.wait_ge(s["so_done"], c(2, 2))
                        wait(act, s["orr_done"], c(1, 0))
                        for q in range(2):
                            i = act.activation(junk[:, 6 + q], pairs(bank[7][:, 0:256])[:, q], ACT.Square,
                                               accum_out=oss[:, q:q + 1])
                        i.then_inc(s["oss_done"], 1)
                    tap(2)
                    copies(0)
                    tap(3)
                    if C:
                        act.wait_ge(s["orr_done"], c(1, 1))
                        wait(act, s["ot_turned"], c(1, 0))
                        for q in range(2):
                            i = act.activation(On[:, q], pairs(bank[7][:, 0:256])[:, q], ACT.Copy, scale=orr[:, q:q + 1])
                        i.then_inc(s["on_done"], 1)
                    decay_of_state(0)
                    copies(1)
                    decay_of_state(1)
                    tap(4)
                    copies(2)
                    decay_of_state(2)
                    if A:
                        act.wait_ge(s["proj_done"], a(NO, NO))
                        wait(act, s["conv_done"], a(NO, 0))
                        act.activation(gt[:], proj_bank(5)[:, :, PAD:], ACT.Tanh, scale=0.5).then_inc(s["gtanh_done"], 1)
                    copies(3)
                    decay_of_state(3)
                    if A:
                        act.wait_ge(s["conv_done"], a(NO, NO - 1))
                        wait(act, s["act_done"], a(1, 0))
                        act.activation(th[:, :], cv[:, :], ACT.Tanh, scale=0.5).then_inc(s["tanh_done"], 1)
                    for l in range(4, LV):
                        copies(l)

                loops(act, body)

            @block.vector
            def _(dve):
                def body(dve, n, u, A=True, B_=True, C=True):
                    a, b, c = at(n, 2), at(n, 1), at(n, 0)
                    v = (u + 1) % 2

                    def conv(o):
                        if not A:
                            return
                        dve.wait_ge(s["tap_done"], a(NO - 1, o + 1))
                        for k in range(PAD):
                            i = dve.scalar_tensor_tensor(conv_out(o), proj_bank(o)[:, :, k:k + CT], cw[:, o, k:k + 1],
                                                         conv_out(o), ALU.mult, ALU.add)
                            if k < PAD - 1:
                                i.then_inc(s["conv_link"], 1)
                                dve.wait_ge(s["conv_link"], a(2 * (NO - 1), 2 * o + k + 1))
                        i.then_inc(s["conv_done"], 1)

                    def masked(l):
                        if B_:
                            wait_apart(dve, passed["dve"], s["x_done"], b(LV, l + 1))
                            dve.copy_predicated(g.Xm[:, l], g.levels[:, l].unsqueeze(1).to_broadcast([P, B, CM]),
                                                by_batch(bank[2])).then_inc(s["xm_done"], 1)

                    if C:
                        dve.wait_ge(s["ks_done"], c(1, 1))
                        wait(dve, s["u_done"], c(1, 0))
                        for q in range(B):
                            i = dve.scalar_tensor_tensor(F[:, q], by_batch(bank[5])[:, q], sc[:, u, 12 + q:13 + q],
                                                         Vb[:, u, q], ALU.mult, ALU.add)
                        i.then_inc(s["f_done"], 1)
                    conv(0)
                    if B_:
                        dve.wait_ge(s["r_done"], b(1, 1))
                        wait(dve, s["turned"], b(2, 0))
                        bc = lambda x: x.unsqueeze(2).to_broadcast([P, B, DH])
                        dve.tensor_tensor(Kn[:], by_batch(bank[2]), bc(rr[:, 0:B]), ALU.mult).then_inc(s["kn_done"], 1)
                        wait(dve, s["so_done"], c(2, 0))
                        dve.tensor_tensor(Kw[:, v], by_batch(bank[2]), bc(rw[:, :]), ALU.mult).then_inc(s["kn_done"], 1)
                        dve.wait_ge(s["natural_done"], b(3, 3))
                        dve.tensor_tensor(Vb[:, v], by_batch(bank[3]), bc(sc[:, v, 8:12]), ALU.mult)\
                            .then_inc(s["kn_done"], 1)
                        dve.wait_ge(s["turned"], b(2, 2))
                        dve.tensor_copy(QTr[:, v].rearrange("p k q n -> p (k q) n"), by_batch(bank[3]))\
                            .then_inc(s["qt_done"], 1)
                    if C:
                        dve.wait_ge(s["so_done"], c(2, 2))
                        for q in range(B):
                            i = dve.scalar_tensor_tensor(g.S[:, q], g.S[:, q], sc[:, u, 20 + q:21 + q],
                                                         by_batch(bank[5])[:, q], ALU.mult, ALU.add)
                        i.then_inc(s["s_done"], 1)
                    conv(1)
                    if B_:
                        dve.wait_ge(s["gram_done"], b(2, 1))
                        dve.wait_ge(s["e_done"], b(2, 1))
                        wait(dve, s["x_done"], b(LV, 0))
                        dve.scalar_tensor_tensor(At[:], by_batch(bank[3]), -1.0, E_[:], ALU.mult, ALU.mult)\
                            .then_inc(s["at_done"], 1)
                        dve.wait_ge(s["gram_done"], b(2, 2))
                        dve.wait_ge(s["e_done"], b(2, 2))
                        dve.tensor_tensor(PT[:, v], bank[6][:, 0:256].rearrange("p (b t) -> p b t", b=B), Eq[:],
                                          ALU.mult).then_inc(s["pt_done"], 1)
                    masked(0)
                    conv(2)
                    masked(1)
                    conv(3)
                    if C:
                        dve.wait_ge(s["ot_turned"], c(1, 1))
                        wait(dve, out_dma[u], (n >> 1) * 16)
                        dve.scalar_tensor_tensor(OT[:, u], bank[7][:, 256:512].rearrange("p (b t) -> p b t", b=B),
                                                 g.normw[:, 0:1], gs[:, u], ALU.mult, ALU.mult).then_inc(s["ot_done"], 1)
                    masked(2)
                    conv(4)
                    masked(3)
                    if A:
                        dve.wait_ge(s["gtanh_done"], a(1, 1))
                        dve.scalar_tensor_tensor(gs[:, u], gt[:], 1.0, proj_bank(5)[:, :, PAD:], ALU.add, ALU.mult)\
                            .then_inc(s["conv_done"], 1)
                    masked(4)
                    if A:
                        dve.wait_ge(s["tanh_done"], a(1, 1))
                        wait(dve, s["natural_done"], a(3, -3))
                        dve.scalar_tensor_tensor(kvq[:, u, :], th[:, :], 1.0, cv[:, :], ALU.add, ALU.mult)\
                            .then_inc(s["act_done"], 1)
                    masked(5)
                    if C:
                        dve.wait_ge(s["da_done"], c(1, 1))
                        dve.wait_ge(s["bx_done"], c(1, 1))
                        flat = lambda x: x.rearrange("p n l -> p (n l)")
                        dve.tensor_tensor_scan(flat(hs[:]), flat(da[:]), flat(hs[:]), 0.0, ALU.mult, ALU.add)\
                            .then_inc(s["scan_done"], 1)
                    masked(6)
                    if C:
                        dve.wait_ge(s["scan_done"], c(1, 1))
                        dve.tensor_tensor(hs[:], hs[:], bcq[:, 1], ALU.mult).then_inc(s["hc_done"], 1)

                dve.memset(da[:, :, 0:1], 0.0)
                dve.memset(ys[:], 0.0).then_inc(s["ya_cleared"], 1)
                loops(dve, body)


def combine(nc, g):
    NT = L // P
    with ExitStack() as ctx:
        sb = lambda name, shape, dt=F32: ctx.enter_context(nc.sbuf_tensor(name, shape, dt))
        pb = lambda name, shape, dt=F32: ctx.enter_context(nc.psum_tensor(name, shape, dt))
        sem = lambda name: ctx.enter_context(nc.semaphore(name))
        wo = sb("wo", [P, H, HID])
        gw = sb("gw", [P, KT, NE])
        ot = sb("ot", [P, 2, H, P])
        xr = sb("xr", [P, 2, HID])
        yr = sb("yr", [P, 2, 2, L])
        x1 = sb("x1", [P, NT, HID])
        st = sb("cst", [P, 2, NT, 6])
        mv = sb("cmv", [P, 2, NT, 2])
        rs = sb("crs", [P, 2, NT])
        z = sb("z", [P, NT, HID])
        zt = sb("zt", [P, NT, HID])
        yd = sb("yd", [P, NT, L])
        w = sb("w", [P, NT, L])
        x2 = sb("x2", [P, 2 * NT, HID])
        xh = sb("xh", [P, NT, HID])
        xhT = sb("xhT", [P, 2, NT, KT, P])
        mean = sb("mean", [P, NT, KT])
        msum = sb("msum", [P, KT])
        lg = sb("lg", [1, 8])
        top = sb("top", [1, 8])
        idx = sb("idx", [1, 8], U32)
        dl = sb("dl", [1, 8])
        pr = sb("pr", [1, 8])
        tot = sb("tot", [1, 4])
        wrow = sb("wrow", [1, 2, P])
        wcol = sb("wcol", [P, 2])
        w1 = sb("w1", [P, 2, KT, FF])
        w2 = sb("w2", [P, 2, len(FT), HID])
        b1 = sb("b1", [P, 2, len(FT)])
        b2 = sb("b2", [1, 2, HID])
        hT = sb("hT", [P, 2, len(FT), L])
        bb = sb("bb", [P, HID])
        res = sb("res", [P, 2, HID])
        bank = [pb(f"cbank{i}", [P, 512]) for i in range(8)]
        names = ("w_in", "wo_done", "x1_done", "var_done", "rs_done", "z_done", "zt_done", "yd_done", "w_done",
                 "wt_done", "x2_done", "var2_done", "rs2_done", "xh_done", "xht_done", "xhT_done", "mean_done",
                 "lg_done", "lg_copied", "dl_done", "pr_done", "wr_done", "wc_done", "wcol_done", "h_done",
                 "gelu_done", "hs_done", "b2_done", "bb_done", "x2b_done", "o_done", "res_done", "x_link",
                 "g_link", "act_link", "pad_done", "expert_in", "s2_done")
        passed = {k: sem(f"c_passed_{k}") for k in ("sp", "pool", "dve")}
        s = {k: sem("c_" + k) for k in names}
        tile_in = [sem("tile_in0"), sem("tile_in1")]
        res_dma = [sem("res_dma0"), sem("res_dma1")]

        def run(eng, X=None, G=None, Y=None):
            go = lambda f, n, off: f and f(n + off, at(n, off))
            go(X, 0, 0)
            go(G, 0, 0)
            go(X, 0, 1)
            go(Y, 0, 0)
            go(G, 0, 1)
            with eng.Fori(1, B - 1) as n:
                go(X, n, 1)
                go(Y, n, 0)
                go(G, n, 1)
            go(Y, B - 1, 0)

        def half(m):
            return (m & 1) * NT

        def pick(a, start):
            return a[:, start] if isinstance(start, int) else a[:, ds(start, 1)].rearrange("p o n -> p (o n)")

        with nc.Block() as block:
            @block.sync
            def _(sp):
                sp.dma_start(wo[:], g.inputs["w_o"]).then_inc(s["w_in"], 16)
                sp.dma_start(gw[:], g.inputs["gate_w"]).then_inc(s["w_in"], 16)

                def X(m, v):
                    one = slice(m, m + 1) if isinstance(m, int) else ds(m, 1)
                    for t in range(NT):
                        wait(sp, s["wo_done"], v(NT, t - 1))
                        wait(sp, s["x1_done"], v(NT, t - 1))
                        wait(sp, s["yd_done"], v(NT, t - 1))
                        u = t % 2
                        src = g.o_dram[:, :, one, t * P:(t + 1) * P]
                        sp.dma_start(ot[:, u], src.rearrange("h v b t -> v h (b t)")).then_inc(tile_in[u], 16)
                        sp.dma_start(xr[:, u], g.inputs["x"].rearrange("(b t p) d -> b t p d", b=B, p=P)[one, t]
                                     .rearrange("b p d -> p (b d)")).then_inc(tile_in[u], 16)
                        sp.dma_start(yr[:, u, 0], g.y_dram[one, t].rearrange("b p l -> p (b l)")).then_inc(tile_in[u], 16)
                        sp.dma_start(yr[:, u, 1], g.ud_dram[one, t].rearrange("b p l -> p (b l)")).then_inc(tile_in[u], 16)

                def G(m, v):
                    wait(sp, s["o_done"], v(NT, 0))
                    wait_apart(sp, passed["sp"], s["g_link"], v(9, 3))
                    for k in range(2):
                        e = sp.value_load(idx[0:1, k:k + 1], min_val=0, max_val=NE - 1)
                        one = ds(e, 1)
                        sp.dma_start(w1[:, k], g.inputs["w1"][one].rearrange("e p k n -> p (e k) n")).then_inc(s["expert_in"], 16)
                        sp.dma_start(w2[:, k], g.inputs["w2"][one].rearrange("e p k n -> p (e k) n")).then_inc(s["expert_in"], 16)
                        sp.dma_start(b1[:, k], g.inputs["b1"][one].rearrange("e p k -> p (e k)")).then_inc(s["expert_in"], 16)
                        sp.dma_start(b2[:, k], g.inputs["b2"][one]).then_inc(s["expert_in"], 16)

                def Y(m, v):
                    one = slice(m, m + 1) if isinstance(m, int) else ds(m, 1)
                    for t in range(NT):
                        sp.wait_ge(s["res_done"], v(NT, t + 1))
                        dst = g.out[one, t * P:(t + 1) * P, :].rearrange("b p d -> p (b d)")
                        sp.dma_start(dst, res[:, t % 2]).then_inc(res_dma[t % 2], 16)

                run(sp, X, G, Y)
                for u in range(2):
                    sp.wait_ge(res_dma[u], 16 * B * NT // 2)

            @block.tensor
            def _(pe):
                pe.wait_ge(s["w_in"], 32)

                def X(m, v):
                    for t in range(NT):
                        pe.wait_ge(tile_in[t % 2], v(128, 64 * (t // 2 + 1)))
                        wait(pe, s["x1_done"], v(NT, t - 1))
                        for h in range(H):
                            i = pe.matmul(bank[t % 2][:, :], ot[:, t % 2, h], wo[:, h], start=(h == 0), stop=(h == H - 1))
                        i.then_inc(s["wo_done"], 1)
                    pe.wait_ge(s["w_done"], v(NT, NT))
                    for t in range(NT):
                        wait(pe, s["x2_done"], v(NT, t - 1))
                        if t < 2:
                            wait(pe, s["xhT_done"], v(NT, t - 1))
                        for k in range(NT):
                            i = pe.transpose(bank[2 + t % 2][:, k * P:(k + 1) * P], w[:, k, t * P:(t + 1) * P], g.ident[:, :])
                        i.then_inc(s["wt_done"], 1)
                    for t in range(NT):
                        pe.wait_ge(s["xh_done"], v(NT, t + 1))
                        if t < 2:
                            pe.wait_ge(s["x2_done"], v(NT, t + 3))
                        else:
                            pe.wait_ge(s["xhT_done"], v(NT, t - 1))
                        for k in range(KT):
                            i = pe.transpose(bank[2 + t % 2][:, k * P:(k + 1) * P], xh[:, t, k * P:(k + 1) * P], g.ident[:, :])
                        i.then_inc(s["xht_done"], 1)

                def G(m, v):
                    pe.wait_ge(s["mean_done"], v(1, 1))
                    wait(pe, s["wcol_done"], v(1, 0))
                    for k in range(KT):
                        i = pe.matmul(bank[7][0:1, 0:NE], msum[:, k:k + 1], gw[:, k, :], start=(k == 0), stop=(k == KT - 1))
                    i.then_inc(s["lg_done"], 1)
                    pe.wait_ge(s["wr_done"], v(1, 1))
                    for k in range(2):
                        i = pe.matmul(bank[7][:, 8 + k:9 + k], wrow[:, k], g.ones[0:1, 0:1], start=True, stop=True)
                    i.then_inc(s["wc_done"], 1)

                def Y(m, v):
                    pe.wait_ge(s["expert_in"], v(128, 128))
                    wait(pe, s["bb_done"], v(1, 0))
                    for k in range(2):
                        i = pe.matmul(bank[6][:, :], wrow[:, k], b2[:, k], start=(k == 0), stop=(k == 1))
                    i.then_inc(s["b2_done"], 1)
                    for j in range(2 * len(FT)):
                        k, f = divmod(j, len(FT))
                        lo, n = FT[f]
                        if j < 2:
                            wait(pe, s["res_done"], v(NT, 0))
                        else:
                            pe.wait_ge(s["gelu_done"], v(2 * len(FT), j - 1))
                        for q in range(KT):
                            start = (m & 1) * NT
                            rhs = xhT[:, m & 1, :, q] if isinstance(m, int) else \
                                xhT[:, ds(m & 1, 1), :, q].rearrange("p o t n -> p (o t) n")
                            i = pe.matmul(bank[4 + j % 2][0:n, :], w1[:, k, q, lo:lo + n], rhs, start=(q == 0), stop=(q == KT - 1))
                        i.then_inc(s["h_done"], 1)
                    pe.wait_ge(s["hs_done"], v(2 * len(FT), 2 * len(FT)))
                    for t in range(NT):
                        if t > 1:
                            pe.wait_ge(s["res_done"], v(NT, t - 1))
                        for j in range(2 * len(FT)):
                            k, f = divmod(j, len(FT))
                            n = FT[f][1]
                            i = pe.matmul(bank[4 + t % 2][:, :], hT[0:n, k, f, t * P:(t + 1) * P], w2[0:n, k, f, :],
                                          start=(j == 0), stop=(j == 2 * len(FT) - 1))
                        i.then_inc(s["o_done"], 1)

                run(pe, X, G, Y)

            @block.gpsimd
            def _(pool):
                def X(m, v):
                    for t in range(NT):
                        pool.wait_ge(tile_in[t % 2], v(128, 64 * (t // 2 + 1)))
                        if t == 0:
                            wait(pool, s["w_done"], v(NT, 0))
                        pool.tensor_tensor(yd[:, t], yr[:, t % 2, 0], yr[:, t % 2, 1], ALU.add).then_inc(s["yd_done"], 1)
                    pool.wait_ge(s["var_done"], v(1, 1))
                    pool.tensor_tensor(rs[:, 0], rs[:, 0], g.mhalf[:, 0:NT], ALU.pow).then_inc(s["rs_done"], 1)
                    pool.wait_ge(s["var2_done"], v(1, 1))
                    pool.tensor_tensor(rs[:, 1], rs[:, 1], g.mhalf[:, 0:NT], ALU.pow).then_inc(s["rs2_done"], 1)

                def Y(m, v):
                    wait_apart(pool, passed["pool"], s["bb_done"], v(1, 1))
                    for t in range(NT):
                        x = pick(x2, half(m) + t)
                        pool.tensor_tensor(x, x, bb[:, :], ALU.add).then_inc(s["x2b_done"], 1)

                run(pool, X, None, Y)

            @block.scalar
            def _(act):
                def X(m, v):
                    for t in range(NT):
                        act.wait_ge(s["z_done"], v(NT, t + 1))
                        act.activation(zt[:, t], z[:, t], ACT.Tanh, scale=0.5).then_inc(s["zt_done"], 1)
                    for t in range(NT):
                        act.wait_ge(s["xht_done"], v(NT, t + 1))
                        if t == 0:
                            wait(act, s["h_done"], v(2 * len(FT), -2 * len(FT)))
                        dst = xhT[:, m & 1, t] if isinstance(m, int) else \
                            xhT[:, ds(m & 1, 1), t].rearrange("p o k n -> p (o k) n")
                        act.activation(dst, bank[2 + t % 2][:, :].rearrange("p (k n) -> p k n", k=KT), ACT.Copy)\
                            .then_inc(s["xhT_done"], 1)

                def G(m, v):
                    act.wait_ge(s["dl_done"], v(1, 1))
                    act.activation(pr[:, :], dl[:, :], ACT.Exp, accum_out=tot[:, 0:1]).then_inc(s["pr_done"], 1)

                def Y(m, v):
                    act.wait_ge(s["b2_done"], v(1, 1))
                    wait(act, s["x2b_done"], v(NT, 0))
                    act.activation(bb[:, :], bank[6][:, :], ACT.Copy).then_inc(s["bb_done"], 1)
                    for j in range(2 * len(FT)):
                        k, f = divmod(j, len(FT))
                        n = FT[f][1]
                        act.wait_ge(s["h_done"], v(2 * len(FT), j + 1))
                        if j == 0:
                            wait(act, s["o_done"], v(NT, 0))
                        act.activation(hT[0:n, k, f, :], bank[4 + j % 2][0:n, :], ACT.Gelu, bias=b1[0:n, k, f:f + 1])\
                            .then_inc(s["gelu_done"], 1)

                run(act, X, G, Y)

            @block.vector
            def _(dve):
                XL = 2 * (NT * 2)

                def norm(src, j, v, base):
                    for t in range(NT):
                        dve.bn_stats(st[:, j, t, :], src(t)).then_inc(s["x_link"], 1)
                        wait_apart(dve, passed["dve"], s["x_link"], v(XL, base + 2 * t + 1))
                        dve.bn_aggr(mv[:, j, t, :], st[:, j, t, :]).then_inc(s["x_link"], 1)
                    dve.wait_ge(s["x_link"], v(XL, base + 2 * NT))
                    dve.tensor_scalar(rs[:, j], mv[:, j, :, 1], EPS, None, ALU.add)\
                        .then_inc(s["var_done" if j == 0 else "var2_done"], 1)

                def X(m, v):
                    for t in range(NT):
                        dve.wait_ge(s["wo_done"], v(NT, t + 1))
                        dve.tensor_tensor(x1[:, t], bank[t % 2][:, :], xr[:, t % 2], ALU.add).then_inc(s["x1_done"], 1)
                    wait_apart(dve, passed["dve"], s["x1_done"], v(NT, NT))
                    norm(lambda t: x1[:, t], 0, v, 0)
                    dve.wait_ge(s["rs_done"], v(1, 1))
                    for t in range(NT):
                        dve.tensor_scalar(z[:, t], x1[:, t], mv[:, 0, t, 0:1], rs[:, 0, t:t + 1],
                                          ALU.subtract, ALU.mult).then_inc(s["z_done"], 1)
                    for t in range(NT):
                        dve.wait_ge(s["zt_done"], v(NT, t + 1))
                        dve.scalar_tensor_tensor(z[:, t], zt[:, t], 1.0, z[:, t], ALU.add, ALU.mult)\
                            .then_inc(s["s2_done"], 1)
                    for t in range(NT):
                        dve.wait_ge(s["s2_done"], v(NT, t + 1))
                        dve.wait_ge(s["yd_done"], v(NT, t + 1))
                        if t == 0:
                            wait(dve, s["wt_done"], v(NT, 0))
                        dve.scalar_tensor_tensor(w[:, t], yd[:, t], 0.5, z[:, t], ALU.mult, ALU.mult)\
                            .then_inc(s["w_done"], 1)
                    for t in range(NT):
                        dve.wait_ge(s["wt_done"], v(NT, t + 1))
                        dve.tensor_tensor(pick(x2, half(m) + t), bank[2 + t % 2][:, :], x1[:, t], ALU.add)\
                            .then_inc(s["x2_done"], 1)
                    wait_apart(dve, passed["dve"], s["x2_done"], v(NT, NT))
                    norm(lambda t: pick(x2, half(m) + t), 1, v, 2 * NT)
                    dve.wait_ge(s["rs2_done"], v(1, 1))
                    wait(dve, s["xht_done"], v(NT, 0))
                    for t in range(NT):
                        dve.tensor_scalar(xh[:, t], pick(x2, half(m) + t), mv[:, 1, t, 0:1], rs[:, 1, t:t + 1],
                                          ALU.subtract, ALU.mult).then_inc(s["xh_done"], 1)

                def G(m, v):
                    def link(k, ins):
                        ins.then_inc(s["g_link"], 1)
                        wait_apart(dve, passed["dve"], s["g_link"], v(9, k))

                    dve.wait_ge(s["xhT_done"], v(NT, NT))
                    src = xhT[:, m & 1] if isinstance(m, int) else \
                        xhT[:, ds(m & 1, 1)].rearrange("p o t k n -> p (o t) k n")
                    link(1, dve.tensor_reduce(mean[:], src, AX.X, ALU.add))
                    wait(dve, s["lg_done"], v(1, 0))
                    dve.tensor_reduce(msum[:, :], mean[:].rearrange("p t k -> p k t"), AX.X, ALU.add)\
                        .then_inc(s["mean_done"], 1)
                    dve.wait_ge(s["lg_done"], v(1, 1))
                    wait(dve, s["expert_in"], v(128, 0))
                    link(2, dve.tensor_scalar(lg[:, 0:NE], bank[7][0:1, 0:NE], 1.0 / L, None, ALU.mult))
                    dve.max(top[:, :], lg[:, :]).then_inc(s["lg_copied"], 1)
                    wait_apart(dve, passed["dve"], s["lg_copied"], v(1, 1))
                    link(3, dve.max_index(idx[:, :], top[:, :], lg[:, :]))
                    dve.tensor_scalar(dl[:, :], top[:, :], top[:, 0:1], None, ALU.subtract).then_inc(s["dl_done"], 1)
                    dve.wait_ge(s["pr_done"], v(1, 1))
                    link(4, dve.reciprocal(tot[:, 1:2], tot[:, 0:1]))
                    link(5, dve.tensor_scalar(pr[:, :], pr[:, :], tot[:, 1:2], None, ALU.mult))
                    link(6, dve.tensor_tensor(tot[:, 2:3], pr[:, 0:1], pr[:, 1:2], ALU.add))
                    link(7, dve.reciprocal(tot[:, 3:4], tot[:, 2:3]))
                    link(8, dve.tensor_scalar(pr[:, 0:2], pr[:, 0:2], tot[:, 3:4], None, ALU.mult))
                    wait(dve, s["b2_done"], v(1, 0))
                    dve.tensor_copy(wrow[:], pr[:, 0:2].unsqueeze(2).to_broadcast([1, 2, P])).then_inc(s["wr_done"], 1)
                    dve.wait_ge(s["wc_done"], v(1, 1))
                    link(9, dve.tensor_copy(wcol[:, :], bank[7][:, 8:10]))
                    dve.nop().then_inc(s["wcol_done"], 1)

                def Y(m, v):
                    for j in range(2 * len(FT)):
                        k, f = divmod(j, len(FT))
                        n = FT[f][1]
                        dve.wait_ge(s["gelu_done"], v(2 * len(FT), j + 1))
                        dve.tensor_scalar(hT[0:n, k, f, :], hT[0:n, k, f, :], wcol[0:n, k:k + 1], None, ALU.mult)\
                            .then_inc(s["hs_done"], 1)
                    for t in range(NT):
                        dve.wait_ge(s["o_done"], v(NT, t + 1))
                        dve.wait_ge(s["x2b_done"], v(NT, t + 1))
                        wait(dve, res_dma[t % 2], v(32, 16 * (t // 2)))
                        dve.tensor_tensor(res[:, t % 2], bank[4 + t % 2][:, :], pick(x2, half(m) + t), ALU.add)\
                            .then_inc(s["res_done"], 1)

                dve.memset(lg[:, :], -1e30).then_inc(s["pad_done"], 1)
                dve.wait_ge(s["pad_done"], 1)
                run(dve, X, G, Y)


class Shared:

    def __init__(self, inputs):
        self.inputs = inputs


def build(nc, arrays, out):
    g = Shared(arrays)
    g.log1p = log1p_coefficients()
    g.ln2 = 0.6931471805599453
    g.out = out
    internal = lambda name, shape: nc.dram_tensor(name, shape, F32, kind="Internal").ap()
    g.dts_dram = internal("dts_scratch", (B, DT, 2, P, L))
    g.ud_dram = internal("ud_scratch", (B, DT, P, L))
    g.bc_dram = internal("bc_scratch", (B, 2 * DS, L))
    g.y_dram = internal("y_scratch", (B, DT, P, L))
    g.o_dram = nc.dram_tensor("o_scratch", (H, DH, B, L), F32, kind="Internal").ap()
    with ExitStack() as ctx:
        sb = lambda name, shape, dt=F32: ctx.enter_context(nc.sbuf_tensor(name, shape, dt))
        g.ident = sb("ident", [P, P])
        g.identb = sb("identb", [P, P], BF16)
        g.ones = sb("ones", [P, P])
        g.mhalf = sb("mhalf", [P, NTT])
        state_inputs(nc, g)
        with ExitStack() as inner:
            sb = lambda name, shape, dt=F32: inner.enter_context(nc.sbuf_tensor(name, shape, dt))
            g.upto = sb("upto", [P, CM])
            g.after = sb("after", [P, CM])
            g.neg = sb("neg", [P, B * CM], BF16)
            g.negq = sb("negq", [P, B * CT], BF16)
            g.levels = sb("levels", [P, LV, CM], U32)
            g.normw = sb("normw", [P, 1])
            g.xT = sb("xT", [P, KT, B, TW])
            g.tab = sb("tab", [P, NIT, 27])
            g.a_neg = sb("a_neg", [P, DT * DS])
            g.Xm = sb("Xm", [P, LV, B, CM])
            g.S = sb("S", [P, B, DH])
            prepare(nc, g)
            delta(nc, g)
        combine(nc, g)


def constants():
    import numpy as np
    i = np.arange(P)
    levels = np.zeros((P, LV, CM), np.uint32)
    for l in range(LV):
        s = 1 << l
        levels[:, l, :] = ((i[:, None] // (2 * s) == i[None, :] // (2 * s)) & (i[:, None] // s % 2 == 1)
                           & (i[None, :] // s % 2 == 0))
    neg = np.where(i[:, None] >= i[None, :], -30000.0, 0.0)
    negq = np.where(i[:, None] > 2 * np.arange(CT)[None, :] + 1, -30000.0, 0.0)
    first = np.ones((P, NIT), np.float32)
    first[:, ::NC] = 0
    flag = np.tile((np.arange(NIT) // 4 % 4 != 0).astype(np.float32), (P, 1))
    return dict(
        c_ident=np.eye(P, dtype=np.float32),
        c_ones=np.ones((P, P), np.float32),
        c_upto=(i[:, None] <= i[None, :]).astype(np.float32), c_after=(i[:, None] > i[None, :]).astype(np.float32),
        c_neg=neg.astype(np.float32), c_negq=negq.astype(np.float32),
        c_levels=levels, c_parity=np.stack([i % 2 == 0, i % 2 == 1], 1).astype(np.float32), c_first=first, c_flag=flag)


def laid_out(v):
    import numpy as np
    f = {k: np.asarray(a) for k, a in v.items()}
    per_head = lambda w: w.reshape(KT, P, -1, P).transpose(2, 1, 0, 3)
    a = "L0_attn_"
    q, k, vv, gg = (per_head(f[a + n]) for n in ("Wq", "Wk", "Wv", "Wg"))
    heads = np.stack([k[:H], k[H:], vv[:H], vv[H:], q, gg], 2)
    cq, ck, cvw = (f[a + n].reshape(-1, P, TAPS) for n in ("conv_q_w", "conv_k_w", "conv_v_w"))
    convs = np.stack([ck[:H], ck[H:], cvw[:H], cvw[H:], cq], 2)
    out = dict(
        x=f["x"].reshape(B * L, HID), w_heads=heads.reshape(H, P, -1), conv_heads=convs.reshape(H, P, -1),
        w_gates=np.concatenate([f[a + "Wb"], f[a + "Wa"]], 1).reshape(KT, P, NG).transpose(1, 0, 2),
        dt_bias=f[a + "dt_bias"], a_log=f[a + "A_log"], norm_w=f[a + "norm_w"].reshape(P, 1),
    )
    m = "L0_xattn_"
    tiles = lambda w: w.reshape(DT, P, -1).transpose(1, 0, 2)
    out.update(
        ctxT=f["ctx_1024"].reshape(B * L, CTXT, P).transpose(2, 1, 0),
        in_w=f[m + "in_proj_w"].T.reshape(CTXT, P, DI).transpose(1, 0, 2),
        s_conv=tiles(f[m + "conv_w"]), s_convb=f[m + "conv_b"].reshape(DT, P).T,
        x_w=tiles(f[m + "x_proj_w"].T), dt_w=f[m + "dt_proj_w"].T, dt_b=f[m + "dt_proj_b"].reshape(DT, P).T,
        s_d=f[m + "D"].reshape(DT, P).T, s_alog=tiles(f[m + "A_log"]).reshape(P, DT, 4, 4).transpose(0, 2, 1, 3).reshape(P, -1),
    )
    e = "L0_ffn_"
    pad = len(FT) * P - FF
    out.update(
        w_o=f[a + "Wo"].reshape(H, DH, HID).transpose(1, 0, 2), gate_w=f[e + "gate_W"].T.reshape(KT, P, NE).transpose(1, 0, 2),
        w1=f[e + "W1"].reshape(NE, KT, P, FF).transpose(0, 2, 1, 3),
        w2=np.pad(f[e + "W2"], ((0, 0), (0, pad), (0, 0))).reshape(NE, len(FT), P, HID).transpose(0, 2, 1, 3),
        b1=np.pad(f[e + "b1"], ((0, 0), (0, pad))).reshape(NE, len(FT), P).transpose(0, 2, 1), b2=f[e + "b2"],
    )
    out.update(constants())
    return {n: np.ascontiguousarray(x) for n, x in out.items()}


def kernel(**inputs):
    import concourse.bacc as bacc
    import numpy as np
    from concourse.bass_utils import run_bass_kernel_spmd

    nc = bacc.Bacc("TRN2", target_bir_lowering=False, num_devices=1)
    arrays = laid_out(inputs)
    aps = {n: nc.dram_tensor("in_" + n, x.shape, mybir.dt.from_np(x.dtype), kind="ExternalInput").ap()
           for n, x in arrays.items()}
    out = nc.dram_tensor("out", (B, L, HID), F32, kind="ExternalOutput").ap()
    build(nc, aps, out)
    r = run_bass_kernel_spmd(nc, [{"in_" + n: x for n, x in arrays.items()}], core_ids=[0])
    return r.results[0]["out"]
```

```python
from contextlib import ExitStack

import concourse.bass as bass
from concourse import mybir
from concourse.bass import ds

F32 = mybir.dt.float32
BF16 = mybir.dt.bfloat16
U32 = mybir.dt.uint32
ALU = mybir.AluOpType
ACT = mybir.ActivationFunctionType
AX = mybir.AxisListType

P = 128
B, L, HID = 4, 512, 512
KT = HID // P
H, DH, NHH = 8, 128, 2
TAPS = 4
CT = 64
CM = CT * NHH
NC = L // CT
NIT = H * NC
LV = 7
PAD = TAPS - 1
TW = L + PAD
EPS = 1e-5
NTT = B * L // P
NG = NHH * H + H
DI, DS, DR = 512, 16, 16
DT = DI // P
CTXT = 2
NE, FF = 6, 352
FT = [(0, 128), (128, 128), (256, 96)]


def log1p_coefficients():
    import numpy as np
    deg = 9
    k = np.arange(400)
    e = (1 + np.cos(np.pi * (k + 0.5) / 400)) / 2
    f = np.log1p(e) / e
    c = np.polynomial.chebyshev.Chebyshev.fit(e, f, deg, domain=[0, 1])
    return [float(v) for v in c.convert(kind=np.polynomial.Polynomial).coef]


def log1p_factors():
    import numpy as np
    k = np.arange(400)
    e = (1 + np.cos(np.pi * (k + 0.5) / 400)) / 2
    f = np.log1p(e) / e
    poly = np.polynomial.chebyshev.Chebyshev.fit(e, f, 8, domain=[0, 1], w=1 / f).convert(kind=np.polynomial.Polynomial)
    roots = [z for z in poly.roots() if z.imag > 0]
    scale = float(poly.coef[-1]) ** (0.5 / len(roots))
    return [(scale, -scale * float(z.real), (scale * float(z.imag)) ** 2) for z in roots]


def at(n, off):
    def val(per, c):
        return n * per + (off * per + c)
    return val


def wait(eng, sem, value):
    if not (isinstance(value, int) and value <= 0):
        eng.wait_ge(sem, value)


def wait_apart(eng, passed, sem, value):
    if not (isinstance(value, int) and value <= 0):
        eng.wait_ge(sem, value)
        eng.sem_inc(passed, 1)




def state_inputs(nc, g):
    with ExitStack() as ctx:
        sb = lambda name, shape, dt=F32: ctx.enter_context(nc.sbuf_tensor(name, shape, dt))
        pb = lambda name, shape, dt=F32: ctx.enter_context(nc.psum_tensor(name, shape, dt))
        sem = lambda name: ctx.enter_context(nc.semaphore(name))
        ctxT = sb("ctxT", [P, CTXT, B * L])
        inw = sb("inw", [P, CTXT, DI])
        xw = sb("xw", [P, DT, DR + 2 * DS])
        dw = sb("dw", [DR, DI])
        cw = sb("scw", [P, DT, TAPS])
        cb = sb("scb", [P, DT])
        db = sb("sdb", [P, DT])
        dd = sb("sdd", [P, DT])
        acc = sb("acc", [P, DT, L])
        th = sb("sth", [P, DT, L])
        u2 = sb("u2", [P, DT, L])
        xd = sb("xd", [DR + 2 * DS, L])
        y = sb("sy", [P, DT, L])
        ya = sb("sya", [P, DT, L])
        e = sb("se", [P, DT, L])
        dt = sb("sdt", [P, DT, L])
        dtu = sb("sdtu", [P, DT, L])
        ud = sb("sud", [P, DT, L])
        sq = sb("ssq", [P, 4, DT, L])
        fb = sb("sfb", [P, 4])
        px = pb("px", [P, DT, 512])
        pd = pb("pd", [P, 512])
        pt = pb("pt", [P, 2, 512])
        names = ("s_in", "in_done", "tap_done", "conv_link", "conv_done", "tanh_done", "u_done", "xd_done",
                 "xd_copied", "dt_done", "abs_done", "e_done", "sq_done", "poly", "fb_done",
                 "ud_done", "out_ready")
        s = {k: sem("si_" + k) for k in names}
        out_dma = sem("si_out")
        passed = sem("si_passed")
        NP = len(g.log1p_factors)

        with nc.Block() as block:
            @block.sync
            def _(sp):
                for dst, src in ((ctxT, g.inputs["ctxT"]), (inw, g.inputs["in_w"]), (cw, g.inputs["s_conv"]), (cb, g.inputs["s_convb"]), (xw, g.inputs["x_w"]),
                                 (dw, g.inputs["dt_w"]), (db, g.inputs["dt_b"]), (dd, g.inputs["s_d"])):
                    sp.dma_start(dst[:], src).then_inc(s["s_in"], 16)
                def batch(b):
                    one = slice(b, b + 1) if isinstance(b, int) else ds(b, 1)
                    sp.wait_ge(s["xd_copied"], b + 1)
                    sp.dma_start(g.bc_dram[one].rearrange("b k l -> (b k) l"), xd[DR:, :]).then_inc(out_dma, 16)
                    sp.wait_ge(s["out_ready"], b + 1)
                    sp.wait_ge(s["ud_done"], b + 1)
                    for dst, src in ((g.dts_dram[one, :, 0], dt), (g.dts_dram[one, :, 1], dtu), (g.ud_dram[one], ud)):
                        sp.dma_start(dst.rearrange("b t p l -> p (b t) l"), src[:]).then_inc(out_dma, 16)

                batch(0)
                with sp.Fori(1, B) as b:
                    batch(b)
                sp.wait_ge(out_dma, 16 * 4 * B)

            def batches(eng, body):
                body(0, True)
                with eng.Fori(1, B - 1) as b:
                    body(b, True)
                body(B - 1, False)

            @block.tensor
            def _(pe):
                def project(b):
                    for t in range(DT):
                        wait(pe, s["conv_done"], b * DT)
                        for k in range(CTXT):
                            src = ctxT[:, k, b * L:(b + 1) * L] if isinstance(b, int) else ctxT[:, k, ds(b * L, L)]
                            i = pe.matmul(px[:, t, :], inw[:, k, t * P:(t + 1) * P], src, start=(k == 0), stop=(k == CTXT - 1))
                        i.then_inc(s["in_done"], 1)

                def batch(b, ahead):
                    if ahead:
                        project(b + 1)
                    pe.wait_ge(s["u_done"], b + 1)
                    for t in range(DT):
                        i = pe.matmul(pd[0:DR + 2 * DS, :], xw[:, t, :], u2[:, t, :], start=(t == 0), stop=(t == DT - 1))
                    i.then_inc(s["xd_done"], 1)
                    pe.wait_ge(s["xd_copied"], b + 1)
                    for t in range(DT):
                        if t > 1:
                            pe.wait_ge(s["abs_done"], b * DT + (t - 1))
                        pe.matmul(pt[:, t % 2, :], dw[:, t * P:(t + 1) * P], xd[0:DR, :], start=True, stop=True)\
                            .then_inc(s["dt_done"], 1)

                pe.wait_ge(s["s_in"], 16 * 8)
                project(0)
                batches(pe, batch)

            @block.scalar
            def _(act):
                def tap(b):
                    for t in range(DT):
                        act.wait_ge(s["in_done"], b * DT + (t + 1))
                        wait(act, s["u_done"], b)
                        act.activation(acc[:, t, :], px[:, t, :], ACT.Identity, bias=cb[:, t:t + 1],
                                       scale=cw[:, t, PAD:TAPS]).then_inc(s["tap_done"], 1)

                def batch(b, ahead):
                    act.wait_ge(s["conv_done"], b * DT + DT)
                    act.activation(th[:], acc[:], ACT.Tanh, scale=0.5).then_inc(s["tanh_done"], 1)
                    act.wait_ge(s["xd_done"], b + 1)
                    wait(act, out_dma, b * 64)
                    act.activation(xd[:, :], pd[0:DR + 2 * DS, :], ACT.Copy, scale=0.5).then_inc(s["xd_copied"], 1)
                    if ahead:
                        tap(b + 1)
                    for t in range(DT):
                        act.wait_ge(s["dt_done"], b * DT + (t + 1))
                        wait(act, s["out_ready"], b)
                        act.activation(y[:, t, :], pt[:, t % 2, :], ACT.Identity, bias=db[:, t:t + 1])
                        act.activation(ya[:, t, :], pt[:, t % 2, :], ACT.Abs, bias=db[:, t:t + 1]).then_inc(s["abs_done"], 1)
                    act.wait_ge(s["abs_done"], b * DT + DT)
                    act.activation(e[:], ya[:], ACT.Exp, scale=-1.0).then_inc(s["e_done"], 1)
                    act.wait_ge(s["e_done"], b + 1)
                    for k, (scale, _, _) in enumerate(g.log1p_factors):
                        act.activation(sq[:, k], e[:], ACT.Square, bias=fb[:, k:k + 1], scale=scale).then_inc(s["sq_done"], 1)

                act.wait_ge(s["s_in"], 16 * 8)
                act.wait_ge(s["fb_done"], 1)
                tap(0)
                batches(act, batch)

            @block.gpsimd
            def _(pool):
                def batch(b, ahead):
                    pool.wait_ge(s["u_done"], b + 1)
                    wait_apart(pool, passed, out_dma, b * 64)
                    for t in range(DT):
                        i = pool.tensor_scalar(ud[:, t, :], u2[:, t, :], dd[:, t:t + 1], 0.5, ALU.mult, ALU.mult)
                    i.then_inc(s["ud_done"], 1)

                pool.wait_ge(s["s_in"], 16 * 8)
                batches(pool, batch)

            @block.vector
            def _(dve):
                def conv(b):
                    for t in range(DT):
                        dve.wait_ge(s["tap_done"], b * DT + (t + 1))
                        for k in range(1, TAPS):
                            i = dve.scalar_tensor_tensor(acc[:, t, k:], px[:, t, 0:L - k], cw[:, t, PAD - k:TAPS - k],
                                                         acc[:, t, k:], ALU.mult, ALU.add)
                            if k < PAD:
                                i.then_inc(s["conv_link"], 1)
                                dve.wait_ge(s["conv_link"], b * (2 * DT) + (2 * t + k))
                        i.then_inc(s["conv_done"], 1)

                def batch(b, ahead):
                    dve.wait_ge(s["tanh_done"], b + 1)
                    wait(dve, s["ud_done"], b)
                    wait(dve, s["out_ready"], b)
                    dve.scalar_tensor_tensor(u2[:], th[:], 1.0, acc[:], ALU.add, ALU.mult).then_inc(s["u_done"], 1)
                    if ahead:
                        conv(b + 1)
                    for k, (_, _, rest) in enumerate(g.log1p_factors):
                        dve.wait_ge(s["sq_done"], b * NP + (k + 1))
                        if k == 0:
                            wait(dve, out_dma, b * 64)
                        else:
                            dve.wait_ge(s["poly"], b * (NP + 1) + k)
                        dve.scalar_tensor_tensor(dt[:], sq[:, k], rest, e[:] if k == 0 else dt[:], ALU.add, ALU.mult)\
                            .then_inc(s["poly"], 1)
                    dve.wait_ge(s["poly"], b * (NP + 1) + NP)
                    dve.scalar_tensor_tensor(dt[:], y[:], 0.0, dt[:], ALU.max, ALU.add).then_inc(s["poly"], 1)
                    dve.wait_ge(s["poly"], b * (NP + 1) + (NP + 1))
                    dve.scalar_tensor_tensor(dtu[:], u2[:], 0.5, dt[:], ALU.mult, ALU.mult).then_inc(s["out_ready"], 1)

                for k, (_, bias, _) in enumerate(g.log1p_factors):
                    i = dve.memset(fb[:, k:k + 1], bias)
                i.then_inc(s["fb_done"], 1)
                dve.wait_ge(s["s_in"], 16 * 8)
                conv(0)
                batches(dve, batch)




def prepare(nc, g):
    with ExitStack() as ctx:
        sb = lambda name, shape, dt=F32: ctx.enter_context(nc.sbuf_tensor(name, shape, dt))
        pb = lambda name, shape, dt=F32: ctx.enter_context(nc.psum_tensor(name, shape, dt))
        sem = lambda name: ctx.enter_context(nc.semaphore(name))
        xin = sb("xin", [P, NTT, HID])
        xhat = sb("xhat", [P, 2, HID])
        stats = sb("stats", [P, 2, 6])
        mv = sb("mv", [P, NTT, 2])
        rstd = sb("rstd", [P, NTT])
        wg = sb("wg", [P, KT, NG])
        logitT = sb("logitT", [NG, B * L, NHH])
        bias_bc = sb("bias_bc", [P, H])
        alog_bc = sb("alog_bc", [P, H])
        expa = sb("expa", [P, H])
        parity = sb("parity", [P, 2])
        first = sb("first", [P, NIT])
        flag = sb("flag", [P, NIT])
        neg = sb("neg32", [P, CM])
        negq = sb("negq32", [P, CT])
        ssa = sb("ssa", [P, DT * DS])
        raw = sb("raw", [P, B * NC, NG])
        y = sb("y", [P, 2, B * NC, H])
        ya = sb("ya", [P, 2, B * NC, H])
        e = sb("e", [P, 2, B * NC, H])
        sp = sb("sp", [P, 2, B * NC, H])
        decay = sb("decay", [P, H, NC, B])
        eG = sb("eG", [P, NIT, B])
        psT = pb("psT", [P, 2, 512])
        psL = pb("psL", [P, 512])
        psR = pb("psR", [P, 2, 512])
        psG = pb("psG", [P, 3, 512])
        x_in, c_in, var_ready, rstd_ready, xhat_ready, t_ready, xT_ready = map(
            sem, ("x_in", "c_in", "var_ready", "rstd_ready", "xhat_ready", "t_ready", "xT_ready"))
        lg_ready, lg_copied, raw_ready, raw_copied, act1, dve1, cum_ready, done_a = map(
            sem, ("lg_ready", "lg_copied", "raw_ready", "raw_copied", "act1", "dve1", "cum_ready", "done_a"))
        chain = sem("prep_chain")
        act_chain = sem("act_chain")
        st_link = sem("st_link")

        with nc.Block() as block:
            @block.sync
            def _(sp_):
                sp_.dma_start(xin[:, :, :], g.inputs["x"].rearrange("(n p) d -> p n d", p=P)).then_inc(x_in, 16)
                for dst, src in ((g.ident, g.inputs["c_ident"]), (g.upto, g.inputs["c_upto"]), (g.after, g.inputs["c_after"]),
                                 (g.ones, g.inputs["c_ones"]), (neg, g.inputs["c_neg"]), (negq, g.inputs["c_negq"]),
                                 (g.levels, g.inputs["c_levels"]), (wg, g.inputs["w_gates"]),
                                 (parity, g.inputs["c_parity"]), (first, g.inputs["c_first"]), (flag, g.inputs["c_flag"]), (ssa, g.inputs["s_alog"]), (g.normw, g.inputs["norm_w"])):
                    sp_.dma_start(dst[:], src).then_inc(c_in, 16)
                sp_.dma_start(bias_bc[:, :], g.inputs["dt_bias"].partition_broadcast(P)).then_inc(c_in, 16)
                sp_.dma_start(alog_bc[:, :], g.inputs["a_log"].partition_broadcast(P)).then_inc(c_in, 16)
            CONSTS = 16 * 15

            @block.vector
            def _(dve):
                dve.wait_ge(x_in, 16)
                for t in range(NTT):
                    dve.bn_stats(stats[:, t % 2, :], xin[:, t, :]).then_inc(st_link, 1)
                    dve.wait_ge(st_link, t + 1)
                    i = dve.bn_aggr(mv[:, t, :], stats[:, t % 2, :])
                i.then_inc(var_ready, 1)
                dve.wait_ge(var_ready, 1)
                dve.tensor_scalar(rstd[:, :], mv[:, :, 1], EPS, None, ALU.add).then_inc(var_ready, 1)
                dve.memset(g.xT[:, :, :, 0:PAD], 0.0)
                dve.wait_ge(rstd_ready, 1)
                for t in range(NTT):
                    wait(dve, t_ready, t - 1)
                    dve.tensor_scalar(xhat[:, t % 2, :], xin[:, t, :], mv[:, t, 0:1], rstd[:, t:t + 1],
                                      ALU.subtract, ALU.mult).then_inc(xhat_ready, 1)
                for k in range(2):
                    dve.wait_ge(raw_ready, k + 1)
                    i = dve.tensor_copy(raw[:, 16 * k:16 * k + 16, :],
                                        psR[:, k, 0:16 * NG].rearrange("p (n c) -> p n c", c=NG))
                i.then_inc(chain, 1)
                dve.wait_ge(chain, 1)
                dve.wait_ge(c_in, CONSTS)
                k = [1]

                def link(ins):
                    k[0] += 1
                    ins.then_inc(chain, 1)
                    dve.wait_ge(chain, k[0])

                bc = lambda a: a.unsqueeze(1).to_broadcast([P, B * NC, H])
                link(dve.tensor_tensor(y[:, 0], raw[:, :, 2 * H:3 * H], bc(bias_bc[:, :]), ALU.add))
                link(dve.tensor_scalar(y[:, 1], raw[:, :, 0:H], parity[:, 0:1], -1.0, ALU.mult, ALU.mult))
                link(dve.tensor_scalar(ya[:, 1], raw[:, :, H:2 * H], parity[:, 1:2], -1.0, ALU.mult, ALU.mult))
                link(dve.tensor_tensor(y[:, 1], y[:, 1], ya[:, 1], ALU.add))
                i = dve.tensor_scalar(ya[:], y[:], -1.0, None, ALU.mult)
                link(i)
                link(dve.tensor_tensor(ya[:], ya[:], y[:], ALU.min))
                dve.nop().then_inc(dve1, 1)
                dve.wait_ge(act1, 2)
                link(dve.tensor_scalar(sp[:], e[:], g.log1p[-1], None, ALU.mult))
                for c in g.log1p[-2::-1]:
                    link(dve.scalar_tensor_tensor(sp[:], sp[:], c, e[:], ALU.add, ALU.mult))
                link(dve.scalar_tensor_tensor(sp[:], y[:], 0.0, sp[:], ALU.max, ALU.add))
                link(dve.tensor_tensor(sp[:, 0], sp[:, 0], bc(expa[:, :]), ALU.mult))
                dv = decay[:, :, :, :].rearrange("p h c b -> p b c h")
                link(dve.tensor_scalar(dv, sp[:, 0].rearrange("p (b c) h -> p b c h", b=B),
                                       parity[:, 0:1], -1.0, ALU.mult, ALU.mult))
                tb = g.tab[:, :, :].rearrange("p (h c) k -> p h c k", h=H)
                for b in range(B):
                    sv = sp[:, 1].rearrange("p (b c) h -> p b h c", b=B)[:, b]
                    dve.tensor_scalar(tb[:, :, :, 4 + b], sv, -1.0, g.ln2, ALU.mult, ALU.add)
                    dve.tensor_scalar(tb[:, :, :, 8 + b], sv, -1.0, None, ALU.mult)
                    i = dve.tensor_copy(tb[:, :, :, b], decay[:, :, :, b])
                link(i)
                dve.nop().then_inc(dve1, 1)
                dve.wait_ge(act1, 3)
                f4 = first[:, :].unsqueeze(2).to_broadcast([P, NIT, B])
                link(dve.scalar_tensor_tensor(eG[:], eG[:], -2.0, f4, ALU.mult, ALU.mult))
                dve.tensor_tensor(g.tab[:, :, 12:16], eG[:], g.tab[:, :, 8:12], ALU.mult)
                dve.tensor_tensor(g.tab[:, :, 20:24], g.tab[:, :, 20:24], f4, ALU.mult)
                dve.tensor_tensor(g.tab[:, :, 24:26], g.tab[:, :, 24:26], f4[:, :, 0:2], ALU.mult)
                dve.tensor_scalar(g.normw[:, :], g.normw[:, :], 0.5, None, ALU.mult)
                dve.tensor_copy(g.tab[:, :, 26:27], flag[:, :].unsqueeze(2))
                dve.tensor_scalar(g.a_neg[:, :], ssa[:, :], -1.0, None, ALU.mult)
                dve.tensor_copy(g.identb[:, :], g.ident[:, :])
                dve.tensor_copy(g.neg[:].rearrange("p (b n) -> p b n", b=B), neg[:, :].unsqueeze(1).to_broadcast([P, B, CM]))
                dve.tensor_copy(g.negq[:].rearrange("p (b n) -> p b n", b=B), negq[:, :].unsqueeze(1).to_broadcast([P, B, CT]))
                for l in range(LV):
                    dve.tensor_copy(g.Xm[:, l], g.ident[:, :].unsqueeze(1).to_broadcast([P, B, P]))
                dve.memset(g.S[:, :, :], 0.0)

            @block.gpsimd
            def _(pool):
                pool.memset(g.mhalf[:, :], -0.5).then_inc(done_a, 1)
                pool.wait_ge(done_a, 1)
                pool.wait_ge(var_ready, 2)
                pool.tensor_tensor(rstd[:, :], rstd[:, :], g.mhalf[:, 0:NTT], ALU.pow).then_inc(rstd_ready, 1)

            @block.tensor
            def _(pe):
                pe.wait_ge(c_in, CONSTS)
                for t in range(NTT):
                    pe.wait_ge(xhat_ready, t + 1)
                    wait(pe, xT_ready, t - 1)
                    for k in range(KT):
                        i = pe.transpose(psT[:, t % 2, k * P:(k + 1) * P], xhat[:, t % 2, k * P:(k + 1) * P],
                                         g.ident[:, :])
                    i.then_inc(t_ready, 1)
                for b in range(B):
                    pe.wait_ge(xT_ready, NTT)
                    wait(pe, lg_copied, b)
                    for k in range(KT):
                        i = pe.matmul(psL[0:NG, :], wg[:, k, :], g.xT[:, k, b, PAD:], start=(k == 0), stop=(k == KT - 1))
                    i.then_inc(lg_ready, 1)
                pe.wait_ge(lg_copied, B)
                for n in range(B * NC):
                    src = logitT[:, n * CT:(n + 1) * CT, :].rearrange("p t j -> p (t j)")
                    i = pe.transpose(psR[:, n // 16, (n % 16) * NG:(n % 16 + 1) * NG], src, g.ident[0:NG, 0:NG])
                    if n % 16 == 15:
                        i.then_inc(raw_ready, 1)
                pe.wait_ge(dve1, 2)
                rhs = decay[:, :, :, :].rearrange("p h c b -> p (h c b)")
                pe.matmul(psG[:, 0, 0:256], g.upto[:, :], rhs, start=True, stop=True)
                pe.matmul(psG[:, 1, 0:256], g.after[:, :], rhs, start=True, stop=True)
                pe.matmul(psG[:, 2, 0:256], g.ones[:, :], rhs, start=True, stop=True)
                uq = g.upto[:, :].rearrange("p (t j) -> p t j", j=2)[:, :, 1]
                for h2 in range(2):
                    i = pe.matmul(psG[h2 * CT:(h2 + 1) * CT, 0, 256:384], uq,
                                  decay[:, :, :, h2::2].rearrange("p h c b -> p (h c) b"),
                                  start=True, stop=True, skip_group_check=True)
                i.then_inc(cum_ready, 1)

            @block.scalar
            def _(act):
                for t in range(NTT):
                    act.wait_ge(t_ready, t + 1)
                    tok = (t % (L // P)) * P
                    act.activation(g.xT[:, :, t // (L // P), PAD + tok:PAD + tok + P],
                                   psT[:, t % 2, :].rearrange("p (k n) -> p k n", k=KT),
                                   ACT.Copy).then_inc(xT_ready, 1)
                for b in range(B):
                    act.wait_ge(lg_ready, b + 1)
                    act.activation(logitT[:, b * L:(b + 1) * L, :],
                                   psL[0:NG, :].unsqueeze(2).to_broadcast([NG, L, NHH]), ACT.Copy).then_inc(lg_copied, 1)
                act.wait_ge(c_in, CONSTS)
                act.activation(ssa[:, :], ssa[:, :], ACT.Exp)
                act.activation(expa[:, :], alog_bc[:, :], ACT.Exp).then_inc(act1, 1)
                act.wait_ge(dve1, 1)
                act.activation(e[:], ya[:], ACT.Exp).then_inc(act1, 1)
                act.wait_ge(cum_ready, 1)
                v = lambda k: psG[:, k, 0:256].rearrange("p (n b) -> p n b", b=B)
                act.activation(eG[:], v(0), ACT.Exp)
                act.activation(g.tab[:, :, 16:20], v(1), ACT.Exp)
                act.activation(g.tab[:, :, 20:24], v(2), ACT.Exp)
                act.activation(g.tab[:, :, 8:12], g.tab[:, :, 8:12], ACT.Exp)
                act.activation(g.tab[:, :, 24:26], psG[:, 0, 256:384].rearrange("p (n b) -> p n b", b=2),
                               ACT.Exp).then_inc(act1, 1)


def delta(nc, g):
    with ExitStack() as ctx:
        sb = lambda name, shape, dt=F32: ctx.enter_context(nc.sbuf_tensor(name, shape, dt))
        pb = lambda name, shape, dt=F32: ctx.enter_context(nc.psum_tensor(name, shape, dt))
        sem = lambda name: ctx.enter_context(nc.semaphore(name))
        K0, V0, Q0, END = 0, B * CM, 2 * B * CM, 2 * B * CM + B * CT
        NO = 6
        W = sb("W", [P, NO, KT, P])
        cw = sb("cw", [P, NO - 1, TAPS])
        cv = sb("cv", [P, END])
        th = sb("th", [P, END])
        kvq = sb("kvq", [P, 2, END])
        gt = sb("gt", [P, B, CT])
        gs = sb("gs", [P, 2, B, CT])
        junk = sb("junk", [P, 8, P])
        sc = sb("sc", [P, 2, 27])
        ss = sb("ss", [P, 6])
        rr = sb("rr", [P, 6])
        sd = sb("sd", [P, 8])
        rq = sb("rq", [P, 2, 2])
        Kn = sb("Kn", [P, B, DH])
        Kw = sb("Kw", [P, 2, B, DH])
        Vb = sb("Vb", [P, 2, B, DH])
        Qn = sb("Qn", [P, 2, 2, DH])
        KTr = sb("KTr", [P, 2, B, CM])
        QTr = sb("QTr", [P, 2, 2, 2, P])
        Dr = sb("Dr", [P, B, CM])
        Dt = sb("Dt", [P, B, CM])
        Dq = sb("Dq", [P, B, CT])
        E_ = sb("E_", [P, B, CM])
        Eq = sb("Eq", [P, B, CT])
        At = sb("At", [P, B, CM])
        PT = sb("PT", [P, 2, B, CT])
        Tb = sb("Tb", [P, B, CM])
        Rf = sb("Rf", [P, 2, B, CM])
        F = sb("F", [P, B, DH])
        U = sb("U", [P, B, DH])
        oss = sb("oss", [P, 2])
        orr = sb("orr", [P, 2])
        On = sb("On", [P, 2, DH])
        OT = sb("OT", [P, 2, B, CT])
        dts = sb("dts", [P, 2, 2, L])
        bcq = sb("bcq", [P, 2, 4, L])
        da = sb("da", [P, 4, L])
        hs = sb("hs", [P, 4, L])
        ys = sb("ys", [P, DT, L])
        bank = [pb(f"bank{i}", [P, 512]) for i in range(8)]
        by_batch = lambda a: a[:, 0:512].rearrange("p (b n) -> p b n", b=B)
        blocks = lambda a, half, s_: a.rearrange("p b (j h s) -> p b h j s", h=2, s=s_)[:, :, half]
        packed = lambda a, s_: a[:, 0:B * CM // 2].rearrange("p (b j s) -> p b j s", b=B, s=s_)
        pairs = lambda a: a.rearrange("p (b n) -> p b n", b=2)

        names = ("cw_in", "proj_done", "tap_done", "conv_done", "gtanh_done", "tanh_done", "act_done",
                 "natural_done", "rk_done", "kw_done", "sd_done", "ss_done", "sc_done", "r_done", "dr_done", "kn_done", "qn_done", "turned",
                 "kt_done", "qt_done", "decay_done", "e_done", "gram_done", "at_done", "pt_done", "x_done",
                 "xm_done", "t_done", "tcopy_done", "rt_done", "rcopy_done", "ks_done", "f_done", "u_done",
                 "ucopy_done", "so_done", "s_done", "oss_done", "orr_done", "on_done", "ot_turned",
                 "ot_done", "conv_link", "pool_link_b", "pool_link_d", "pool_link_c", "bc_in", "ya_cleared",
                 "da_done", "bx_done", "scan_done", "hc_done", "ys_link", "ys_done")
        passed = {k: sem(f"passed_{k}") for k in ("sp", "pool", "dve")}
        s = {k: sem(k) for k in names}
        out_dma = [sem("out_dma0"), sem("out_dma1")]
        dt_in = [sem("dt_in0"), sem("dt_in1")]
        y_dma = sem("y_dma")
        w_in = [sem(f"w_in{o}") for o in range(NO)]
        PARTS = ((K0, V0), (V0, Q0), (Q0, END))
        seq = {0: K0, 1: K0, 2: V0, 3: V0}

        def loops(eng, body):
            body(eng, -2, 0, C=False, B_=False)
            body(eng, -1, 1, C=False)
            body(eng, 0, 0)
            body(eng, 1, 1)
            with eng.Fori(2, NIT - 3, 2) as i:
                for u in range(2):
                    body(eng, i + u, u)
            body(eng, NIT - 2, 0, A=False)
            body(eng, NIT - 1, 1, A=False, B_=False)

        def conv_out(o):
            if o == 4:
                return cv[:, Q0:END].rearrange("p (b t) -> p b t", b=B)
            return cv[:, seq[o]:seq[o] + B * CM].rearrange("p (b t j) -> p j b t", b=B, j=NHH)[:, o % 2]

        def proj_bank(o):
            return bank[o % 2][:, 0:B * (CT + PAD)].rearrange("p (b t) -> p b t", b=B)

        with nc.Block() as block:
            @block.sync
            def _(sp):
                def load(w, ready):
                    one = slice(w, w + 1) if isinstance(w, int) else ds(w, 1)
                    for o in range(NO):
                        if o == NO - 1:
                            ready(s["conv_done"], NO - 2)
                            sp.dma_start(cw[:, :, :], g.inputs["conv_heads"][one].rearrange("h p (o k) -> p (h o) k", k=TAPS))\
                                .then_inc(s["cw_in"], 16)
                        ready(s["proj_done"], o)
                        src = g.inputs["w_heads"][one].rearrange("h p (o k n) -> p (h o) k n", o=NO, k=KT)
                        sp.dma_start(W[:, o], src[:, o]).then_inc(w_in[o], 16)

                def store(h, c, u):
                    sp.wait_ge(s["ot_done"], h * NC + (c + 1))
                    one = slice(h, h + 1) if isinstance(h, int) else ds(h, 1)
                    sp.dma_start(g.o_dram[one, :, :, c * CT:(c + 1) * CT].rearrange("o v b t -> v (o b) t"),
                                 OT[:, u]).then_inc(out_dma[u], 16)

                def scan_inputs(b, k):
                    n = b * 16 + k
                    wait(sp, s["da_done"], 2 * (n - 1))
                    wait_apart(sp, passed["sp"], s["bx_done"], n - 1)
                    one = slice(b, b + 1) if isinstance(b, int) else ds(b, 1)
                    if k % 4 == 0:
                        wait(sp, s["hc_done"], n)
                        src = g.bc_dram[one].rearrange("b (i n) l -> (b i) n l", i=2)[:, k // 4 * 4:k // 4 * 4 + 4, :]
                        sp.dma_start(bcq[:], src.partition_broadcast(P)).then_inc(s["bc_in"], 16)
                    sp.dma_start(dts[:, k % 2], g.dts_dram[one, k % 4].rearrange("b i p l -> p (b i) l"))\
                        .then_inc(dt_in[k % 2], 16)

                def flush(b, t):
                    sp.wait_ge(s["ys_done"], b * 16 + (13 + t))
                    one = slice(b, b + 1) if isinstance(b, int) else ds(b, 1)
                    sp.dma_start(g.y_dram[one, t].rearrange("b p l -> p (b l)"), ys[:, t]).then_inc(y_dma, 16)

                def span(b, first):
                    for k in range(16):
                        if not (first and k < 2):
                            scan_inputs(b, k)
                        h, c = b * 2 + k // NC, k % NC
                        if c == NC - 3 and not (isinstance(b, int) and b == B - 1 and k >= NC):
                            load(h + 1, lambda sem_, o: sp.wait_ge(sem_, h * (NC * NO) + ((NC - 1) * NO + o + 1)))
                        store(h, c, c % 2)
                        if k > 12:
                            flush(b, k - 13)
                    flush(b, 3)

                sp.sem_inc(y_dma, 16 * DT)
                load(0, lambda sem_, o: None)
                scan_inputs(0, 0)
                scan_inputs(0, 1)
                span(0, True)
                with sp.Fori(1, B - 1) as b:
                    span(b, False)
                span(B - 1, False)
                sp.wait_ge(y_dma, 16 * DT * (B + 1))
                for u in range(2):
                    sp.wait_ge(out_dma[u], 16 * NIT // 2)

            @block.gpsimd
            def _(pool):
                def link(sname, per, val, k, ins):
                    ins.then_inc(s[sname], 1)
                    wait_apart(pool, passed["pool"], s[sname], val(per, k))

                def body(pool, n, u, A=True, B_=True, C=True):
                    a, b, c = at(n, 2), at(n, 1), at(n, 0)
                    v = (u + 1) % 2
                    row = lambda m: g.tab[:, m:m + 1, :] if isinstance(m, int) else g.tab[:, ds(m, 1), :]
                    if B_:
                        wait(pool, s["s_done"], c(1, 0))
                        wait(pool, s["ys_done"], c(1, 0))
                        wait(pool, s["kn_done"], b(2, 0))
                        wait_apart(pool, passed["pool"], s["qn_done"], b(1, 0))
                        pool.tensor_copy(sc[:, v:v + 1, :], row(n + 1)).then_inc(s["sc_done"], 1)
                        pool.wait_ge(s["sc_done"], b(1, 1))
                        wait_apart(pool, passed["pool"], s["ss_done"], b(2, 1))
                        link("pool_link_b", 3, b, 1, pool.tensor_scalar(rr[:, 0:B], ss[:, 0:B], 4e-24, None, ALU.max))
                        pool.tensor_tensor(rr[:, 0:B], rr[:, 0:B], g.mhalf[:, 0:B], ALU.pow).then_inc(s["rk_done"], 1)
                        wait_apart(pool, passed["pool"], s["ss_done"], b(2, 2))
                        link("pool_link_b", 3, b, 2, pool.tensor_scalar(rr[:, B:6], ss[:, B:6], 4e-24, None, ALU.max))
                        link("pool_link_b", 3, b, 3, pool.tensor_tensor(rr[:, B:6], rr[:, B:6], g.mhalf[:, 0:2], ALU.pow))
                        pool.tensor_scalar(rq[:, 0, :], rr[:, B:6], DH ** -0.5, None, ALU.mult).then_inc(s["r_done"], 1)
                        pool.wait_ge(s["r_done"], b(2, 1))
                        pool.tensor_tensor(rq[:, 1, :], rq[:, 0, :], sc[:, v, 24:26], ALU.mult).then_inc(s["r_done"], 1)
                        wait(pool, s["so_done"], c(2, 0))
                        pool.wait_ge(s["kn_done"], b(2, 1))
                        pool.tensor_tensor(Kw[:, v], Kn[:], sc[:, v, 16:20].unsqueeze(2).to_broadcast([P, B, DH]),
                                           ALU.mult).then_inc(s["kw_done"], 1)
                    if C:
                        pool.wait_ge(dt_in[u], ((n >> 1) + 1) * 16)
                        pool.wait_ge(s["bc_in"], ((n >> 2) + 1) * 16)
                        wait(pool, s["ys_done"], c(1, 0))
                        pool.tensor_tensor(hs[:], dts[:, u, 1, :].unsqueeze(1).to_broadcast([P, 4, L]), bcq[:, 0],
                                           ALU.mult).then_inc(s["bx_done"], 1)
                        wait(pool, s["on_done"], c(1, 0))
                        wait_apart(pool, passed["pool"], s["oss_done"], c(1, 1))
                        link("pool_link_c", 1, c, 1,
                             pool.tensor_scalar(orr[:, :], oss[:, :], 1.0 / DH, EPS, ALU.mult, ALU.add))
                        pool.tensor_tensor(orr[:, :], orr[:, :], g.mhalf[:, 0:2], ALU.pow).then_inc(s["orr_done"], 1)
                    if A:
                        pool.tensor_copy(sd[:].unsqueeze(1), row(n + 2)[:, :, 0:8]).then_inc(s["sd_done"], 1)
                        pool.wait_ge(s["sd_done"], a(1, 1))
                        wait(pool, s["decay_done"], a(2, 0))
                        gb = lambda w: sd[:, 0:B].unsqueeze(2).to_broadcast([P, B, w])
                        up = g.upto[:, :].unsqueeze(1).to_broadcast([P, B, CM])
                        upq = g.upto[:, :].rearrange("p (t j) -> p t j", j=2)[:, :, 1].unsqueeze(1).to_broadcast([P, B, CT])
                        pool.tensor_tensor(Dr[:], up, gb(CM), ALU.mult)
                        link("pool_link_d", 2, a, 1,
                             pool.tensor_tensor(Dt[:], g.ident[:, :].unsqueeze(1).to_broadcast([P, B, CM]),
                                                sd[:, 4:8].unsqueeze(2).to_broadcast([P, B, CM]), ALU.mult))
                        link("pool_link_d", 2, a, 2, pool.tensor_tensor(Dr[:], Dr[:], Dt[:], ALU.add))
                        pool.tensor_tensor(Dq[:], upq, gb(CT), ALU.mult).then_inc(s["dr_done"], 1)
                    if C:
                        pool.wait_ge(s["hc_done"], c(1, 1))
                        t = ds((n & 3) * L, L) if not isinstance(n, int) else slice((n & 3) * L, (n & 3) * L + L)
                        yt = ys[:].rearrange("p t l -> p (t l)")[:, t]
                        pool.wait_ge(y_dma, (n >> 4) * (16 * DT) + 16 * DT)
                        link("ys_link", 3, c, 1, pool.tensor_tensor(hs[:, 0:2], hs[:, 0:2], hs[:, 2:4], ALU.add))
                        link("ys_link", 3, c, 2, pool.tensor_tensor(hs[:, 0], hs[:, 0], hs[:, 1], ALU.add))
                        link("ys_link", 3, c, 3, pool.tensor_tensor(yt, yt, sc[:, u, 26:27].to_broadcast([P, L]), ALU.mult))
                        pool.tensor_tensor(yt, yt, hs[:, 0], ALU.add).then_inc(s["ys_done"], 1)

                pool.wait_ge(s["ya_cleared"], 1)
                loops(pool, body)

            @block.tensor
            def _(pe):
                def body(pe, n, u, A=True, B_=True, C=True):
                    a, b, c = at(n, 2), at(n, 1), at(n, 0)
                    v = (u + 1) % 2

                    def proj(o, half):
                        if not A:
                            return
                        m = n + 2
                        if half == 0:
                            pe.wait_ge(w_in[o], ((m >> 3) + 1) * 16)
                            wait(pe, s["conv_done"], a(NO, o - 1))
                        off = (m & 7) * CT
                        for k in range(half * KT // 2, (half + 1) * KT // 2):
                            src = g.xT[:, k, :, off:off + CT + PAD] if isinstance(m, int) else g.xT[:, k, :, ds(off, CT + PAD)]
                            i = pe.matmul(proj_bank(o), W[:, o, k, :], src, start=(k == 0), stop=(k == KT - 1))
                        if half == 1:
                            i.then_inc(s["proj_done"], 1)

                    half_of = lambda x, half, s_: x.rearrange("p (j h s) -> p h j s", h=2, s=s_)[:, half]
                    out_of = lambda i, q, s_: bank[i][:, q * CT:(q + 1) * CT].rearrange("p (j s) -> p j s", s=s_)

                    def level_x(l):
                        if not B_:
                            return
                        if l == 0:
                            pe.wait_ge(s["at_done"], b(1, 1))
                        elif l > 1:
                            pe.wait_ge(s["tcopy_done"], b(LV - 1, l))
                        for q in range(B):
                            if l == 0:
                                i = pe.transpose(by_batch(bank[2])[:, q], At[:, q], g.ident[:, :])
                                continue
                            t = g.Xm[:, 0, q] if l == 1 else Tb[:, q]
                            i = pe.matmul(out_of(2, q, 1 << l), At[:, q], half_of(t, 0, 1 << l), start=True, stop=True)
                        i.then_inc(s["x_done"], 1)

                    def level_tr(l):
                        if not B_:
                            return
                        pe.wait_ge(s["xm_done"], b(LV, l + 1))
                        if l == 0:
                            for q in range(B):
                                i = pe.transpose(by_batch(bank[4])[:, q], g.Xm[:, 0, q], g.ident[:, :])
                            i.then_inc(s["rt_done"], 1)
                            return
                        pe.wait_ge(s["rcopy_done"], b(LV, l))
                        if l < LV - 1:
                            for q in range(B):
                                i = pe.matmul(out_of(3, q, 1 << l), Rf[:, v, q], half_of(g.Xm[:, l, q], 0, 1 << l),
                                              start=True, stop=True)
                            i.then_inc(s["t_done"], 1)
                        for q in range(B):
                            i = pe.matmul(out_of(4, q, 1 << l), g.Xm[:, l, q], half_of(Rf[:, v, q], 1, 1 << l),
                                          start=True, stop=True)
                        i.then_inc(s["rt_done"], 1)

                    def natural(bank_out, start, tiles, part, free):
                        if not B_:
                            return
                        pe.wait_ge(s["act_done"], b(3, part))
                        wait(pe, s[free[0]], free[1])
                        for q in range(tiles):
                            i = pe.transpose(bank_out[:, q * P:(q + 1) * P], kvq[:, v, start + q * P:start + (q + 1) * P],
                                             g.ident[:, :])
                        i.then_inc(s["natural_done"], 1)

                    natural(bank[2], K0, B, 1, ("xm_done", b(LV, 0)))
                    if C:
                        pe.wait_ge(s["kt_done"], c(1, 1))
                        wait(pe, s["s_done"], c(1, 0))
                        for q in range(B):
                            i = pe.matmul(by_batch(bank[5])[:, q], KTr[:, u, q], g.S[:, q], start=True, stop=True)
                        i.then_inc(s["ks_done"], 1)
                    natural(bank[4], Q0, 2, 3, ("rcopy_done", b(LV, 0)))
                    natural(bank[3], V0, B, 2, ("tcopy_done", b(LV - 1, 0)))
                    proj(0, 0)
                    if C:
                        pe.wait_ge(s["f_done"], c(1, 1))
                        pe.wait_ge(s["rcopy_done"], c(LV, LV))
                        pe.wait_ge(s["pt_done"], c(1, 1))
                        for q in range(B):
                            i = pe.matmul(by_batch(bank[6])[:, q], Rf[:, u, q], F[:, q], start=True, stop=True)
                        i.then_inc(s["u_done"], 1)
                    proj(0, 1)
                    if C:
                        pe.wait_ge(s["ucopy_done"], c(1, 1))
                        pe.wait_ge(s["kw_done"], c(1, 1))
                        for q in range(B):
                            i = pe.matmul(by_batch(bank[5])[:, q], Kw[:, u, q], U[:, q], start=True, stop=True)
                        i.then_inc(s["so_done"], 1)
                        wait(pe, s["ot_done"], c(1, 0))
                        O = pairs(bank[7][:, 0:256])
                        for q in range(B):
                            rows = slice((q % 2) * CT, (q % 2 + 1) * CT)
                            pe.matmul(O[rows, q // 2], QTr[:, u, 1, q // 2, rows], g.S[:, q], start=True, stop=False)
                            i = pe.matmul(O[rows, q // 2], PT[:, u, q], U[:, q], start=False, stop=True)
                        i.then_inc(s["so_done"], 1)
                    if B_:
                        pe.wait_ge(s["kn_done"], b(2, 1))
                        for q in range(B):
                            i = pe.transpose(by_batch(bank[2])[:, q], Kn[:, q], g.ident[:, :])
                        i.then_inc(s["turned"], 1)
                    proj(1, 0)
                    if B_:
                        pe.wait_ge(s["dr_done"], b(1, 1))
                        if C:
                            pe.wait_ge(s["s_done"], c(1, 1))
                        pe.matmul(bank[5][:, :], g.after[:, :], Dr[:].rearrange("p b n -> p (b n)"), start=True, stop=False)
                        pe.matmul(bank[5][:, :], g.identb[:, :], g.neg[:, :], start=False, stop=True)\
                            .then_inc(s["decay_done"], 1)
                        pe.matmul(bank[6][:, 256:512], g.after[:, :], Dq[:].rearrange("p b n -> p (b n)"), start=True, stop=False)
                        pe.matmul(bank[6][:, 256:512], g.identb[:, :], g.negq[:, :], start=False, stop=True)\
                            .then_inc(s["decay_done"], 1)
                        pe.wait_ge(s["kt_done"], b(1, 1))
                        pe.wait_ge(s["kn_done"], b(2, 2))
                        for q in range(B):
                            i = pe.matmul(by_batch(bank[3])[:, q], KTr[:, v, q], KTr[:, v, q], start=True, stop=True)
                        i.then_inc(s["gram_done"], 1)
                        pe.wait_ge(s["qn_done"], b(1, 1))
                        for q in range(4):
                            i = pe.transpose(by_batch(bank[4])[:, q], Qn[:, q // 2, q % 2], g.ident[:, :])
                        i.then_inc(s["turned"], 1)
                    proj(1, 1)
                    level_x(0)
                    proj(2, 0)
                    if B_:
                        pe.wait_ge(s["qt_done"], b(1, 1))
                        pe.wait_ge(s["e_done"], b(2, 2))
                        for q in range(B):
                            i = pe.matmul(bank[6][:, q * CT:(q + 1) * CT], KTr[:, v, q],
                                          QTr[:, v, 0, q // 2, (q % 2) * CT:(q % 2 + 1) * CT], start=True, stop=True)
                        i.then_inc(s["gram_done"], 1)
                    level_tr(0)
                    level_x(1)
                    proj(2, 1)
                    level_tr(1)
                    proj(3, 0)
                    level_x(2)
                    if C:
                        pe.wait_ge(s["on_done"], c(1, 1))
                        for q in range(2):
                            i = pe.transpose(bank[7][:, 256 + q * P:256 + (q + 1) * P], On[:, q], g.ident[:, :])
                        i.then_inc(s["ot_turned"], 1)
                    level_tr(2)
                    proj(3, 1)
                    level_x(3)
                    proj(4, 0)
                    level_tr(3)
                    level_x(4)
                    proj(4, 1)
                    level_tr(4)
                    level_x(5)
                    proj(5, 0)
                    level_tr(5)
                    level_x(6)
                    proj(5, 1)
                    level_tr(6)

                loops(pe, body)

            @block.scalar
            def _(act):
                act.wait_ge(s["ya_cleared"], 1)

                def body(act, n, u, A=True, B_=True, C=True):
                    a, b, c = at(n, 2), at(n, 1), at(n, 0)
                    v = (u + 1) % 2

                    def tap(o):
                        if A:
                            if o == 0:
                                act.wait_ge(s["cw_in"], ((n + 2 >> 3) + 1) * 16)
                            act.wait_ge(s["proj_done"], a(NO, o + 1))
                            if o == 0:
                                wait(act, s["act_done"], a(3, 0))
                            act.activation(conv_out(o), proj_bank(o)[:, :, PAD:], ACT.Copy,
                                           scale=cw[:, o, PAD:TAPS]).then_inc(s["tap_done"], 1)

                    def decay_of_state(j):
                        if not C:
                            return
                        if j == 0:
                            act.wait_ge(dt_in[u], ((n >> 1) + 1) * 16)
                        if j % 2 == 0:
                            wait(act, s["scan_done"], c(2, j // 2 - 1))
                        k = (n & 15) * 4 + j
                        i = act.activation(da[:, j, 1:], dts[:, u, 0, 1:], ACT.Exp,
                                           scale=g.a_neg[:, k:k + 1] if isinstance(k, int) else g.a_neg[:, ds(k, 1)])
                        if j % 2 == 1:
                            i.then_inc(s["da_done"], 1)

                    def rcopy(l):
                        if not B_:
                            return
                        pe_out = by_batch(bank[4]) if l == 0 else packed(bank[4], 1 << l)
                        act.wait_ge(s["rt_done"], b(LV, l + 1))
                        if l == 0:
                            wait(act, s["u_done"], c(1, 0))
                        dst = Rf[:, v] if l == 0 else blocks(Rf[:, v], 1, 1 << l)
                        act.activation(dst, pe_out, ACT.Copy).then_inc(s["rcopy_done"], 1)

                    def tcopy(l):
                        if not B_:
                            return
                        if l == 0:
                            act.wait_ge(s["xm_done"], b(LV, 1))
                            wait(act, s["x_done"], b(LV, 0))
                            act.activation(Tb[:], g.Xm[:, 0], ACT.Copy).then_inc(s["tcopy_done"], 1)
                        else:
                            act.wait_ge(s["t_done"], b(LV - 2, l))
                            if l == 1:
                                act.wait_ge(s["tcopy_done"], b(LV - 1, 1))
                            act.activation(blocks(Tb[:], 0, 1 << l), packed(bank[3], 1 << l), ACT.Copy)\
                                .then_inc(s["tcopy_done"], 1)

                    def tanh(part):
                        if not A:
                            return
                        lo, hi = PARTS[part]
                        act.wait_ge(s["conv_done"], a(NO, min(2 * part + 2, NO - 1)))
                        wait(act, s["act_done"], a(3, 0))
                        act.activation(th[:, lo:hi], cv[:, lo:hi], ACT.Tanh, scale=0.5).then_inc(s["tanh_done"], 1)

                    if B_:
                        wait(act, s["r_done"], b(2, 0))
                        act.wait_ge(s["natural_done"], b(3, 1))
                        for q in range(B):
                            i = act.activation(junk[:, q], by_batch(bank[2])[:, q], ACT.Square, accum_out=ss[:, q:q + 1])
                        i.then_inc(s["ss_done"], 1)
                        act.wait_ge(s["natural_done"], b(3, 2))
                        for q in range(2):
                            i = act.activation(junk[:, 4 + q], pairs(bank[4][:, 0:256])[:, q], ACT.Square,
                                               accum_out=ss[:, 4 + q:5 + q])
                        i.then_inc(s["ss_done"], 1)
                    if C:
                        act.wait_ge(s["u_done"], c(1, 1))
                        wait(act, s["so_done"], c(2, 0))
                        act.activation(U[:], by_batch(bank[6]), ACT.Copy).then_inc(s["ucopy_done"], 1)
                    tap(0)
                    for j in range(4):
                        decay_of_state(j)
                    if B_:
                        act.wait_ge(s["turned"], b(2, 1))
                        wait(act, s["ks_done"], c(1, 0))
                        act.activation(KTr[:, v], by_batch(bank[2]), ACT.Copy).then_inc(s["kt_done"], 1)
                        act.wait_ge(s["r_done"], b(2, 2))
                        for k in range(2):
                            for q in range(2):
                                i = act.activation(Qn[:, k, q], pairs(bank[4][:, 0:256])[:, q], ACT.Copy,
                                                   scale=rq[:, k, q:q + 1])
                        i.then_inc(s["qn_done"], 1)
                        act.wait_ge(s["decay_done"], b(2, 1))
                        wait(act, s["at_done"], b(1, 0))
                        act.activation(E_[:], by_batch(bank[5]), ACT.Exp).then_inc(s["e_done"], 1)
                        act.wait_ge(s["decay_done"], b(2, 2))
                        wait(act, s["pt_done"], b(1, 0))
                        act.activation(Eq[:], bank[6][:, 256:512].rearrange("p (b t) -> p b t", b=B), ACT.Exp)\
                            .then_inc(s["e_done"], 1)
                    if C:
                        act.wait_ge(s["so_done"], c(2, 2))
                        wait(act, s["orr_done"], c(1, 0))
                        for q in range(2):
                            i = act.activation(junk[:, 6 + q], pairs(bank[7][:, 0:256])[:, q], ACT.Square,
                                               accum_out=oss[:, q:q + 1])
                        i.then_inc(s["oss_done"], 1)
                    tap(1)
                    rcopy(0)
                    tcopy(0)
                    tcopy(1)
                    rcopy(1)
                    tap(2)
                    if C:
                        act.wait_ge(s["orr_done"], c(1, 1))
                        wait(act, s["ot_turned"], c(1, 0))
                        for q in range(2):
                            i = act.activation(On[:, q], pairs(bank[7][:, 0:256])[:, q], ACT.Copy, scale=orr[:, q:q + 1])
                        i.then_inc(s["on_done"], 1)
                    tcopy(2)
                    rcopy(2)
                    tanh(0)
                    tap(3)
                    tcopy(3)
                    rcopy(3)
                    tcopy(4)
                    rcopy(4)
                    tap(4)
                    tanh(1)
                    tcopy(5)
                    rcopy(5)
                    tanh(2)
                    rcopy(6)
                    if A:
                        act.wait_ge(s["proj_done"], a(NO, NO))
                        wait(act, s["conv_done"], a(NO, 0))
                        act.activation(gt[:], proj_bank(5)[:, :, PAD:], ACT.Tanh, scale=0.5).then_inc(s["gtanh_done"], 1)

                loops(act, body)

            @block.vector
            def _(dve):
                def body(dve, n, u, A=True, B_=True, C=True):
                    a, b, c = at(n, 2), at(n, 1), at(n, 0)
                    v = (u + 1) % 2

                    def conv(o, *steps):
                        if not A:
                            return
                        for k in steps:
                            if k == 0:
                                dve.wait_ge(s["tap_done"], a(NO - 1, o + 1))
                            else:
                                dve.wait_ge(s["conv_link"], a(2 * (NO - 1), 2 * o + k))
                            dve.scalar_tensor_tensor(conv_out(o), proj_bank(o)[:, :, k:k + CT], cw[:, o, k:k + 1],
                                                     conv_out(o), ALU.mult, ALU.add)\
                                .then_inc(s["conv_link" if k < PAD - 1 else "conv_done"], 1)

                    def masked(l):
                        if B_:
                            wait_apart(dve, passed["dve"], s["x_done"], b(LV, l + 1))
                            mask = g.levels[:, l].rearrange("p (j s) -> p j s", s=1 << l).unsqueeze(1)\
                                .to_broadcast([P, B, CT >> l, 1 << l])
                            dve.copy_predicated(blocks(g.Xm[:, l], 0, 1 << l), mask,
                                                blocks(by_batch(bank[2]), 0, 1) if l == 0 else packed(bank[2], 1 << l))\
                                .then_inc(s["xm_done"], 1)

                    def activated(part):
                        if not A:
                            return
                        lo, hi = PARTS[part]
                        dve.wait_ge(s["tanh_done"], a(3, part + 1))
                        wait(dve, s["natural_done"], a(3, -3))
                        dve.scalar_tensor_tensor(kvq[:, u, lo:hi], th[:, lo:hi], 1.0, cv[:, lo:hi], ALU.add, ALU.mult)\
                            .then_inc(s["act_done"], 1)

                    def gate():
                        if A:
                            dve.wait_ge(s["gtanh_done"], a(1, 1))
                            dve.scalar_tensor_tensor(gs[:, u], gt[:], 1.0, proj_bank(5)[:, :, PAD:], ALU.add, ALU.mult)\
                                .then_inc(s["conv_done"], 1)

                    flat = lambda x: x.rearrange("p n l -> p (n l)")

                    def scan(h):
                        if not C:
                            return
                        two = slice(2 * h, 2 * h + 2)
                        dve.wait_ge(s["da_done"], c(2, h + 1))
                        if h == 0:
                            dve.wait_ge(s["bx_done"], c(1, 1))
                        dve.tensor_tensor_scan(flat(hs[:, two]), flat(da[:, two]), flat(hs[:, two]), 0.0, ALU.mult, ALU.add)\
                            .then_inc(s["scan_done"], 1)

                    def read_out(h):
                        if not C:
                            return
                        two = slice(2 * h, 2 * h + 2)
                        dve.wait_ge(s["scan_done"], c(2, h + 1))
                        i = dve.tensor_tensor(hs[:, two], hs[:, two], bcq[:, 1, two], ALU.mult)
                        if h == 1:
                            i.then_inc(s["hc_done"], 1)

                    if C:
                        dve.wait_ge(s["ks_done"], c(1, 1))
                        wait(dve, s["u_done"], c(1, 0))
                        for q in range(B):
                            i = dve.scalar_tensor_tensor(F[:, q], by_batch(bank[5])[:, q], sc[:, u, 12 + q:13 + q],
                                                         Vb[:, u, q], ALU.mult, ALU.add)
                        i.then_inc(s["f_done"], 1)
                    if B_:
                        bc = lambda x: x.unsqueeze(2).to_broadcast([P, B, DH])
                        dve.wait_ge(s["rk_done"], b(1, 1))
                        wait(dve, s["turned"], b(2, 0))
                        wait(dve, s["kw_done"], b(1, 0))
                        dve.tensor_tensor(Kn[:], by_batch(bank[2]), bc(rr[:, 0:B]), ALU.mult).then_inc(s["kn_done"], 1)
                        dve.wait_ge(s["natural_done"], b(3, 3))
                        dve.tensor_tensor(Vb[:, v], by_batch(bank[3]), bc(sc[:, v, 8:12]), ALU.mult)\
                            .then_inc(s["kn_done"], 1)
                    conv(0, 0, 1, 2)
                    if C:
                        dve.wait_ge(s["so_done"], c(2, 2))
                        for q in range(B):
                            i = dve.scalar_tensor_tensor(g.S[:, q], g.S[:, q], sc[:, u, 20 + q:21 + q],
                                                         by_batch(bank[5])[:, q], ALU.mult, ALU.add)
                        i.then_inc(s["s_done"], 1)
                    if B_:
                        dve.wait_ge(s["gram_done"], b(2, 1))
                        dve.wait_ge(s["e_done"], b(2, 1))
                        wait(dve, s["x_done"], b(LV, 0))
                        dve.scalar_tensor_tensor(At[:], by_batch(bank[3]), -1.0, E_[:], ALU.mult, ALU.mult)\
                            .then_inc(s["at_done"], 1)
                        dve.wait_ge(s["turned"], b(2, 2))
                        dve.tensor_copy(QTr[:, v].rearrange("p k q n -> p (k q) n"), by_batch(bank[4]))\
                            .then_inc(s["qt_done"], 1)
                    masked(0)
                    conv(1, 0, 1, 2)
                    if B_:
                        dve.wait_ge(s["gram_done"], b(2, 2))
                        dve.wait_ge(s["e_done"], b(2, 2))
                        dve.tensor_tensor(PT[:, v], bank[6][:, 0:256].rearrange("p (b t) -> p b t", b=B), Eq[:],
                                          ALU.mult).then_inc(s["pt_done"], 1)
                    masked(1)
                    scan(0)
                    conv(2, 0, 1, 2)
                    masked(2)
                    scan(1)
                    activated(0)
                    masked(3)
                    read_out(0)
                    conv(3, 0, 1, 2)
                    masked(4)
                    if C:
                        dve.wait_ge(s["ot_turned"], c(1, 1))
                        wait(dve, out_dma[u], (n >> 1) * 16)
                        dve.scalar_tensor_tensor(OT[:, u], bank[7][:, 256:512].rearrange("p (b t) -> p b t", b=B),
                                                 g.normw[:, 0:1], gs[:, u], ALU.mult, ALU.mult).then_inc(s["ot_done"], 1)
                    read_out(1)
                    activated(1)
                    masked(5)
                    conv(4, 0, 1, 2)
                    masked(6)
                    activated(2)
                    gate()

                dve.memset(da[:, :, 0:1], 0.0)
                dve.memset(ys[:], 0.0).then_inc(s["ya_cleared"], 1)
                loops(dve, body)


def combine(nc, g):
    NT = L // P
    with ExitStack() as ctx:
        sb = lambda name, shape, dt=F32: ctx.enter_context(nc.sbuf_tensor(name, shape, dt))
        pb = lambda name, shape, dt=F32: ctx.enter_context(nc.psum_tensor(name, shape, dt))
        sem = lambda name: ctx.enter_context(nc.semaphore(name))
        wo = sb("wo", [P, H, HID])
        gw = sb("gw", [P, KT, NE])
        ot = sb("ot", [P, 2, H, P])
        xr = sb("xr", [P, 2, HID])
        yr = sb("yr", [P, 2, 2, L])
        x1 = sb("x1", [P, NT, HID])
        st = sb("cst", [P, 2, NT, 6])
        mv = sb("cmv", [P, 2, NT, 2])
        rs = sb("crs", [P, 2, NT])
        z = sb("z", [P, NT, HID])
        zt = sb("zt", [P, NT, HID])
        yd = sb("yd", [P, NT, L])
        w = sb("w", [P, NT, L])
        x2 = sb("x2", [P, 2 * NT, HID])
        xh = sb("xh", [P, NT, HID])
        xhT = sb("xhT", [P, 2, NT, KT, P])
        mean = sb("mean", [P, NT, KT])
        msum = sb("msum", [P, KT])
        lg = sb("lg", [1, 8])
        top = sb("top", [1, 8])
        idx = sb("idx", [1, 8], U32)
        dl = sb("dl", [1, 8])
        pr = sb("pr", [1, 8])
        tot = sb("tot", [1, 4])
        wrow = sb("wrow", [1, 2, P])
        wcol = sb("wcol", [P, 2])
        w1 = sb("w1", [P, 2, KT, FF])
        w2 = sb("w2", [P, 2, len(FT), HID])
        b1 = sb("b1", [P, 2, len(FT)])
        b2 = sb("b2", [1, 2, HID])
        hT = sb("hT", [P, 2, len(FT), L])
        bb = sb("bb", [P, HID])
        res = sb("res", [P, 2, HID])
        bank = [pb(f"cbank{i}", [P, 512]) for i in range(8)]
        names = ("w_in", "wo_done", "x1_done", "var_done", "rs_done", "z_done", "zt_done", "yd_done", "w_done",
                 "wt_done", "x2_done", "var2_done", "rs2_done", "xh_done", "xht_done", "xhT_done", "mean_done",
                 "lg_done", "lg_copied", "dl_done", "pr_done", "wr_done", "wc_done", "wcol_done", "h_done",
                 "gelu_done", "hs_done", "b2_done", "bb_done", "x2b_done", "o_done", "res_done", "x_link",
                 "g_link", "act_link", "pad_done", "expert_in", "s2_done")
        passed = {k: sem(f"c_passed_{k}") for k in ("sp", "pool", "dve")}
        s = {k: sem("c_" + k) for k in names}
        tile_in = [sem("tile_in0"), sem("tile_in1")]
        res_dma = [sem("res_dma0"), sem("res_dma1")]

        def run(eng, X=None, G=None, Y=None):
            go = lambda f, n, off: f and f(n + off, at(n, off))
            go(X, 0, 0)
            go(G, 0, 0)
            go(X, 0, 1)
            go(Y, 0, 0)
            go(G, 0, 1)
            with eng.Fori(1, B - 1) as n:
                go(X, n, 1)
                go(Y, n, 0)
                go(G, n, 1)
            go(Y, B - 1, 0)

        def half(m):
            return (m & 1) * NT

        def pick(a, start):
            return a[:, start] if isinstance(start, int) else a[:, ds(start, 1)].rearrange("p o n -> p (o n)")

        with nc.Block() as block:
            @block.sync
            def _(sp):
                sp.dma_start(wo[:], g.inputs["w_o"]).then_inc(s["w_in"], 16)
                sp.dma_start(gw[:], g.inputs["gate_w"]).then_inc(s["w_in"], 16)

                def X(m, v):
                    one = slice(m, m + 1) if isinstance(m, int) else ds(m, 1)
                    for t in range(NT):
                        wait(sp, s["wo_done"], v(NT, t - 1))
                        wait(sp, s["x1_done"], v(NT, t - 1))
                        wait(sp, s["yd_done"], v(NT, t - 1))
                        u = t % 2
                        src = g.o_dram[:, :, one, t * P:(t + 1) * P]
                        sp.dma_start(ot[:, u], src.rearrange("h v b t -> v h (b t)")).then_inc(tile_in[u], 16)
                        sp.dma_start(xr[:, u], g.inputs["x"].rearrange("(b t p) d -> b t p d", b=B, p=P)[one, t]
                                     .rearrange("b p d -> p (b d)")).then_inc(tile_in[u], 16)
                        sp.dma_start(yr[:, u, 0], g.y_dram[one, t].rearrange("b p l -> p (b l)")).then_inc(tile_in[u], 16)
                        sp.dma_start(yr[:, u, 1], g.ud_dram[one, t].rearrange("b p l -> p (b l)")).then_inc(tile_in[u], 16)

                def G(m, v):
                    wait(sp, s["o_done"], v(NT, 0))
                    wait_apart(sp, passed["sp"], s["g_link"], v(9, 3))
                    for k in range(2):
                        e = sp.value_load(idx[0:1, k:k + 1], min_val=0, max_val=NE - 1)
                        one = ds(e, 1)
                        sp.dma_start(w1[:, k], g.inputs["w1"][one].rearrange("e p k n -> p (e k) n")).then_inc(s["expert_in"], 16)
                        sp.dma_start(w2[:, k], g.inputs["w2"][one].rearrange("e p k n -> p (e k) n")).then_inc(s["expert_in"], 16)
                        sp.dma_start(b1[:, k], g.inputs["b1"][one].rearrange("e p k -> p (e k)")).then_inc(s["expert_in"], 16)
                        sp.dma_start(b2[:, k], g.inputs["b2"][one]).then_inc(s["expert_in"], 16)

                def Y(m, v):
                    one = slice(m, m + 1) if isinstance(m, int) else ds(m, 1)
                    for t in range(NT):
                        sp.wait_ge(s["res_done"], v(NT, t + 1))
                        dst = g.out[one, t * P:(t + 1) * P, :].rearrange("b p d -> p (b d)")
                        sp.dma_start(dst, res[:, t % 2]).then_inc(res_dma[t % 2], 16)

                run(sp, X, G, Y)
                for u in range(2):
                    sp.wait_ge(res_dma[u], 16 * B * NT // 2)

            @block.tensor
            def _(pe):
                pe.wait_ge(s["w_in"], 32)

                def X(m, v):
                    for t in range(NT):
                        pe.wait_ge(tile_in[t % 2], v(128, 64 * (t // 2 + 1)))
                        wait(pe, s["x1_done"], v(NT, t - 1))
                        for h in range(H):
                            i = pe.matmul(bank[t % 2][:, :], ot[:, t % 2, h], wo[:, h], start=(h == 0), stop=(h == H - 1))
                        i.then_inc(s["wo_done"], 1)
                    pe.wait_ge(s["w_done"], v(NT, NT))
                    for t in range(NT):
                        wait(pe, s["x2_done"], v(NT, t - 1))
                        if t < 2:
                            wait(pe, s["xhT_done"], v(NT, t - 1))
                        for k in range(NT):
                            i = pe.transpose(bank[2 + t % 2][:, k * P:(k + 1) * P], w[:, k, t * P:(t + 1) * P], g.ident[:, :])
                        i.then_inc(s["wt_done"], 1)
                    for t in range(NT):
                        pe.wait_ge(s["xh_done"], v(NT, t + 1))
                        if t < 2:
                            pe.wait_ge(s["x2_done"], v(NT, t + 3))
                        else:
                            pe.wait_ge(s["xhT_done"], v(NT, t - 1))
                        for k in range(KT):
                            i = pe.transpose(bank[2 + t % 2][:, k * P:(k + 1) * P], xh[:, t, k * P:(k + 1) * P], g.ident[:, :])
                        i.then_inc(s["xht_done"], 1)

                def G(m, v):
                    pe.wait_ge(s["mean_done"], v(1, 1))
                    wait(pe, s["wcol_done"], v(1, 0))
                    for k in range(KT):
                        i = pe.matmul(bank[7][0:1, 0:NE], msum[:, k:k + 1], gw[:, k, :], start=(k == 0), stop=(k == KT - 1))
                    i.then_inc(s["lg_done"], 1)
                    pe.wait_ge(s["wr_done"], v(1, 1))
                    for k in range(2):
                        i = pe.matmul(bank[7][:, 8 + k:9 + k], wrow[:, k], g.ones[0:1, 0:1], start=True, stop=True)
                    i.then_inc(s["wc_done"], 1)

                def Y(m, v):
                    pe.wait_ge(s["expert_in"], v(128, 128))
                    wait(pe, s["bb_done"], v(1, 0))
                    for k in range(2):
                        i = pe.matmul(bank[6][:, :], wrow[:, k], b2[:, k], start=(k == 0), stop=(k == 1))
                    i.then_inc(s["b2_done"], 1)
                    for j in range(2 * len(FT)):
                        k, f = divmod(j, len(FT))
                        lo, n = FT[f]
                        if j < 2:
                            wait(pe, s["res_done"], v(NT, 0))
                        else:
                            pe.wait_ge(s["gelu_done"], v(2 * len(FT), j - 1))
                        for q in range(KT):
                            start = (m & 1) * NT
                            rhs = xhT[:, m & 1, :, q] if isinstance(m, int) else \
                                xhT[:, ds(m & 1, 1), :, q].rearrange("p o t n -> p (o t) n")
                            i = pe.matmul(bank[4 + j % 2][0:n, :], w1[:, k, q, lo:lo + n], rhs, start=(q == 0), stop=(q == KT - 1))
                        i.then_inc(s["h_done"], 1)
                    pe.wait_ge(s["hs_done"], v(2 * len(FT), 2 * len(FT)))
                    for t in range(NT):
                        if t > 1:
                            pe.wait_ge(s["res_done"], v(NT, t - 1))
                        for j in range(2 * len(FT)):
                            k, f = divmod(j, len(FT))
                            n = FT[f][1]
                            i = pe.matmul(bank[4 + t % 2][:, :], hT[0:n, k, f, t * P:(t + 1) * P], w2[0:n, k, f, :],
                                          start=(j == 0), stop=(j == 2 * len(FT) - 1))
                        i.then_inc(s["o_done"], 1)

                run(pe, X, G, Y)

            @block.gpsimd
            def _(pool):
                def X(m, v):
                    for t in range(NT):
                        pool.wait_ge(tile_in[t % 2], v(128, 64 * (t // 2 + 1)))
                        if t == 0:
                            wait(pool, s["w_done"], v(NT, 0))
                        pool.tensor_tensor(yd[:, t], yr[:, t % 2, 0], yr[:, t % 2, 1], ALU.add).then_inc(s["yd_done"], 1)
                    pool.wait_ge(s["var_done"], v(1, 1))
                    pool.tensor_tensor(rs[:, 0], rs[:, 0], g.mhalf[:, 0:NT], ALU.pow).then_inc(s["rs_done"], 1)
                    pool.wait_ge(s["var2_done"], v(1, 1))
                    pool.tensor_tensor(rs[:, 1], rs[:, 1], g.mhalf[:, 0:NT], ALU.pow).then_inc(s["rs2_done"], 1)

                def Y(m, v):
                    wait_apart(pool, passed["pool"], s["bb_done"], v(1, 1))
                    for t in range(NT):
                        x = pick(x2, half(m) + t)
                        pool.tensor_tensor(x, x, bb[:, :], ALU.add).then_inc(s["x2b_done"], 1)

                run(pool, X, None, Y)

            @block.scalar
            def _(act):
                def X(m, v):
                    for t in range(NT):
                        act.wait_ge(s["z_done"], v(NT, t + 1))
                        act.activation(zt[:, t], z[:, t], ACT.Tanh, scale=0.5).then_inc(s["zt_done"], 1)
                    for t in range(NT):
                        act.wait_ge(s["xht_done"], v(NT, t + 1))
                        if t == 0:
                            wait(act, s["h_done"], v(2 * len(FT), -2 * len(FT)))
                        dst = xhT[:, m & 1, t] if isinstance(m, int) else \
                            xhT[:, ds(m & 1, 1), t].rearrange("p o k n -> p (o k) n")
                        act.activation(dst, bank[2 + t % 2][:, :].rearrange("p (k n) -> p k n", k=KT), ACT.Copy)\
                            .then_inc(s["xhT_done"], 1)

                def G(m, v):
                    act.wait_ge(s["dl_done"], v(1, 1))
                    act.activation(pr[:, :], dl[:, :], ACT.Exp, accum_out=tot[:, 0:1]).then_inc(s["pr_done"], 1)

                def Y(m, v):
                    act.wait_ge(s["b2_done"], v(1, 1))
                    wait(act, s["x2b_done"], v(NT, 0))
                    act.activation(bb[:, :], bank[6][:, :], ACT.Copy).then_inc(s["bb_done"], 1)
                    for j in range(2 * len(FT)):
                        k, f = divmod(j, len(FT))
                        n = FT[f][1]
                        act.wait_ge(s["h_done"], v(2 * len(FT), j + 1))
                        if j == 0:
                            wait(act, s["o_done"], v(NT, 0))
                        act.activation(hT[0:n, k, f, :], bank[4 + j % 2][0:n, :], ACT.Gelu, bias=b1[0:n, k, f:f + 1])\
                            .then_inc(s["gelu_done"], 1)

                run(act, X, G, Y)

            @block.vector
            def _(dve):
                XL = 2 * (NT * 2)

                def norm(src, j, v, base):
                    for t in range(NT):
                        dve.bn_stats(st[:, j, t, :], src(t)).then_inc(s["x_link"], 1)
                        wait_apart(dve, passed["dve"], s["x_link"], v(XL, base + 2 * t + 1))
                        dve.bn_aggr(mv[:, j, t, :], st[:, j, t, :]).then_inc(s["x_link"], 1)
                    dve.wait_ge(s["x_link"], v(XL, base + 2 * NT))
                    dve.tensor_scalar(rs[:, j], mv[:, j, :, 1], EPS, None, ALU.add)\
                        .then_inc(s["var_done" if j == 0 else "var2_done"], 1)

                def X(m, v):
                    for t in range(NT):
                        dve.wait_ge(s["wo_done"], v(NT, t + 1))
                        dve.tensor_tensor(x1[:, t], bank[t % 2][:, :], xr[:, t % 2], ALU.add).then_inc(s["x1_done"], 1)
                    wait_apart(dve, passed["dve"], s["x1_done"], v(NT, NT))
                    norm(lambda t: x1[:, t], 0, v, 0)
                    dve.wait_ge(s["rs_done"], v(1, 1))
                    for t in range(NT):
                        dve.tensor_scalar(z[:, t], x1[:, t], mv[:, 0, t, 0:1], rs[:, 0, t:t + 1],
                                          ALU.subtract, ALU.mult).then_inc(s["z_done"], 1)
                    for t in range(NT):
                        dve.wait_ge(s["zt_done"], v(NT, t + 1))
                        dve.scalar_tensor_tensor(z[:, t], zt[:, t], 1.0, z[:, t], ALU.add, ALU.mult)\
                            .then_inc(s["s2_done"], 1)
                    for t in range(NT):
                        dve.wait_ge(s["s2_done"], v(NT, t + 1))
                        dve.wait_ge(s["yd_done"], v(NT, t + 1))
                        if t == 0:
                            wait(dve, s["wt_done"], v(NT, 0))
                        dve.scalar_tensor_tensor(w[:, t], yd[:, t], 0.5, z[:, t], ALU.mult, ALU.mult)\
                            .then_inc(s["w_done"], 1)
                    for t in range(NT):
                        dve.wait_ge(s["wt_done"], v(NT, t + 1))
                        dve.tensor_tensor(pick(x2, half(m) + t), bank[2 + t % 2][:, :], x1[:, t], ALU.add)\
                            .then_inc(s["x2_done"], 1)
                    wait_apart(dve, passed["dve"], s["x2_done"], v(NT, NT))
                    norm(lambda t: pick(x2, half(m) + t), 1, v, 2 * NT)
                    dve.wait_ge(s["rs2_done"], v(1, 1))
                    wait(dve, s["xht_done"], v(NT, 0))
                    for t in range(NT):
                        dve.tensor_scalar(xh[:, t], pick(x2, half(m) + t), mv[:, 1, t, 0:1], rs[:, 1, t:t + 1],
                                          ALU.subtract, ALU.mult).then_inc(s["xh_done"], 1)

                def G(m, v):
                    def link(k, ins):
                        ins.then_inc(s["g_link"], 1)
                        wait_apart(dve, passed["dve"], s["g_link"], v(9, k))

                    dve.wait_ge(s["xhT_done"], v(NT, NT))
                    src = xhT[:, m & 1] if isinstance(m, int) else \
                        xhT[:, ds(m & 1, 1)].rearrange("p o t k n -> p (o t) k n")
                    link(1, dve.tensor_reduce(mean[:], src, AX.X, ALU.add))
                    wait(dve, s["lg_done"], v(1, 0))
                    dve.tensor_reduce(msum[:, :], mean[:].rearrange("p t k -> p k t"), AX.X, ALU.add)\
                        .then_inc(s["mean_done"], 1)
                    dve.wait_ge(s["lg_done"], v(1, 1))
                    wait(dve, s["expert_in"], v(128, 0))
                    link(2, dve.tensor_scalar(lg[:, 0:NE], bank[7][0:1, 0:NE], 1.0 / L, None, ALU.mult))
                    dve.max(top[:, :], lg[:, :]).then_inc(s["lg_copied"], 1)
                    wait_apart(dve, passed["dve"], s["lg_copied"], v(1, 1))
                    link(3, dve.max_index(idx[:, :], top[:, :], lg[:, :]))
                    dve.tensor_scalar(dl[:, :], top[:, :], top[:, 0:1], None, ALU.subtract).then_inc(s["dl_done"], 1)
                    dve.wait_ge(s["pr_done"], v(1, 1))
                    link(4, dve.reciprocal(tot[:, 1:2], tot[:, 0:1]))
                    link(5, dve.tensor_scalar(pr[:, :], pr[:, :], tot[:, 1:2], None, ALU.mult))
                    link(6, dve.tensor_tensor(tot[:, 2:3], pr[:, 0:1], pr[:, 1:2], ALU.add))
                    link(7, dve.reciprocal(tot[:, 3:4], tot[:, 2:3]))
                    link(8, dve.tensor_scalar(pr[:, 0:2], pr[:, 0:2], tot[:, 3:4], None, ALU.mult))
                    wait(dve, s["b2_done"], v(1, 0))
                    dve.tensor_copy(wrow[:], pr[:, 0:2].unsqueeze(2).to_broadcast([1, 2, P])).then_inc(s["wr_done"], 1)
                    dve.wait_ge(s["wc_done"], v(1, 1))
                    link(9, dve.tensor_copy(wcol[:, :], bank[7][:, 8:10]))
                    dve.nop().then_inc(s["wcol_done"], 1)

                def Y(m, v):
                    for j in range(2 * len(FT)):
                        k, f = divmod(j, len(FT))
                        n = FT[f][1]
                        dve.wait_ge(s["gelu_done"], v(2 * len(FT), j + 1))
                        dve.tensor_scalar(hT[0:n, k, f, :], hT[0:n, k, f, :], wcol[0:n, k:k + 1], None, ALU.mult)\
                            .then_inc(s["hs_done"], 1)
                    for t in range(NT):
                        dve.wait_ge(s["o_done"], v(NT, t + 1))
                        dve.wait_ge(s["x2b_done"], v(NT, t + 1))
                        wait(dve, res_dma[t % 2], v(32, 16 * (t // 2)))
                        dve.tensor_tensor(res[:, t % 2], bank[4 + t % 2][:, :], pick(x2, half(m) + t), ALU.add)\
                            .then_inc(s["res_done"], 1)

                dve.memset(lg[:, :], -1e30).then_inc(s["pad_done"], 1)
                dve.wait_ge(s["pad_done"], 1)
                run(dve, X, G, Y)


class Shared:

    def __init__(self, inputs):
        self.inputs = inputs


def build(nc, arrays, out):
    g = Shared(arrays)
    g.log1p = log1p_coefficients()
    g.log1p_factors = log1p_factors()
    g.ln2 = 0.6931471805599453
    g.out = out
    internal = lambda name, shape: nc.dram_tensor(name, shape, F32, kind="Internal").ap()
    g.dts_dram = internal("dts_scratch", (B, DT, 2, P, L))
    g.ud_dram = internal("ud_scratch", (B, DT, P, L))
    g.bc_dram = internal("bc_scratch", (B, 2 * DS, L))
    g.y_dram = internal("y_scratch", (B, DT, P, L))
    g.o_dram = nc.dram_tensor("o_scratch", (H, DH, B, L), F32, kind="Internal").ap()
    with ExitStack() as ctx:
        sb = lambda name, shape, dt=F32: ctx.enter_context(nc.sbuf_tensor(name, shape, dt))
        g.ident = sb("ident", [P, P])
        g.identb = sb("identb", [P, P], BF16)
        g.ones = sb("ones", [P, P])
        g.mhalf = sb("mhalf", [P, NTT])
        state_inputs(nc, g)
        with ExitStack() as inner:
            sb = lambda name, shape, dt=F32: inner.enter_context(nc.sbuf_tensor(name, shape, dt))
            g.upto = sb("upto", [P, CM])
            g.after = sb("after", [P, CM])
            g.neg = sb("neg", [P, B * CM], BF16)
            g.negq = sb("negq", [P, B * CT], BF16)
            g.levels = sb("levels", [P, LV, CT], U32)
            g.normw = sb("normw", [P, 1])
            g.xT = sb("xT", [P, KT, B, TW])
            g.tab = sb("tab", [P, NIT, 27])
            g.a_neg = sb("a_neg", [P, DT * DS])
            g.Xm = sb("Xm", [P, LV, B, CM])
            g.S = sb("S", [P, B, DH])
            prepare(nc, g)
            delta(nc, g)
        combine(nc, g)


def constants():
    import numpy as np
    i = np.arange(P)
    levels = np.zeros((P, LV, CT), np.uint32)
    for l in range(LV):
        s = 1 << l
        levels[:, l, :] = (i[:, None] // (2 * s) == i[None, :CT] // s) & (i[:, None] // s % 2 == 1)
    neg = np.where(i[:, None] >= i[None, :], -30000.0, 0.0)
    negq = np.where(i[:, None] > 2 * np.arange(CT)[None, :] + 1, -30000.0, 0.0)
    first = np.ones((P, NIT), np.float32)
    first[:, ::NC] = 0
    flag = np.tile((np.arange(NIT) // 4 % 4 != 0).astype(np.float32), (P, 1))
    return dict(
        c_ident=np.eye(P, dtype=np.float32),
        c_ones=np.ones((P, P), np.float32),
        c_upto=(i[:, None] <= i[None, :]).astype(np.float32), c_after=(i[:, None] > i[None, :]).astype(np.float32),
        c_neg=neg.astype(np.float32), c_negq=negq.astype(np.float32),
        c_levels=levels, c_parity=np.stack([i % 2 == 0, i % 2 == 1], 1).astype(np.float32), c_first=first, c_flag=flag)


def laid_out(v):
    import numpy as np
    f = {k: np.asarray(a) for k, a in v.items()}
    per_head = lambda w: w.reshape(KT, P, -1, P).transpose(2, 1, 0, 3)
    a = "L0_attn_"
    q, k, vv, gg = (per_head(f[a + n]) for n in ("Wq", "Wk", "Wv", "Wg"))
    heads = np.stack([k[:H], k[H:], vv[:H], vv[H:], q, gg], 2)
    cq, ck, cvw = (f[a + n].reshape(-1, P, TAPS) for n in ("conv_q_w", "conv_k_w", "conv_v_w"))
    convs = np.stack([ck[:H], ck[H:], cvw[:H], cvw[H:], cq], 2)
    out = dict(
        x=f["x"].reshape(B * L, HID), w_heads=heads.reshape(H, P, -1), conv_heads=convs.reshape(H, P, -1),
        w_gates=np.concatenate([f[a + "Wb"], f[a + "Wa"]], 1).reshape(KT, P, NG).transpose(1, 0, 2),
        dt_bias=f[a + "dt_bias"], a_log=f[a + "A_log"], norm_w=f[a + "norm_w"].reshape(P, 1),
    )
    m = "L0_xattn_"
    tiles = lambda w: w.reshape(DT, P, -1).transpose(1, 0, 2)
    out.update(
        ctxT=f["ctx_1024"].reshape(B * L, CTXT, P).transpose(2, 1, 0),
        in_w=f[m + "in_proj_w"].T.reshape(CTXT, P, DI).transpose(1, 0, 2),
        s_conv=tiles(f[m + "conv_w"]), s_convb=f[m + "conv_b"].reshape(DT, P).T,
        x_w=tiles(f[m + "x_proj_w"].T), dt_w=f[m + "dt_proj_w"].T, dt_b=f[m + "dt_proj_b"].reshape(DT, P).T,
        s_d=f[m + "D"].reshape(DT, P).T, s_alog=tiles(f[m + "A_log"]).reshape(P, DT, 4, 4).transpose(0, 2, 1, 3).reshape(P, -1),
    )
    e = "L0_ffn_"
    pad = len(FT) * P - FF
    out.update(
        w_o=f[a + "Wo"].reshape(H, DH, HID).transpose(1, 0, 2), gate_w=f[e + "gate_W"].T.reshape(KT, P, NE).transpose(1, 0, 2),
        w1=f[e + "W1"].reshape(NE, KT, P, FF).transpose(0, 2, 1, 3),
        w2=np.pad(f[e + "W2"], ((0, 0), (0, pad), (0, 0))).reshape(NE, len(FT), P, HID).transpose(0, 2, 1, 3),
        b1=np.pad(f[e + "b1"], ((0, 0), (0, pad))).reshape(NE, len(FT), P).transpose(0, 2, 1), b2=f[e + "b2"],
    )
    out.update(constants())
    return {n: np.ascontiguousarray(x) for n, x in out.items()}


def kernel(**inputs):
    import concourse.bacc as bacc
    import numpy as np
    from concourse.bass_utils import run_bass_kernel_spmd

    nc = bacc.Bacc("TRN2", target_bir_lowering=False, num_devices=1)
    arrays = laid_out(inputs)
    aps = {n: nc.dram_tensor("in_" + n, x.shape, mybir.dt.from_np(x.dtype), kind="ExternalInput").ap()
           for n, x in arrays.items()}
    out = nc.dram_tensor("out", (B, L, HID), F32, kind="ExternalOutput").ap()
    build(nc, aps, out)
    r = run_bass_kernel_spmd(nc, [{"in_" + n: x for n, x in arrays.items()}], core_ids=[0])
    return r.results[0]["out"]
```

```python
from contextlib import ExitStack

import concourse.bass as bass
from concourse import mybir
from concourse.bass import ds

F32 = mybir.dt.float32
BF16 = mybir.dt.bfloat16
U32 = mybir.dt.uint32
ALU = mybir.AluOpType
ACT = mybir.ActivationFunctionType
AX = mybir.AxisListType

P = 128
B, L, HID = 4, 512, 512
KT = HID // P
H, DH, NHH = 8, 128, 2
TAPS = 4
CT = 64
CM = CT * NHH
NC = L // CT
NIT = H * NC
LV = 7
NO = 6
PAD = TAPS - 1
TW = L + PAD
EPS = 1e-5
NTT = B * L // P
NG = NHH * H + H
DI, DS, DR = 512, 16, 16
DT = DI // P
CTXT = 2
NE, FF = 6, 352
FT = [(0, 128), (128, 128), (256, 96)]


def log1p_coefficients():
    import numpy as np
    deg = 9
    k = np.arange(400)
    e = (1 + np.cos(np.pi * (k + 0.5) / 400)) / 2
    f = np.log1p(e) / e
    c = np.polynomial.chebyshev.Chebyshev.fit(e, f, deg, domain=[0, 1])
    return [float(v) for v in c.convert(kind=np.polynomial.Polynomial).coef]


def log1p_factors():
    import numpy as np
    k = np.arange(400)
    e = (1 + np.cos(np.pi * (k + 0.5) / 400)) / 2
    f = np.log1p(e) / e
    poly = np.polynomial.chebyshev.Chebyshev.fit(e, f, 8, domain=[0, 1], w=1 / f).convert(kind=np.polynomial.Polynomial)
    roots = [z for z in poly.roots() if z.imag > 0]
    scale = float(poly.coef[-1]) ** (0.5 / len(roots))
    return [(scale, -scale * float(z.real), (scale * float(z.imag)) ** 2) for z in roots]


def at(n, off):
    def val(per, c):
        return n * per + (off * per + c)
    return val


def wait(eng, sem, value):
    if not (isinstance(value, int) and value <= 0):
        eng.wait_ge(sem, value)


def wait_apart(eng, passed, sem, value):
    if not (isinstance(value, int) and value <= 0):
        eng.wait_ge(sem, value)
        eng.sem_inc(passed, 1)




class StateWeights:

    def __init__(self, ctx, nc):
        sb = lambda name, shape: ctx.enter_context(nc.sbuf_tensor(name, shape, F32))
        self.ctxT = sb("ctxT", [P, CTXT, B * L])
        self.inw = sb("inw", [P, CTXT, DI])
        self.xw = sb("xw", [P, DT, DR + 2 * DS])
        self.dw = sb("dw", [DR, DI])
        self.cw = sb("scw", [P, DT, TAPS])
        self.cb = sb("scb", [P, DT])
        self.db = sb("sdb", [P, DT])
        self.dd = sb("sdd", [P, DT])

    def pairs(self, inputs):
        return ((self.ctxT, inputs["ctxT"]), (self.inw, inputs["in_w"]), (self.cw, inputs["s_conv"]),
                (self.cb, inputs["s_convb"]), (self.xw, inputs["x_w"]), (self.dw, inputs["dt_w"]),
                (self.db, inputs["dt_b"]), (self.dd, inputs["s_d"]))


def state_inputs(nc, g, sw):
    ctxT, inw, xw, dw, cw, cb, db, dd = sw.ctxT, sw.inw, sw.xw, sw.dw, sw.cw, sw.cb, sw.db, sw.dd
    with ExitStack() as ctx:
        sb = lambda name, shape, dt=F32: ctx.enter_context(nc.sbuf_tensor(name, shape, dt))
        pb = lambda name, shape, dt=F32: ctx.enter_context(nc.psum_tensor(name, shape, dt))
        sem = lambda name: ctx.enter_context(nc.semaphore(name))
        acc = sb("acc", [P, DT, L])
        th = sb("sth", [P, DT, L])
        u2 = sb("u2", [P, DT, L])
        xd = sb("xd", [DR + 2 * DS, L])
        y = sb("sy", [P, DT, L])
        ya = sb("sya", [P, DT, L])
        e = sb("se", [P, DT, L])
        dt = sb("sdt", [P, DT, L])
        dtu = sb("sdtu", [P, DT, L])
        ud = sb("sud", [P, DT, L])
        sq = sb("ssq", [P, 4, DT, L])
        fb = sb("sfb", [P, 4])
        px = pb("px", [P, DT, 512])
        pd = pb("pd", [P, 512])
        pt = pb("pt", [P, 2, 512])
        names = ("in_done", "tap_done", "conv_link", "conv_done", "tanh_done", "u_done", "xd_done",
                 "xd_copied", "dt_done", "abs_done", "e_done", "sq_done", "poly", "fb_done",
                 "ud_done", "out_ready")
        s = {k: sem("si_" + k) for k in names}
        out_dma, bc_out = sem("si_out"), sem("si_bc_out")
        passed = sem("si_passed")
        NP = len(g.log1p_factors)

        with nc.Block() as block:
            @block.sync
            def _(sp):
                load_head(sp, g, 0, lambda sem_, o: None)
                def batch(b):
                    one = slice(b, b + 1) if isinstance(b, int) else ds(b, 1)
                    sp.wait_ge(s["xd_copied"], b + 1)
                    sp.dma_start(g.bc_dram[one].rearrange("b k l -> (b k) l"), xd[DR:, :]).then_inc(bc_out, 16)
                    sp.wait_ge(s["out_ready"], b + 1)
                    sp.wait_ge(s["ud_done"], b + 1)
                    for dst, src in ((g.dts_dram[one, :, 0], dt), (g.dts_dram[one, :, 1], dtu), (g.ud_dram[one], ud)):
                        sp.dma_start(dst.rearrange("b t p l -> p (b t) l"), src[:]).then_inc(out_dma, 16)

                batch(0)
                with sp.Fori(1, B) as b:
                    batch(b)
                sp.wait_ge(out_dma, 16 * 3 * B)
                sp.wait_ge(bc_out, 16 * B)

            def batches(eng, body):
                body(0, True)
                with eng.Fori(1, B - 1) as b:
                    body(b, True)
                body(B - 1, False)

            @block.tensor
            def _(pe):
                def project(b):
                    for t in range(DT):
                        wait(pe, s["conv_done"], b * DT)
                        for k in range(CTXT):
                            src = ctxT[:, k, b * L:(b + 1) * L] if isinstance(b, int) else ctxT[:, k, ds(b * L, L)]
                            i = pe.matmul(px[:, t, :], inw[:, k, t * P:(t + 1) * P], src, start=(k == 0), stop=(k == CTXT - 1))
                        i.then_inc(s["in_done"], 1)

                def batch(b, ahead):
                    if ahead:
                        project(b + 1)
                    pe.wait_ge(s["u_done"], b + 1)
                    for t in range(DT):
                        i = pe.matmul(pd[0:DR + 2 * DS, :], xw[:, t, :], u2[:, t, :], start=(t == 0), stop=(t == DT - 1))
                    i.then_inc(s["xd_done"], 1)
                    pe.wait_ge(s["xd_copied"], b + 1)
                    for t in range(DT):
                        if t > 1:
                            pe.wait_ge(s["abs_done"], b * DT + (t - 1))
                        pe.matmul(pt[:, t % 2, :], dw[:, t * P:(t + 1) * P], xd[0:DR, :], start=True, stop=True)\
                            .then_inc(s["dt_done"], 1)

                project(0)
                batches(pe, batch)

            @block.scalar
            def _(act):
                def tap(b):
                    for t in range(DT):
                        act.wait_ge(s["in_done"], b * DT + (t + 1))
                        wait(act, s["u_done"], b)
                        act.activation(acc[:, t, :], px[:, t, :], ACT.Identity, bias=cb[:, t:t + 1],
                                       scale=cw[:, t, PAD:TAPS]).then_inc(s["tap_done"], 1)

                def batch(b, ahead):
                    act.wait_ge(s["conv_done"], b * DT + DT)
                    act.activation(th[:], acc[:], ACT.Tanh, scale=0.5).then_inc(s["tanh_done"], 1)
                    act.wait_ge(s["xd_done"], b + 1)
                    wait(act, bc_out, b * 16)
                    act.activation(xd[:, :], pd[0:DR + 2 * DS, :], ACT.Copy, scale=0.5).then_inc(s["xd_copied"], 1)
                    if ahead:
                        tap(b + 1)
                    for t in range(DT):
                        act.wait_ge(s["dt_done"], b * DT + (t + 1))
                        wait(act, s["out_ready"], b)
                        act.activation(y[:, t, :], pt[:, t % 2, :], ACT.Identity, bias=db[:, t:t + 1])
                        act.activation(ya[:, t, :], pt[:, t % 2, :], ACT.Abs, bias=db[:, t:t + 1]).then_inc(s["abs_done"], 1)
                    act.wait_ge(s["abs_done"], b * DT + DT)
                    act.activation(e[:], ya[:], ACT.Exp, scale=-1.0).then_inc(s["e_done"], 1)
                    act.wait_ge(s["e_done"], b + 1)
                    for k, (scale, _, _) in enumerate(g.log1p_factors):
                        act.activation(sq[:, k], e[:], ACT.Square, bias=fb[:, k:k + 1], scale=scale).then_inc(s["sq_done"], 1)

                act.wait_ge(s["fb_done"], 1)
                tap(0)
                batches(act, batch)

            @block.gpsimd
            def _(pool):
                def batch(b, ahead):
                    pool.wait_ge(s["u_done"], b + 1)
                    wait_apart(pool, passed, out_dma, b * 48)
                    for t in range(DT):
                        i = pool.tensor_scalar(ud[:, t, :], u2[:, t, :], dd[:, t:t + 1], 0.5, ALU.mult, ALU.mult)
                    i.then_inc(s["ud_done"], 1)

                batches(pool, batch)

            @block.vector
            def _(dve):
                def conv(b):
                    for t in range(DT):
                        dve.wait_ge(s["tap_done"], b * DT + (t + 1))
                        for k in range(1, TAPS):
                            i = dve.scalar_tensor_tensor(acc[:, t, k:], px[:, t, 0:L - k], cw[:, t, PAD - k:TAPS - k],
                                                         acc[:, t, k:], ALU.mult, ALU.add)
                            if k < PAD:
                                i.then_inc(s["conv_link"], 1)
                                dve.wait_ge(s["conv_link"], b * (2 * DT) + (2 * t + k))
                        i.then_inc(s["conv_done"], 1)

                def batch(b, ahead):
                    dve.wait_ge(s["tanh_done"], b + 1)
                    wait(dve, s["ud_done"], b)
                    wait(dve, s["out_ready"], b)
                    dve.scalar_tensor_tensor(u2[:], th[:], 1.0, acc[:], ALU.add, ALU.mult).then_inc(s["u_done"], 1)
                    if ahead:
                        conv(b + 1)
                    for k, (_, _, rest) in enumerate(g.log1p_factors):
                        dve.wait_ge(s["sq_done"], b * NP + (k + 1))
                        if k > 0:
                            dve.wait_ge(s["poly"], b * (NP + 1) + k)
                        dve.scalar_tensor_tensor(sq[:, 0], sq[:, k], rest, e[:] if k == 0 else sq[:, 0], ALU.add, ALU.mult)\
                            .then_inc(s["poly"], 1)
                    dve.wait_ge(s["poly"], b * (NP + 1) + NP)
                    wait(dve, out_dma, b * 48)
                    dve.scalar_tensor_tensor(dt[:], y[:], 0.0, sq[:, 0], ALU.max, ALU.add).then_inc(s["poly"], 1)
                    dve.wait_ge(s["poly"], b * (NP + 1) + (NP + 1))
                    dve.scalar_tensor_tensor(dtu[:], u2[:], 0.5, dt[:], ALU.mult, ALU.mult).then_inc(s["out_ready"], 1)

                for k, (_, bias, _) in enumerate(g.log1p_factors):
                    i = dve.memset(fb[:, k:k + 1], bias)
                i.then_inc(s["fb_done"], 1)
                conv(0)
                batches(dve, batch)




def prepare(nc, g, sw):
    with ExitStack() as ctx:
        sb = lambda name, shape, dt=F32: ctx.enter_context(nc.sbuf_tensor(name, shape, dt))
        pb = lambda name, shape, dt=F32: ctx.enter_context(nc.psum_tensor(name, shape, dt))
        sem = lambda name: ctx.enter_context(nc.semaphore(name))
        xin = sb("xin", [P, NTT, HID])
        xhat = sb("xhat", [P, 2, HID])
        stats = sb("stats", [P, 2, 6])
        mv = sb("mv", [P, NTT, 2])
        rstd = sb("rstd", [P, NTT])
        wg = sb("wg", [P, KT, NG])
        logitT = sb("logitT", [NG, B * L, NHH])
        bias_bc = sb("bias_bc", [P, H])
        alog_bc = sb("alog_bc", [P, H])
        expa = sb("expa", [P, H])
        parity = sb("parity", [P, 2])
        first = sb("first", [P, NIT])
        flag = sb("flag", [P, NIT])
        neg = sb("neg32", [P, CM])
        negq = sb("negq32", [P, CT])
        ssa = sb("ssa", [P, DT * DS])
        raw = sb("raw", [P, B * NC, NG])
        y = sb("y", [P, 2, B * NC, H])
        ya = sb("ya", [P, 2, B * NC, H])
        e = sb("e", [P, 2, B * NC, H])
        sp = sb("sp", [P, 2, B * NC, H])
        decay = sb("decay", [P, H, NC, B])
        eG = sb("eG", [P, NIT, B])
        psT = pb("psT", [P, 2, 512])
        psL = pb("psL", [P, 512])
        psR = pb("psR", [P, 2, 512])
        psG = pb("psG", [P, 3, 512])
        x_in = [sem(f"x_in{k}") for k in range(4)]
        s_in = sem("s_in")
        c_in, var_ready, rstd_ready, xhat_ready, t_ready, xT_ready = map(
            sem, ("c_in", "var_ready", "rstd_ready", "xhat_ready", "t_ready", "xT_ready"))
        lg_ready, lg_copied, raw_ready, raw_copied, act1, dve1, cum_ready, done_a = map(
            sem, ("lg_ready", "lg_copied", "raw_ready", "raw_copied", "act1", "dve1", "cum_ready", "done_a"))
        chain = sem("prep_chain")
        act_chain = sem("act_chain")
        st_link = sem("st_link")

        with nc.Block() as block:
            @block.sync
            def _(sp_):
                src = g.inputs["x"].rearrange("(n p) d -> p n d", p=P)
                for k in range(4):
                    quarter = slice(k * NTT // 4, (k + 1) * NTT // 4)
                    sp_.dma_start(xin[:, quarter, :], src[:, quarter]).then_inc(x_in[k], 16)
                for dst, src in ((g.ident, g.inputs["c_ident"]), (g.upto, g.inputs["c_upto"]), (g.after, g.inputs["c_after"]),
                                 (g.ones, g.inputs["c_ones"]), (neg, g.inputs["c_neg"]), (negq, g.inputs["c_negq"]),
                                 (g.levels, g.inputs["c_levels"]), (wg, g.inputs["w_gates"]),
                                 (parity, g.inputs["c_parity"]), (first, g.inputs["c_first"]), (flag, g.inputs["c_flag"]), (ssa, g.inputs["s_alog"]), (g.normw, g.inputs["norm_w"])):
                    sp_.dma_start(dst[:], src).then_inc(c_in, 16)
                sp_.dma_start(bias_bc[:, :], g.inputs["dt_bias"].partition_broadcast(P)).then_inc(c_in, 16)
                sp_.dma_start(alog_bc[:, :], g.inputs["a_log"].partition_broadcast(P)).then_inc(c_in, 16)
                for dst, src in sw.pairs(g.inputs):
                    sp_.dma_start(dst[:], src).then_inc(s_in, 16)
                sp_.wait_ge(s_in, 16 * len(sw.pairs(g.inputs)))
            CONSTS = 16 * 15

            @block.vector
            def _(dve):
                for t in range(NTT):
                    if t % (NTT // 4) == 0:
                        dve.wait_ge(x_in[t // (NTT // 4)], 16)
                    dve.bn_stats(stats[:, t % 2, :], xin[:, t, :]).then_inc(st_link, 1)
                    dve.wait_ge(st_link, t + 1)
                    i = dve.bn_aggr(mv[:, t, :], stats[:, t % 2, :])
                i.then_inc(var_ready, 1)
                dve.wait_ge(var_ready, 1)
                dve.tensor_scalar(rstd[:, :], mv[:, :, 1], EPS, None, ALU.add).then_inc(var_ready, 1)
                dve.memset(g.xT[:, :, :, 0:PAD], 0.0)
                dve.wait_ge(rstd_ready, 1)
                for t in range(NTT):
                    wait(dve, t_ready, t - 1)
                    dve.tensor_scalar(xhat[:, t % 2, :], xin[:, t, :], mv[:, t, 0:1], rstd[:, t:t + 1],
                                      ALU.subtract, ALU.mult).then_inc(xhat_ready, 1)
                for k in range(2):
                    dve.wait_ge(raw_ready, k + 1)
                    i = dve.tensor_copy(raw[:, 16 * k:16 * k + 16, :],
                                        psR[:, k, 0:16 * NG].rearrange("p (n c) -> p n c", c=NG))
                i.then_inc(chain, 1)
                dve.wait_ge(chain, 1)
                dve.wait_ge(c_in, CONSTS)
                k = [1]

                def link(ins):
                    k[0] += 1
                    ins.then_inc(chain, 1)
                    dve.wait_ge(chain, k[0])

                bc = lambda a: a.unsqueeze(1).to_broadcast([P, B * NC, H])
                link(dve.tensor_tensor(y[:, 0], raw[:, :, 2 * H:3 * H], bc(bias_bc[:, :]), ALU.add))
                link(dve.tensor_scalar(y[:, 1], raw[:, :, 0:H], parity[:, 0:1], -1.0, ALU.mult, ALU.mult))
                link(dve.tensor_scalar(ya[:, 1], raw[:, :, H:2 * H], parity[:, 1:2], -1.0, ALU.mult, ALU.mult))
                link(dve.tensor_tensor(y[:, 1], y[:, 1], ya[:, 1], ALU.add))
                i = dve.tensor_scalar(ya[:], y[:], -1.0, None, ALU.mult)
                link(i)
                link(dve.tensor_tensor(ya[:], ya[:], y[:], ALU.min))
                dve.nop().then_inc(dve1, 1)
                dve.wait_ge(act1, 2)
                link(dve.tensor_scalar(sp[:], e[:], g.log1p[-1], None, ALU.mult))
                for c in g.log1p[-2::-1]:
                    link(dve.scalar_tensor_tensor(sp[:], sp[:], c, e[:], ALU.add, ALU.mult))
                link(dve.scalar_tensor_tensor(sp[:], y[:], 0.0, sp[:], ALU.max, ALU.add))
                link(dve.tensor_tensor(sp[:, 0], sp[:, 0], bc(expa[:, :]), ALU.mult))
                dv = decay[:, :, :, :].rearrange("p h c b -> p b c h")
                link(dve.tensor_scalar(dv, sp[:, 0].rearrange("p (b c) h -> p b c h", b=B),
                                       parity[:, 0:1], -1.0, ALU.mult, ALU.mult))
                tb = g.tab[:, :, :].rearrange("p (h c) k -> p h c k", h=H)
                for b in range(B):
                    sv = sp[:, 1].rearrange("p (b c) h -> p b h c", b=B)[:, b]
                    dve.tensor_scalar(tb[:, :, :, 4 + b], sv, -1.0, g.ln2, ALU.mult, ALU.add)
                    dve.tensor_scalar(tb[:, :, :, 8 + b], sv, -1.0, None, ALU.mult)
                    i = dve.tensor_copy(tb[:, :, :, b], decay[:, :, :, b])
                link(i)
                dve.nop().then_inc(dve1, 1)
                dve.wait_ge(act1, 3)
                f4 = first[:, :].unsqueeze(2).to_broadcast([P, NIT, B])
                link(dve.scalar_tensor_tensor(eG[:], eG[:], -2.0, f4, ALU.mult, ALU.mult))
                dve.tensor_tensor(g.tab[:, :, 12:16], eG[:], g.tab[:, :, 8:12], ALU.mult)
                dve.tensor_tensor(g.tab[:, :, 20:24], g.tab[:, :, 20:24], f4, ALU.mult)
                dve.tensor_tensor(g.tab[:, :, 24:26], g.tab[:, :, 24:26], f4[:, :, 0:2], ALU.mult)
                dve.tensor_scalar(g.normw[:, :], g.normw[:, :], 0.5, None, ALU.mult)
                dve.tensor_copy(g.tab[:, :, 26:27], flag[:, :].unsqueeze(2))
                dve.tensor_scalar(g.a_neg[:, :], ssa[:, :], -1.0, None, ALU.mult)
                dve.tensor_copy(g.identb[:, :], g.ident[:, :])
                dve.tensor_copy(g.neg[:].rearrange("p (b n) -> p b n", b=B), neg[:, :].unsqueeze(1).to_broadcast([P, B, CM]))
                dve.tensor_copy(g.negq[:].rearrange("p (b n) -> p b n", b=B), negq[:, :].unsqueeze(1).to_broadcast([P, B, CT]))
                for l in range(LV):
                    dve.tensor_copy(g.Xm[:, l], g.ident[:, :].unsqueeze(1).to_broadcast([P, B, P]))
                dve.memset(g.S[:, :, :], 0.0)

            @block.gpsimd
            def _(pool):
                pool.memset(g.mhalf[:, :], -0.5).then_inc(done_a, 1)
                pool.wait_ge(done_a, 1)
                pool.wait_ge(var_ready, 2)
                pool.tensor_tensor(rstd[:, :], rstd[:, :], g.mhalf[:, 0:NTT], ALU.pow).then_inc(rstd_ready, 1)

            @block.tensor
            def _(pe):
                pe.wait_ge(c_in, CONSTS)
                for t in range(NTT):
                    pe.wait_ge(xhat_ready, t + 1)
                    wait(pe, xT_ready, t - 1)
                    for k in range(KT):
                        i = pe.transpose(psT[:, t % 2, k * P:(k + 1) * P], xhat[:, t % 2, k * P:(k + 1) * P],
                                         g.ident[:, :])
                    i.then_inc(t_ready, 1)
                for b in range(B):
                    pe.wait_ge(xT_ready, NTT)
                    wait(pe, lg_copied, b)
                    for k in range(KT):
                        i = pe.matmul(psL[0:NG, :], wg[:, k, :], g.xT[:, k, b, PAD:], start=(k == 0), stop=(k == KT - 1))
                    i.then_inc(lg_ready, 1)
                pe.wait_ge(lg_copied, B)
                for n in range(B * NC):
                    src = logitT[:, n * CT:(n + 1) * CT, :].rearrange("p t j -> p (t j)")
                    i = pe.transpose(psR[:, n // 16, (n % 16) * NG:(n % 16 + 1) * NG], src, g.ident[0:NG, 0:NG])
                    if n % 16 == 15:
                        i.then_inc(raw_ready, 1)
                pe.wait_ge(dve1, 2)
                rhs = decay[:, :, :, :].rearrange("p h c b -> p (h c b)")
                pe.matmul(psG[:, 0, 0:256], g.upto[:, :], rhs, start=True, stop=True)
                pe.matmul(psG[:, 1, 0:256], g.after[:, :], rhs, start=True, stop=True)
                pe.matmul(psG[:, 2, 0:256], g.ones[:, :], rhs, start=True, stop=True)
                uq = g.upto[:, :].rearrange("p (t j) -> p t j", j=2)[:, :, 1]
                for h2 in range(2):
                    i = pe.matmul(psG[h2 * CT:(h2 + 1) * CT, 0, 256:384], uq,
                                  decay[:, :, :, h2::2].rearrange("p h c b -> p (h c) b"),
                                  start=True, stop=True, skip_group_check=True)
                i.then_inc(cum_ready, 1)

            @block.scalar
            def _(act):
                for t in range(NTT):
                    act.wait_ge(t_ready, t + 1)
                    tok = (t % (L // P)) * P
                    act.activation(g.xT[:, :, t // (L // P), PAD + tok:PAD + tok + P],
                                   psT[:, t % 2, :].rearrange("p (k n) -> p k n", k=KT),
                                   ACT.Copy).then_inc(xT_ready, 1)
                for b in range(B):
                    act.wait_ge(lg_ready, b + 1)
                    act.activation(logitT[:, b * L:(b + 1) * L, :],
                                   psL[0:NG, :].unsqueeze(2).to_broadcast([NG, L, NHH]), ACT.Copy).then_inc(lg_copied, 1)
                act.wait_ge(c_in, CONSTS)
                act.activation(ssa[:, :], ssa[:, :], ACT.Exp)
                act.activation(expa[:, :], alog_bc[:, :], ACT.Exp).then_inc(act1, 1)
                act.wait_ge(dve1, 1)
                act.activation(e[:], ya[:], ACT.Exp).then_inc(act1, 1)
                act.wait_ge(cum_ready, 1)
                v = lambda k: psG[:, k, 0:256].rearrange("p (n b) -> p n b", b=B)
                act.activation(eG[:], v(0), ACT.Exp)
                act.activation(g.tab[:, :, 16:20], v(1), ACT.Exp)
                act.activation(g.tab[:, :, 20:24], v(2), ACT.Exp)
                act.activation(g.tab[:, :, 8:12], g.tab[:, :, 8:12], ACT.Exp)
                act.activation(g.tab[:, :, 24:26], psG[:, 0, 256:384].rearrange("p (n b) -> p n b", b=2),
                               ACT.Exp).then_inc(act1, 1)


def load_head(sp, g, w, ready):
    one = slice(w, w + 1) if isinstance(w, int) else ds(w, 1)
    for o in range(NO):
        if o == NO - 1:
            ready(g.conv_done, NO - 2)
            sp.dma_start(g.cw[:, :, :], g.inputs["conv_heads"][one].rearrange("h p (o k) -> p (h o) k", k=TAPS))\
                .then_inc(g.cw_in, 16)
        ready(g.proj_done, o)
        src = g.inputs["w_heads"][one].rearrange("h p (o k n) -> p (h o) k n", o=NO, k=KT)
        sp.dma_start(g.W[:, o], src[:, o]).then_inc(g.w_in[o], 16)


def delta(nc, g):
    with ExitStack() as ctx:
        sb = lambda name, shape, dt=F32: ctx.enter_context(nc.sbuf_tensor(name, shape, dt))
        pb = lambda name, shape, dt=F32: ctx.enter_context(nc.psum_tensor(name, shape, dt))
        sem = lambda name: ctx.enter_context(nc.semaphore(name))
        K0, V0, Q0, END = 0, B * CM, 2 * B * CM, 2 * B * CM + B * CT
        cw = g.cw
        cv = sb("cv", [P, END])
        th = sb("th", [P, END])
        kvq = sb("kvq", [P, 2, END])
        gt = sb("gt", [P, B, CT])
        gs = sb("gs", [P, 2, B, CT])
        junk = sb("junk", [P, 8, P])
        sc = sb("sc", [P, 2, 27])
        ss = sb("ss", [P, 6])
        rr = sb("rr", [P, 6])
        sd = sb("sd", [P, 8])
        rq = sb("rq", [P, 2, 2])
        Kn = sb("Kn", [P, B, DH])
        Kw = sb("Kw", [P, 2, B, DH])
        Vb = sb("Vb", [P, 2, B, DH])
        Qn = sb("Qn", [P, 2, 2, DH])
        KTr = sb("KTr", [P, 2, B, CM])
        QTr = sb("QTr", [P, 2, 2, 2, P])
        Dr = sb("Dr", [P, B, CM])
        Dt = sb("Dt", [P, B, CM])
        Dq = sb("Dq", [P, B, CT])
        E_ = sb("E_", [P, B, CM])
        Eq = sb("Eq", [P, B, CT])
        At = sb("At", [P, B, CM])
        PT = sb("PT", [P, 2, B, CT])
        Wl = sb("Wl", [P, B, CM])
        MT = sb("MT", [P, B, CM])
        Rf = sb("Rf", [P, 2, B, CM])
        F = sb("F", [P, B, DH])
        U = sb("U", [P, B, DH])
        oss = sb("oss", [P, 2])
        orr = sb("orr", [P, 2])
        On = sb("On", [P, 2, DH])
        OT = sb("OT", [P, 2, B, CT])
        dts = sb("dts", [P, 2, 2, L])
        bcq = sb("bcq", [P, 2, 4, L])
        da = sb("da", [P, 4, L])
        hs = sb("hs", [P, 4, L])
        ys = sb("ys", [P, DT, L])
        bank = [pb(f"bank{i}", [P, 512]) for i in range(8)]
        by_batch = lambda a: a[:, 0:512].rearrange("p (b n) -> p b n", b=B)
        blocks = lambda a, half, s_: a.rearrange("p b (j h s) -> p b h j s", h=2, s=s_)[:, :, half]
        pairs = lambda a: a.rearrange("p (b n) -> p b n", b=2)

        names = ("tap_done", "gtanh_done", "tanh_done", "act_done", "natural_done", "rk_done", "kw_done",
                 "sd_done", "ss_done", "sc_done", "r_done", "dr_done", "kn_done", "qn_done", "turned",
                 "kt_done", "qt_done", "decay_done", "e_done", "gram_done", "at_done", "pt_done", "x_done",
                 "xm_done", "mt_done", "mtcopy_done", "wcopy_done", "rt_done", "rcopy_done", "ks_done",
                 "f_done", "u_done", "ucopy_done", "so_done", "s_done", "oss_done", "orr_done", "on_done",
                 "ot_turned", "ot_done", "conv_link", "pool_link_b", "pool_link_d", "pool_link_c", "bc_in",
                 "ya_cleared", "da_done", "bx_done", "scan_done", "hc_done", "hcp_done", "ys_link", "ys_done")
        passed = {k: sem(f"passed_{k}") for k in ("sp", "pool", "dve")}
        s = {k: sem(k) for k in names}
        s["conv_done"], s["proj_done"] = g.conv_done, g.proj_done
        out_dma = [sem("out_dma0"), sem("out_dma1")]
        dt_in = [sem("dt_in0"), sem("dt_in1")]
        y_dma = sem("y_dma")
        PARTS = ((K0, V0), (V0, Q0), (Q0, END))
        seq = {0: K0, 1: K0, 2: V0, 3: V0}

        def loops(eng, body):
            body(eng, -2, 0, C=False, B_=False)
            body(eng, -1, 1, C=False)
            body(eng, 0, 0)
            body(eng, 1, 1)
            with eng.Fori(2, NIT - 3, 2) as i:
                for u in range(2):
                    body(eng, i + u, u)
            body(eng, NIT - 2, 0, A=False)
            body(eng, NIT - 1, 1, A=False, B_=False)

        def conv_out(o):
            if o == 4:
                return cv[:, Q0:END].rearrange("p (b t) -> p b t", b=B)
            return cv[:, seq[o]:seq[o] + B * CM].rearrange("p (b t j) -> p j b t", b=B, j=NHH)[:, o % 2]

        def proj_bank(o):
            return bank[o % 2][:, 0:B * (CT + PAD)].rearrange("p (b t) -> p b t", b=B)

        with nc.Block() as block:
            @block.sync
            def _(sp):
                def store(h, c, u):
                    sp.wait_ge(s["ot_done"], h * NC + (c + 1))
                    one = slice(h, h + 1) if isinstance(h, int) else ds(h, 1)
                    sp.dma_start(g.o_dram[one, :, :, c * CT:(c + 1) * CT].rearrange("o v b t -> v (o b) t"),
                                 OT[:, u]).then_inc(out_dma[u], 16)

                def scan_inputs(b, k):
                    n = b * 16 + k
                    wait(sp, s["da_done"], 2 * (n - 1))
                    wait_apart(sp, passed["sp"], s["bx_done"], n - 1)
                    one = slice(b, b + 1) if isinstance(b, int) else ds(b, 1)
                    if k % 4 == 0:
                        wait(sp, s["hc_done"], n)
                        wait(sp, s["hcp_done"], n)
                        src = g.bc_dram[one].rearrange("b (i n) l -> (b i) n l", i=2)[:, k // 4 * 4:k // 4 * 4 + 4, :]
                        sp.dma_start(bcq[:], src.partition_broadcast(P)).then_inc(s["bc_in"], 16)
                    sp.dma_start(dts[:, k % 2], g.dts_dram[one, k % 4].rearrange("b i p l -> p (b i) l"))\
                        .then_inc(dt_in[k % 2], 16)

                def flush(b, t):
                    sp.wait_ge(s["ys_done"], b * 16 + (13 + t))
                    one = slice(b, b + 1) if isinstance(b, int) else ds(b, 1)
                    sp.dma_start(g.y_dram[one, t].rearrange("b p l -> p (b l)"), ys[:, t]).then_inc(y_dma, 16)

                def span(b, first):
                    for k in range(16):
                        if not (first and k < 2):
                            scan_inputs(b, k)
                        h, c = b * 2 + k // NC, k % NC
                        if c == NC - 3 and not (isinstance(b, int) and b == B - 1 and k >= NC):
                            load_head(sp, g, h + 1, lambda sem_, o: sp.wait_ge(sem_, h * (NC * NO) + ((NC - 1) * NO + o + 1)))
                        store(h, c, c % 2)
                        if k > 12:
                            flush(b, k - 13)
                    flush(b, 3)

                sp.sem_inc(y_dma, 16 * DT)
                scan_inputs(0, 0)
                scan_inputs(0, 1)
                span(0, True)
                with sp.Fori(1, B - 1) as b:
                    span(b, False)
                span(B - 1, False)
                sp.wait_ge(y_dma, 16 * DT * (B + 1))
                for u in range(2):
                    sp.wait_ge(out_dma[u], 16 * NIT // 2)

            @block.gpsimd
            def _(pool):
                def link(sname, per, val, k, ins):
                    ins.then_inc(s[sname], 1)
                    wait_apart(pool, passed["pool"], s[sname], val(per, k))

                def body(pool, n, u, A=True, B_=True, C=True):
                    a, b, c = at(n, 2), at(n, 1), at(n, 0)
                    v = (u + 1) % 2
                    row = lambda m: g.tab[:, m:m + 1, :] if isinstance(m, int) else g.tab[:, ds(m, 1), :]
                    if B_:
                        wait(pool, s["s_done"], c(1, 0))
                        wait(pool, s["ys_done"], c(1, 0))
                        wait(pool, s["kn_done"], b(2, 0))
                        wait_apart(pool, passed["pool"], s["qn_done"], b(1, 0))
                        pool.tensor_copy(sc[:, v:v + 1, :], row(n + 1)).then_inc(s["sc_done"], 1)
                        pool.wait_ge(s["sc_done"], b(1, 1))
                        wait_apart(pool, passed["pool"], s["ss_done"], b(2, 1))
                        link("pool_link_b", 3, b, 1, pool.tensor_scalar(rr[:, 0:B], ss[:, 0:B], 4e-24, None, ALU.max))
                        pool.tensor_tensor(rr[:, 0:B], rr[:, 0:B], g.mhalf[:, 0:B], ALU.pow).then_inc(s["rk_done"], 1)
                        wait_apart(pool, passed["pool"], s["ss_done"], b(2, 2))
                        link("pool_link_b", 3, b, 2, pool.tensor_scalar(rr[:, B:6], ss[:, B:6], 4e-24, None, ALU.max))
                        link("pool_link_b", 3, b, 3, pool.tensor_tensor(rr[:, B:6], rr[:, B:6], g.mhalf[:, 0:2], ALU.pow))
                        pool.tensor_scalar(rq[:, 0, :], rr[:, B:6], DH ** -0.5, None, ALU.mult).then_inc(s["r_done"], 1)
                        pool.wait_ge(s["r_done"], b(2, 1))
                        pool.tensor_tensor(rq[:, 1, :], rq[:, 0, :], sc[:, v, 24:26], ALU.mult).then_inc(s["r_done"], 1)
                    if C:
                        pool.wait_ge(dt_in[u], ((n >> 1) + 1) * 16)
                        pool.wait_ge(s["bc_in"], ((n >> 2) + 1) * 16)
                        wait(pool, s["ys_done"], c(1, 0))
                        pool.tensor_tensor(hs[:], dts[:, u, 1, :].unsqueeze(1).to_broadcast([P, 4, L]), bcq[:, 0],
                                           ALU.mult).then_inc(s["bx_done"], 1)
                    if B_:
                        wait(pool, s["so_done"], c(2, 0))
                        pool.wait_ge(s["kn_done"], b(2, 1))
                        pool.tensor_tensor(Kw[:, v], Kn[:], sc[:, v, 16:20].unsqueeze(2).to_broadcast([P, B, DH]),
                                           ALU.mult).then_inc(s["kw_done"], 1)
                    if C:
                        wait(pool, s["on_done"], c(1, 0))
                        wait_apart(pool, passed["pool"], s["oss_done"], c(1, 1))
                        link("pool_link_c", 1, c, 1,
                             pool.tensor_scalar(orr[:, :], oss[:, :], 1.0 / DH, EPS, ALU.mult, ALU.add))
                        pool.tensor_tensor(orr[:, :], orr[:, :], g.mhalf[:, 0:2], ALU.pow).then_inc(s["orr_done"], 1)
                    if A:
                        pool.tensor_copy(sd[:].unsqueeze(1), row(n + 2)[:, :, 0:8]).then_inc(s["sd_done"], 1)
                        pool.wait_ge(s["sd_done"], a(1, 1))
                        wait(pool, s["decay_done"], a(2, 0))
                        gb = lambda w: sd[:, 0:B].unsqueeze(2).to_broadcast([P, B, w])
                        up = g.upto[:, :].unsqueeze(1).to_broadcast([P, B, CM])
                        upq = g.upto[:, :].rearrange("p (t j) -> p t j", j=2)[:, :, 1].unsqueeze(1).to_broadcast([P, B, CT])
                        pool.tensor_tensor(Dr[:], up, gb(CM), ALU.mult)
                        link("pool_link_d", 2, a, 1,
                             pool.tensor_tensor(Dt[:], g.ident[:, :].unsqueeze(1).to_broadcast([P, B, CM]),
                                                sd[:, 4:8].unsqueeze(2).to_broadcast([P, B, CM]), ALU.mult))
                        link("pool_link_d", 2, a, 2, pool.tensor_tensor(Dr[:], Dr[:], Dt[:], ALU.add))
                        pool.tensor_tensor(Dq[:], upq, gb(CT), ALU.mult).then_inc(s["dr_done"], 1)
                    if C:
                        pool.wait_ge(s["scan_done"], c(2, 1))
                        pool.tensor_tensor(hs[:, 0:2], hs[:, 0:2], bcq[:, 1, 0:2], ALU.mult).then_inc(s["hcp_done"], 1)
                        pool.wait_ge(s["hcp_done"], c(1, 1))
                        pool.wait_ge(s["hc_done"], c(1, 1))
                        t = ds((n & 3) * L, L) if not isinstance(n, int) else slice((n & 3) * L, (n & 3) * L + L)
                        yt = ys[:].rearrange("p t l -> p (t l)")[:, t]
                        pool.wait_ge(y_dma, (n >> 4) * (16 * DT) + 16 * DT)
                        link("ys_link", 3, c, 1, pool.tensor_tensor(hs[:, 0:2], hs[:, 0:2], hs[:, 2:4], ALU.add))
                        link("ys_link", 3, c, 2, pool.tensor_tensor(hs[:, 0], hs[:, 0], hs[:, 1], ALU.add))
                        link("ys_link", 3, c, 3, pool.tensor_tensor(yt, yt, sc[:, u, 26:27].to_broadcast([P, L]), ALU.mult))
                        pool.tensor_tensor(yt, yt, hs[:, 0], ALU.add).then_inc(s["ys_done"], 1)

                pool.wait_ge(s["ya_cleared"], 1)
                loops(pool, body)

            @block.tensor
            def _(pe):
                def body(pe, n, u, A=True, B_=True, C=True):
                    a, b, c = at(n, 2), at(n, 1), at(n, 0)
                    v = (u + 1) % 2

                    def proj(o, *parts):
                        if not A:
                            return
                        m = n + 2
                        off = (m & 7) * CT
                        for k in parts:
                            if k == 0:
                                pe.wait_ge(g.w_in[o], ((m >> 3) + 1) * 16)
                                wait(pe, s["conv_done"], a(NO, o - 1))
                            src = g.xT[:, k, :, off:off + CT + PAD] if isinstance(m, int) else g.xT[:, k, :, ds(off, CT + PAD)]
                            i = pe.matmul(proj_bank(o), g.W[:, o, k, :], src, start=(k == 0), stop=(k == KT - 1))
                            if k == KT - 1:
                                i.then_inc(s["proj_done"], 1)

                    def level_start():
                        if not B_:
                            return
                        pe.wait_ge(s["at_done"], b(1, 1))
                        for q in range(B):
                            i = pe.transpose(by_batch(bank[2])[:, q], At[:, q], g.ident[:, :])
                        i.then_inc(s["x_done"], 1)

                    def level_turn(l):
                        if not B_:
                            return
                        pe.wait_ge(s["xm_done"], b(LV, l + 1))
                        for q in range(B):
                            i = pe.transpose(by_batch(bank[3])[:, q], g.Xm[:, l, q], g.ident[:, :])
                        i.then_inc(s["mt_done"], 1)

                    def level_product(l):
                        if not B_:
                            return
                        pe.wait_ge(s["wcopy_done"], b(LV, l + 1))
                        pe.wait_ge(s["mtcopy_done"], b(LV, l + 1))
                        for q in range(B):
                            if l < LV - 1:
                                i = pe.matmul(by_batch(bank[2])[:, q], MT[:, q], Wl[:, q], start=True, stop=True)
                            else:
                                i = pe.matmul(by_batch(bank[4])[:, q], Wl[:, q], MT[:, q], start=True, stop=True)
                        i.then_inc(s["x_done" if l < LV - 1 else "rt_done"], 1)

                    def natural(bank_out, start, tiles, part, free, w, val):
                        pe.wait_ge(s["act_done"], val(3, part))
                        wait(pe, s[free[0]], free[1])
                        for q in range(tiles):
                            i = pe.transpose(bank_out[:, q * P:(q + 1) * P], kvq[:, w, start + q * P:start + (q + 1) * P],
                                             g.ident[:, :])
                        i.then_inc(s["natural_done"], 1)

                    if C:
                        pe.wait_ge(s["kt_done"], c(1, 1))
                        wait(pe, s["s_done"], c(1, 0))
                        if B_:
                            pe.wait_ge(s["e_done"], b(2, 1))
                        for q in range(B):
                            i = pe.matmul(by_batch(bank[5])[:, q], KTr[:, u, q], g.S[:, q], start=True, stop=True)
                        i.then_inc(s["ks_done"], 1)
                    if B_:
                        natural(bank[3], V0, B, 2, ("mtcopy_done", b(LV, 0)), v, b)
                    proj(0, 0, 1, 2, 3)
                    if C:
                        pe.wait_ge(s["f_done"], c(1, 1))
                        pe.wait_ge(s["rcopy_done"], c(1, 1))
                        pe.wait_ge(s["pt_done"], c(1, 1))
                        if B_:
                            pe.wait_ge(s["e_done"], b(2, 2))
                        for q in range(B):
                            i = pe.matmul(by_batch(bank[6])[:, q], Rf[:, u, q], F[:, q], start=True, stop=True)
                        i.then_inc(s["u_done"], 1)
                    if B_:
                        pe.wait_ge(s["kn_done"], b(2, 1))
                        for q in range(B):
                            i = pe.transpose(by_batch(bank[2])[:, q], Kn[:, q], g.ident[:, :])
                        i.then_inc(s["turned"], 1)
                    if B_:
                        natural(bank[4], Q0, 2, 3, ("rcopy_done", b(1, 0)), v, b)
                    if C:
                        pe.wait_ge(s["ucopy_done"], c(1, 1))
                        pe.wait_ge(s["kw_done"], c(1, 1))
                        for q in range(B):
                            i = pe.matmul(by_batch(bank[5])[:, q], Kw[:, u, q], U[:, q], start=True, stop=True)
                        i.then_inc(s["so_done"], 1)
                    if B_:
                        pe.wait_ge(s["kt_done"], b(1, 1))
                        pe.wait_ge(s["kn_done"], b(2, 2))
                        for q in range(B):
                            i = pe.matmul(by_batch(bank[3])[:, q], KTr[:, v, q], KTr[:, v, q], start=True, stop=True)
                        i.then_inc(s["gram_done"], 1)
                    if C:
                        wait(pe, s["ot_done"], c(1, 0))
                        O = pairs(bank[7][:, 0:256])
                        for q in range(B):
                            rows = slice((q % 2) * CT, (q % 2 + 1) * CT)
                            pe.matmul(O[rows, q // 2], QTr[:, u, 1, q // 2, rows], g.S[:, q], start=True, stop=False)
                            i = pe.matmul(O[rows, q // 2], PT[:, u, q], U[:, q], start=False, stop=True)
                        i.then_inc(s["so_done"], 1)
                    level_start()
                    if B_:
                        pe.wait_ge(s["qn_done"], b(1, 1))
                        for q in range(4):
                            i = pe.transpose(by_batch(bank[4])[:, q], Qn[:, q // 2, q % 2], g.ident[:, :])
                        i.then_inc(s["turned"], 1)
                    proj(1, 0, 1)
                    level_turn(0)
                    proj(1, 2, 3)
                    if B_:
                        pe.wait_ge(s["qt_done"], b(1, 1))
                        pe.wait_ge(s["e_done"], b(2, 2))
                        for q in range(B):
                            i = pe.matmul(bank[6][:, q * CT:(q + 1) * CT], KTr[:, v, q],
                                          QTr[:, v, 0, q // 2, (q % 2) * CT:(q % 2 + 1) * CT], start=True, stop=True)
                        i.then_inc(s["gram_done"], 1)
                    level_product(0)
                    proj(2, 0, 1)
                    level_turn(1)
                    proj(2, 2, 3)
                    level_product(1)
                    proj(3, 0)
                    level_turn(2)
                    proj(3, 1, 2)
                    level_product(2)
                    proj(3, 3)
                    level_turn(3)
                    proj(4, 0, 1)
                    level_product(3)
                    proj(4, 2)
                    level_turn(4)
                    proj(4, 3)
                    if C:
                        pe.wait_ge(s["on_done"], c(1, 1))
                        for q in range(2):
                            i = pe.transpose(bank[7][:, 256 + q * P:256 + (q + 1) * P], On[:, q], g.ident[:, :])
                        i.then_inc(s["ot_turned"], 1)
                    level_product(4)
                    if A:
                        pe.wait_ge(s["dr_done"], a(1, 1))
                        if C:
                            pe.wait_ge(s["s_done"], c(1, 1))
                        pe.matmul(bank[5][:, :], g.after[:, :], Dr[:].rearrange("p b n -> p (b n)"), start=True, stop=False)
                        pe.matmul(bank[5][:, :], g.identb[:, :], g.neg[:, :], start=False, stop=True)\
                            .then_inc(s["decay_done"], 1)
                    level_turn(5)
                    if A:
                        if B_:
                            pe.wait_ge(s["pt_done"], b(1, 1))
                        pe.matmul(bank[6][:, 256:512], g.after[:, :], Dq[:].rearrange("p b n -> p (b n)"), start=True, stop=False)
                        pe.matmul(bank[6][:, 256:512], g.identb[:, :], g.negq[:, :], start=False, stop=True)\
                            .then_inc(s["decay_done"], 1)
                    level_product(5)
                    proj(5, 0)
                    level_turn(6)
                    proj(5, 1)
                    if A:
                        natural(bank[2], K0, B, 1, ("wcopy_done", b(LV, LV)), u, a)
                    proj(5, 2)
                    level_product(6)
                    proj(5, 3)

                loops(pe, body)

            @block.scalar
            def _(act):
                act.wait_ge(s["ya_cleared"], 1)

                def body(act, n, u, A=True, B_=True, C=True):
                    a, b, c = at(n, 2), at(n, 1), at(n, 0)
                    v = (u + 1) % 2

                    def tap(o):
                        if A:
                            if o == 0:
                                act.wait_ge(g.cw_in, ((n + 2 >> 3) + 1) * 16)
                            act.wait_ge(s["proj_done"], a(NO, o + 1))
                            if o == 0:
                                wait(act, s["act_done"], a(3, 0))
                            act.activation(conv_out(o), proj_bank(o)[:, :, PAD:], ACT.Copy,
                                           scale=cw[:, o, PAD:TAPS]).then_inc(s["tap_done"], 1)

                    def decay_of_state(j):
                        if not C:
                            return
                        if j == 0:
                            act.wait_ge(dt_in[u], ((n >> 1) + 1) * 16)
                        if j % 2 == 0:
                            wait(act, s["scan_done"], c(2, j // 2 - 1))
                        k = (n & 15) * 4 + j
                        i = act.activation(da[:, j, 1:], dts[:, u, 0, 1:], ACT.Exp,
                                           scale=g.a_neg[:, k:k + 1] if isinstance(k, int) else g.a_neg[:, ds(k, 1)])
                        if j % 2 == 1:
                            i.then_inc(s["da_done"], 1)

                    def copies(l):
                        if not B_:
                            return
                        act.wait_ge(s["xm_done"], b(LV, l + 1))
                        if l == 0:
                            wait(act, s["rt_done"], b(1, 0))
                        act.activation(Wl[:], by_batch(bank[2]), ACT.Copy).then_inc(s["wcopy_done"], 1)
                        act.wait_ge(s["mt_done"], b(LV, l + 1))
                        act.activation(MT[:], by_batch(bank[3]), ACT.Copy).then_inc(s["mtcopy_done"], 1)

                    def tanh(part):
                        if not A:
                            return
                        lo, hi = PARTS[part]
                        act.wait_ge(s["conv_done"], a(NO, min(2 * part + 2, NO - 1)))
                        wait(act, s["act_done"], a(3, 0))
                        act.activation(th[:, lo:hi], cv[:, lo:hi], ACT.Tanh, scale=0.5).then_inc(s["tanh_done"], 1)

                    tap(0)
                    if C:
                        act.wait_ge(s["u_done"], c(1, 1))
                        wait(act, s["so_done"], c(2, 0))
                        act.activation(U[:], by_batch(bank[6]), ACT.Copy).then_inc(s["ucopy_done"], 1)
                    if B_:
                        act.wait_ge(s["turned"], b(2, 1))
                        wait(act, s["ks_done"], c(1, 0))
                        act.activation(KTr[:, v], by_batch(bank[2]), ACT.Copy).then_inc(s["kt_done"], 1)
                    if B_:
                        act.wait_ge(s["natural_done"], b(3, 3))
                        for q in range(2):
                            i = act.activation(junk[:, 4 + q], pairs(bank[4][:, 0:256])[:, q], ACT.Square,
                                               accum_out=ss[:, 4 + q:5 + q])
                        i.then_inc(s["ss_done"], 1)
                    for j in (0, 1):
                        decay_of_state(j)
                    if B_:
                        act.wait_ge(s["r_done"], b(2, 2))
                        for k in range(2):
                            for q in range(2):
                                i = act.activation(Qn[:, k, q], pairs(bank[4][:, 0:256])[:, q], ACT.Copy,
                                                   scale=rq[:, k, q:q + 1])
                        i.then_inc(s["qn_done"], 1)
                    for j in (2, 3):
                        decay_of_state(j)
                    if C:
                        act.wait_ge(s["so_done"], c(2, 2))
                        wait(act, s["orr_done"], c(1, 0))
                        for q in range(2):
                            i = act.activation(junk[:, 6 + q], pairs(bank[7][:, 0:256])[:, q], ACT.Square,
                                               accum_out=oss[:, q:q + 1])
                        i.then_inc(s["oss_done"], 1)
                    copies(0)
                    tap(1)
                    copies(1)
                    tap(2)
                    if C:
                        act.wait_ge(s["orr_done"], c(1, 1))
                        wait(act, s["ot_turned"], c(1, 0))
                        for q in range(2):
                            i = act.activation(On[:, q], pairs(bank[7][:, 0:256])[:, q], ACT.Copy, scale=orr[:, q:q + 1])
                        i.then_inc(s["on_done"], 1)
                    copies(2)
                    copies(3)
                    tanh(0)
                    copies(4)
                    tap(3)
                    copies(5)
                    tap(4)
                    if A:
                        act.wait_ge(s["decay_done"], a(2, 1))
                        wait(act, s["at_done"], b(1, 1) if B_ else 0)
                        act.activation(E_[:], by_batch(bank[5]), ACT.Exp).then_inc(s["e_done"], 1)
                        act.wait_ge(s["decay_done"], a(2, 2))
                        wait(act, s["pt_done"], b(1, 1) if B_ else 0)
                        act.activation(Eq[:], bank[6][:, 256:512].rearrange("p (b t) -> p b t", b=B), ACT.Exp)\
                            .then_inc(s["e_done"], 1)
                    tanh(1)
                    copies(6)
                    if A:
                        wait(act, s["r_done"], b(2, 2))
                        act.wait_ge(s["natural_done"], a(3, 1))
                        for q in range(B):
                            i = act.activation(junk[:, q], by_batch(bank[2])[:, q], ACT.Square, accum_out=ss[:, q:q + 1])
                        i.then_inc(s["ss_done"], 1)
                    tanh(2)
                    if A:
                        act.wait_ge(s["proj_done"], a(NO, NO))
                        wait(act, s["conv_done"], a(NO, 0))
                        act.activation(gt[:], proj_bank(5)[:, :, PAD:], ACT.Tanh, scale=0.5).then_inc(s["gtanh_done"], 1)

                loops(act, body)

            @block.vector
            def _(dve):
                def body(dve, n, u, A=True, B_=True, C=True):
                    a, b, c = at(n, 2), at(n, 1), at(n, 0)
                    v = (u + 1) % 2

                    def conv(o, *steps):
                        if not A:
                            return
                        for k in steps:
                            if k == 0:
                                dve.wait_ge(s["tap_done"], a(NO - 1, o + 1))
                            else:
                                dve.wait_ge(s["conv_link"], a(2 * (NO - 1), 2 * o + k))
                            dve.scalar_tensor_tensor(conv_out(o), proj_bank(o)[:, :, k:k + CT], cw[:, o, k:k + 1],
                                                     conv_out(o), ALU.mult, ALU.add)\
                                .then_inc(s["conv_link" if k < PAD - 1 else "conv_done"], 1)

                    def masked(l):
                        if B_:
                            wait_apart(dve, passed["dve"], s["x_done"], b(LV, l + 1))
                            mask = g.levels[:, l].rearrange("p (j s) -> p j s", s=1 << l).unsqueeze(1)\
                                .to_broadcast([P, B, CT >> l, 1 << l])
                            dve.copy_predicated(blocks(g.Xm[:, l], 0, 1 << l), mask, blocks(by_batch(bank[2]), 0, 1 << l))\
                                .then_inc(s["xm_done"], 1)

                    def activated(part):
                        if not A:
                            return
                        lo, hi = PARTS[part]
                        dve.wait_ge(s["tanh_done"], a(3, part + 1))
                        wait(dve, s["natural_done"], a(3, -3))
                        dve.scalar_tensor_tensor(kvq[:, u, lo:hi], th[:, lo:hi], 1.0, cv[:, lo:hi], ALU.add, ALU.mult)\
                            .then_inc(s["act_done"], 1)

                    def gate():
                        if A:
                            dve.wait_ge(s["gtanh_done"], a(1, 1))
                            dve.scalar_tensor_tensor(gs[:, u], gt[:], 1.0, proj_bank(5)[:, :, PAD:], ALU.add, ALU.mult)\
                                .then_inc(s["conv_done"], 1)

                    flat = lambda x: x.rearrange("p n l -> p (n l)")

                    def scan(h):
                        if not C:
                            return
                        two = slice(2 * h, 2 * h + 2)
                        dve.wait_ge(s["da_done"], c(2, h + 1))
                        if h == 0:
                            dve.wait_ge(s["bx_done"], c(1, 1))
                        dve.tensor_tensor_scan(flat(hs[:, two]), flat(da[:, two]), flat(hs[:, two]), 0.0, ALU.mult, ALU.add)\
                            .then_inc(s["scan_done"], 1)

                    def read_out():
                        if not C:
                            return
                        dve.wait_ge(s["scan_done"], c(2, 2))
                        dve.tensor_tensor(hs[:, 2:4], hs[:, 2:4], bcq[:, 1, 2:4], ALU.mult).then_inc(s["hc_done"], 1)

                    if C:
                        dve.wait_ge(s["ks_done"], c(1, 1))
                        wait(dve, s["u_done"], c(1, 0))
                        for q in range(B):
                            i = dve.scalar_tensor_tensor(F[:, q], by_batch(bank[5])[:, q], sc[:, u, 12 + q:13 + q],
                                                         Vb[:, u, q], ALU.mult, ALU.add)
                        i.then_inc(s["f_done"], 1)
                    if B_:
                        bc = lambda x: x.unsqueeze(2).to_broadcast([P, B, DH])
                        dve.wait_ge(s["rk_done"], b(1, 1))
                        wait(dve, s["turned"], b(2, 0))
                        wait(dve, s["kw_done"], b(1, 0))
                        dve.tensor_tensor(Kn[:], by_batch(bank[2]), bc(rr[:, 0:B]), ALU.mult).then_inc(s["kn_done"], 1)
                        dve.wait_ge(s["natural_done"], b(3, 2))
                        dve.tensor_tensor(Vb[:, v], by_batch(bank[3]), bc(sc[:, v, 8:12]), ALU.mult)\
                            .then_inc(s["kn_done"], 1)
                    conv(0, 0, 1, 2)
                    if B_:
                        dve.wait_ge(s["gram_done"], b(2, 1))
                        dve.wait_ge(s["e_done"], b(2, 1))
                        wait(dve, s["x_done"], b(LV, 0))
                        dve.scalar_tensor_tensor(At[:], by_batch(bank[3]), -1.0, E_[:], ALU.mult, ALU.mult)\
                            .then_inc(s["at_done"], 1)
                    masked(0)
                    if C:
                        dve.wait_ge(s["so_done"], c(2, 2))
                        for q in range(B):
                            i = dve.scalar_tensor_tensor(g.S[:, q], g.S[:, q], sc[:, u, 20 + q:21 + q],
                                                         by_batch(bank[5])[:, q], ALU.mult, ALU.add)
                        i.then_inc(s["s_done"], 1)
                    if B_:
                        dve.wait_ge(s["turned"], b(2, 2))
                        dve.tensor_copy(QTr[:, v].rearrange("p k q n -> p (k q) n"), by_batch(bank[4]))\
                            .then_inc(s["qt_done"], 1)
                    scan(0)
                    if B_:
                        dve.wait_ge(s["gram_done"], b(2, 2))
                        dve.wait_ge(s["e_done"], b(2, 2))
                        dve.tensor_tensor(PT[:, v], bank[6][:, 0:256].rearrange("p (b t) -> p b t", b=B), Eq[:],
                                          ALU.mult).then_inc(s["pt_done"], 1)
                    masked(1)
                    conv(1, 0, 1, 2)
                    masked(2)
                    conv(2, 0, 1, 2)
                    masked(3)
                    scan(1)
                    masked(4)
                    read_out()
                    if C:
                        dve.wait_ge(s["ot_turned"], c(1, 1))
                        wait(dve, out_dma[u], (n >> 1) * 16)
                        dve.scalar_tensor_tensor(OT[:, u], bank[7][:, 256:512].rearrange("p (b t) -> p b t", b=B),
                                                 g.normw[:, 0:1], gs[:, u], ALU.mult, ALU.mult).then_inc(s["ot_done"], 1)
                    masked(5)
                    conv(3, 0, 1, 2)
                    activated(0)
                    masked(6)
                    activated(1)
                    conv(4, 0, 1, 2)
                    if B_:
                        dve.wait_ge(s["rt_done"], b(1, 1))
                        wait(dve, s["u_done"], c(1, 0))
                        dve.tensor_tensor(Rf[:, v], by_batch(bank[4]), g.ident[:, :].unsqueeze(1).to_broadcast([P, B, CM]),
                                          ALU.add).then_inc(s["rcopy_done"], 1)
                    activated(2)
                    gate()

                dve.memset(da[:, :, 0:1], 0.0)
                dve.memset(ys[:], 0.0).then_inc(s["ya_cleared"], 1)
                loops(dve, body)


def combine(nc, g):
    NT = L // P
    with ExitStack() as ctx:
        sb = lambda name, shape, dt=F32: ctx.enter_context(nc.sbuf_tensor(name, shape, dt))
        pb = lambda name, shape, dt=F32: ctx.enter_context(nc.psum_tensor(name, shape, dt))
        sem = lambda name: ctx.enter_context(nc.semaphore(name))
        wo = sb("wo", [P, H, HID])
        gw = sb("gw", [P, KT, NE])
        ot = sb("ot", [P, 2, H, P])
        xr = sb("xr", [P, 2, HID])
        yr = sb("yr", [P, 2, 2, L])
        x1 = sb("x1", [P, NT, HID])
        st = sb("cst", [P, 2, NT, 6])
        mv = sb("cmv", [P, 2, NT, 2])
        rs = sb("crs", [P, 2, NT])
        z = sb("z", [P, NT, HID])
        zt = sb("zt", [P, NT, HID])
        yd = sb("yd", [P, NT, L])
        w = sb("w", [P, NT, L])
        x2 = sb("x2", [P, 2 * NT, HID])
        xh = sb("xh", [P, NT, HID])
        xhT = sb("xhT", [P, 2, NT, KT, P])
        mean = sb("mean", [P, NT, KT])
        msum = sb("msum", [P, KT])
        lg = sb("lg", [1, 8])
        top = sb("top", [1, 8])
        idx = sb("idx", [1, 8], U32)
        dl = sb("dl", [1, 8])
        pr = sb("pr", [1, 8])
        tot = sb("tot", [1, 4])
        wrow = sb("wrow", [1, 2, P])
        wcol = sb("wcol", [P, 2])
        w1 = sb("w1", [P, 2, KT, FF])
        w2 = sb("w2", [P, 2, len(FT), HID])
        b1 = sb("b1", [P, 2, len(FT)])
        b2 = sb("b2", [1, 2, HID])
        hT = sb("hT", [P, 2, len(FT), L])
        bb = sb("bb", [P, HID])
        res = sb("res", [P, 2, HID])
        bank = [pb(f"cbank{i}", [P, 512]) for i in range(8)]
        names = ("w_in", "wo_done", "x1_done", "var_done", "rs_done", "z_done", "zt_done", "yd_done", "w_done",
                 "wt_done", "x2_done", "var2_done", "rs2_done", "xh_done", "xht_done", "xhT_done", "mean_done",
                 "lg_done", "lg_copied", "dl_done", "pr_done", "wr_done", "wc_done", "wcol_done", "h_done",
                 "gelu_done", "hs_done", "b2_done", "bb_done", "x2b_done", "o_done", "res_done", "x_link",
                 "g_link", "pad_done", "expert_in", "s2_done")
        passed = {k: sem(f"c_passed_{k}") for k in ("sp", "pool", "dve")}
        s = {k: sem("c_" + k) for k in names}
        tile_in = [sem("tile_in0"), sem("tile_in1")]
        res_dma = [sem("res_dma0"), sem("res_dma1")]

        def run(eng, order, X1=None, X2=None, X3=None, G=None, Y1=None, Y2=None):
            go = lambda f, n, off: f and f(n + off, at(n, off))
            for f in (X1, X2, X3, G):
                go(f, 0, 0)
            step = lambda n, last: [go(f, n, off) for f, off in order if not (last and off)]
            step(0, False)
            with eng.Fori(1, B - 1) as n:
                step(n, False)
            step(B - 1, True)

        def half(m):
            return (m & 1) * NT

        def pick(a, start):
            return a[:, start] if isinstance(start, int) else a[:, ds(start, 1)].rearrange("p o n -> p (o n)")

        with nc.Block() as block:
            @block.sync
            def _(sp):
                sp.dma_start(wo[:], g.inputs["w_o"]).then_inc(s["w_in"], 16)
                sp.dma_start(gw[:], g.inputs["gate_w"]).then_inc(s["w_in"], 16)

                def X(m, v, tiles):
                    one = slice(m, m + 1) if isinstance(m, int) else ds(m, 1)
                    for t in tiles:
                        wait(sp, s["wo_done"], v(NT, t - 1))
                        wait(sp, s["x1_done"], v(NT, t - 1))
                        wait(sp, s["yd_done"], v(NT, t - 1))
                        u = t % 2
                        src = g.o_dram[:, :, one, t * P:(t + 1) * P]
                        sp.dma_start(ot[:, u], src.rearrange("h v b t -> v h (b t)")).then_inc(tile_in[u], 16)
                        sp.dma_start(xr[:, u], g.inputs["x"].rearrange("(b t p) d -> b t p d", b=B, p=P)[one, t]
                                     .rearrange("b p d -> p (b d)")).then_inc(tile_in[u], 16)
                        sp.dma_start(yr[:, u, 0], g.y_dram[one, t].rearrange("b p l -> p (b l)")).then_inc(tile_in[u], 16)
                        sp.dma_start(yr[:, u, 1], g.ud_dram[one, t].rearrange("b p l -> p (b l)")).then_inc(tile_in[u], 16)

                def G(m, v):
                    wait(sp, s["o_done"], v(NT, 0))
                    wait_apart(sp, passed["sp"], s["g_link"], v(9, 3))
                    for k in range(2):
                        e = sp.value_load(idx[0:1, k:k + 1], min_val=0, max_val=NE - 1)
                        one = ds(e, 1)
                        sp.dma_start(w1[:, k], g.inputs["w1"][one].rearrange("e p k n -> p (e k) n")).then_inc(s["expert_in"], 16)
                        sp.dma_start(w2[:, k], g.inputs["w2"][one].rearrange("e p k n -> p (e k) n")).then_inc(s["expert_in"], 16)
                        sp.dma_start(b1[:, k], g.inputs["b1"][one].rearrange("e p k -> p (e k)")).then_inc(s["expert_in"], 16)
                        sp.dma_start(b2[:, k], g.inputs["b2"][one]).then_inc(s["expert_in"], 16)

                def Y(m, v):
                    one = slice(m, m + 1) if isinstance(m, int) else ds(m, 1)
                    for t in range(NT):
                        sp.wait_ge(s["res_done"], v(NT, t + 1))
                        dst = g.out[one, t * P:(t + 1) * P, :].rearrange("b p d -> p (b d)")
                        sp.dma_start(dst, res[:, t % 2]).then_inc(res_dma[t % 2], 16)

                def step(n, loads):
                    X(n + 1, at(n, 1), (2, 3))
                    if loads:
                        X(n + 2, at(n, 2), (0, 1))
                    Y(n, at(n, 0))
                    G(n + 1, at(n, 1))

                X(0, at(0, 0), range(NT))
                X(1, at(0, 1), (0, 1))
                G(0, at(0, 0))
                step(0, True)
                with sp.Fori(1, B - 2) as n:
                    step(n, True)
                step(B - 2, False)
                Y(B - 1, at(B - 1, 0))
                for u in range(2):
                    sp.wait_ge(res_dma[u], 16 * B * NT // 2)

            @block.tensor
            def _(pe):
                pe.wait_ge(s["w_in"], 32)

                def X1(m, v):
                    for t in range(NT):
                        pe.wait_ge(tile_in[t % 2], v(128, 64 * (t // 2 + 1)))
                        wait(pe, s["x1_done"], v(NT, t - 1))
                        for h in range(H):
                            i = pe.matmul(bank[t % 2][:, :], ot[:, t % 2, h], wo[:, h], start=(h == 0), stop=(h == H - 1))
                        i.then_inc(s["wo_done"], 1)

                def X2(m, v):
                    pe.wait_ge(s["w_done"], v(NT, NT))
                    for t in range(NT):
                        wait(pe, s["x2_done"], v(NT, t - 1))
                        if t < 2:
                            wait(pe, s["xhT_done"], v(NT, t - 1))
                        for k in range(NT):
                            i = pe.transpose(bank[2 + t % 2][:, k * P:(k + 1) * P], w[:, k, t * P:(t + 1) * P], g.ident[:, :])
                        i.then_inc(s["wt_done"], 1)

                def X3(m, v):
                    for t in range(NT):
                        pe.wait_ge(s["xh_done"], v(NT, t + 1))
                        if t < 2:
                            pe.wait_ge(s["x2_done"], v(NT, t + 3))
                        else:
                            pe.wait_ge(s["xhT_done"], v(NT, t - 1))
                        for k in range(KT):
                            i = pe.transpose(bank[2 + t % 2][:, k * P:(k + 1) * P], xh[:, t, k * P:(k + 1) * P], g.ident[:, :])
                        i.then_inc(s["xht_done"], 1)

                def G(m, v):
                    pe.wait_ge(s["mean_done"], v(1, 1))
                    wait(pe, s["wcol_done"], v(1, 0))
                    for k in range(KT):
                        i = pe.matmul(bank[7][0:1, 0:NE], msum[:, k:k + 1], gw[:, k, :], start=(k == 0), stop=(k == KT - 1))
                    i.then_inc(s["lg_done"], 1)
                    pe.wait_ge(s["wr_done"], v(1, 1))
                    for k in range(2):
                        i = pe.matmul(bank[7][:, 8 + k:9 + k], wrow[:, k], g.ones[0:1, 0:1], start=True, stop=True)
                    i.then_inc(s["wc_done"], 1)

                def Y1(m, v):
                    pe.wait_ge(s["expert_in"], v(128, 128))
                    wait(pe, s["bb_done"], v(1, 0))
                    for k in range(2):
                        i = pe.matmul(bank[6][:, :], wrow[:, k], b2[:, k], start=(k == 0), stop=(k == 1))
                    i.then_inc(s["b2_done"], 1)
                    for j in range(2 * len(FT)):
                        k, f = divmod(j, len(FT))
                        lo, n = FT[f]
                        if j < 2:
                            wait(pe, s["res_done"], v(NT, 0))
                        else:
                            pe.wait_ge(s["gelu_done"], v(2 * len(FT), j - 1))
                        for q in range(KT):
                            start = (m & 1) * NT
                            rhs = xhT[:, m & 1, :, q] if isinstance(m, int) else \
                                xhT[:, ds(m & 1, 1), :, q].rearrange("p o t n -> p (o t) n")
                            i = pe.matmul(bank[4 + j % 2][0:n, :], w1[:, k, q, lo:lo + n], rhs, start=(q == 0), stop=(q == KT - 1))
                        i.then_inc(s["h_done"], 1)

                def Y2(m, v):
                    pe.wait_ge(s["hs_done"], v(2 * len(FT), 2 * len(FT)))
                    for t in range(NT):
                        if t > 1:
                            pe.wait_ge(s["res_done"], v(NT, t - 1))
                        for j in range(2 * len(FT)):
                            k, f = divmod(j, len(FT))
                            n = FT[f][1]
                            i = pe.matmul(bank[4 + t % 2][:, :], hT[0:n, k, f, t * P:(t + 1) * P], w2[0:n, k, f, :],
                                          start=(j == 0), stop=(j == 2 * len(FT) - 1))
                        i.then_inc(s["o_done"], 1)

                run(pe, [(X1, 1), (Y1, 0), (X2, 1), (Y2, 0), (X3, 1), (G, 1)], X1, X2, X3, G)

            @block.gpsimd
            def _(pool):
                def X1(m, v):
                    for t in range(NT):
                        pool.wait_ge(tile_in[t % 2], v(128, 64 * (t // 2 + 1)))
                        if t == 0:
                            wait(pool, s["w_done"], v(NT, 0))
                        pool.tensor_tensor(yd[:, t], yr[:, t % 2, 0], yr[:, t % 2, 1], ALU.add).then_inc(s["yd_done"], 1)
                    pool.wait_ge(s["var_done"], v(1, 1))
                    pool.tensor_tensor(rs[:, 0], rs[:, 0], g.mhalf[:, 0:NT], ALU.pow).then_inc(s["rs_done"], 1)

                def X2(m, v):
                    pool.wait_ge(s["var2_done"], v(1, 1))
                    pool.tensor_tensor(rs[:, 1], rs[:, 1], g.mhalf[:, 0:NT], ALU.pow).then_inc(s["rs2_done"], 1)

                def Y1(m, v):
                    wait_apart(pool, passed["pool"], s["bb_done"], v(1, 1))
                    for t in range(NT):
                        x = pick(x2, half(m) + t)
                        pool.tensor_tensor(x, x, bb[:, :], ALU.add).then_inc(s["x2b_done"], 1)

                run(pool, [(X1, 1), (Y1, 0), (X2, 1)], X1, X2)

            @block.scalar
            def _(act):
                def X1(m, v):
                    for t in range(NT):
                        act.wait_ge(s["z_done"], v(NT, t + 1))
                        act.activation(zt[:, t], z[:, t], ACT.Tanh, scale=0.5).then_inc(s["zt_done"], 1)

                def X3(m, v):
                    for t in range(NT):
                        act.wait_ge(s["xht_done"], v(NT, t + 1))
                        if t == 0:
                            wait(act, s["h_done"], v(2 * len(FT), -2 * len(FT)))
                        dst = xhT[:, m & 1, t] if isinstance(m, int) else \
                            xhT[:, ds(m & 1, 1), t].rearrange("p o k n -> p (o k) n")
                        act.activation(dst, bank[2 + t % 2][:, :].rearrange("p (k n) -> p k n", k=KT), ACT.Copy)\
                            .then_inc(s["xhT_done"], 1)

                def G(m, v):
                    act.wait_ge(s["dl_done"], v(1, 1))
                    act.activation(pr[:, :], dl[:, :], ACT.Exp, accum_out=tot[:, 0:1]).then_inc(s["pr_done"], 1)

                def Y1a(m, v):
                    act.wait_ge(s["b2_done"], v(1, 1))
                    wait(act, s["x2b_done"], v(NT, 0))
                    act.activation(bb[:, :], bank[6][:, :], ACT.Copy).then_inc(s["bb_done"], 1)
                    gelu(v, range(2))

                def Y1b(m, v):
                    gelu(v, range(2, 2 * len(FT)))

                def gelu(v, parts):
                    for j in parts:
                        k, f = divmod(j, len(FT))
                        n = FT[f][1]
                        act.wait_ge(s["h_done"], v(2 * len(FT), j + 1))
                        if j == 0:
                            wait(act, s["o_done"], v(NT, 0))
                        act.activation(hT[0:n, k, f, :], bank[4 + j % 2][0:n, :], ACT.Gelu, bias=b1[0:n, k, f:f + 1])\
                            .then_inc(s["gelu_done"], 1)

                run(act, [(Y1a, 0), (X1, 1), (Y1b, 0), (X3, 1), (G, 1)], X1, None, X3, G)

            @block.vector
            def _(dve):
                XL = 2 * (NT * 2)

                def norm(src, j, v, base):
                    for t in range(NT):
                        dve.bn_stats(st[:, j, t, :], src(t)).then_inc(s["x_link"], 1)
                        wait_apart(dve, passed["dve"], s["x_link"], v(XL, base + 2 * t + 1))
                        dve.bn_aggr(mv[:, j, t, :], st[:, j, t, :]).then_inc(s["x_link"], 1)
                    dve.wait_ge(s["x_link"], v(XL, base + 2 * NT))
                    dve.tensor_scalar(rs[:, j], mv[:, j, :, 1], EPS, None, ALU.add)\
                        .then_inc(s["var_done" if j == 0 else "var2_done"], 1)

                def X1(m, v):
                    for t in range(NT):
                        dve.wait_ge(s["wo_done"], v(NT, t + 1))
                        dve.tensor_tensor(x1[:, t], bank[t % 2][:, :], xr[:, t % 2], ALU.add).then_inc(s["x1_done"], 1)
                    wait_apart(dve, passed["dve"], s["x1_done"], v(NT, NT))
                    norm(lambda t: x1[:, t], 0, v, 0)
                    dve.wait_ge(s["rs_done"], v(1, 1))
                    for t in range(NT):
                        dve.tensor_scalar(z[:, t], x1[:, t], mv[:, 0, t, 0:1], rs[:, 0, t:t + 1],
                                          ALU.subtract, ALU.mult).then_inc(s["z_done"], 1)
                    for t in range(NT):
                        dve.wait_ge(s["zt_done"], v(NT, t + 1))
                        dve.scalar_tensor_tensor(z[:, t], zt[:, t], 1.0, z[:, t], ALU.add, ALU.mult)\
                            .then_inc(s["s2_done"], 1)
                    for t in range(NT):
                        dve.wait_ge(s["s2_done"], v(NT, t + 1))
                        dve.wait_ge(s["yd_done"], v(NT, t + 1))
                        if t == 0:
                            wait(dve, s["wt_done"], v(NT, 0))
                        dve.scalar_tensor_tensor(w[:, t], yd[:, t], 0.5, z[:, t], ALU.mult, ALU.mult)\
                            .then_inc(s["w_done"], 1)

                def X2(m, v):
                    for t in range(NT):
                        dve.wait_ge(s["wt_done"], v(NT, t + 1))
                        dve.tensor_tensor(pick(x2, half(m) + t), bank[2 + t % 2][:, :], x1[:, t], ALU.add)\
                            .then_inc(s["x2_done"], 1)
                    wait_apart(dve, passed["dve"], s["x2_done"], v(NT, NT))
                    norm(lambda t: pick(x2, half(m) + t), 1, v, 2 * NT)
                    dve.wait_ge(s["rs2_done"], v(1, 1))
                    wait(dve, s["xht_done"], v(NT, 0))
                    for t in range(NT):
                        dve.tensor_scalar(xh[:, t], pick(x2, half(m) + t), mv[:, 1, t, 0:1], rs[:, 1, t:t + 1],
                                          ALU.subtract, ALU.mult).then_inc(s["xh_done"], 1)

                def G(m, v):
                    def link(k, ins):
                        ins.then_inc(s["g_link"], 1)
                        wait_apart(dve, passed["dve"], s["g_link"], v(9, k))

                    dve.wait_ge(s["xhT_done"], v(NT, NT))
                    src = xhT[:, m & 1] if isinstance(m, int) else \
                        xhT[:, ds(m & 1, 1)].rearrange("p o t k n -> p (o t) k n")
                    link(1, dve.tensor_reduce(mean[:], src, AX.X, ALU.add))
                    wait(dve, s["lg_done"], v(1, 0))
                    dve.tensor_reduce(msum[:, :], mean[:].rearrange("p t k -> p k t"), AX.X, ALU.add)\
                        .then_inc(s["mean_done"], 1)
                    dve.wait_ge(s["lg_done"], v(1, 1))
                    wait(dve, s["expert_in"], v(128, 0))
                    link(2, dve.tensor_scalar(lg[:, 0:NE], bank[7][0:1, 0:NE], 1.0 / L, None, ALU.mult))
                    dve.max(top[:, :], lg[:, :]).then_inc(s["lg_copied"], 1)
                    wait_apart(dve, passed["dve"], s["lg_copied"], v(1, 1))
                    link(3, dve.max_index(idx[:, :], top[:, :], lg[:, :]))
                    dve.tensor_scalar(dl[:, :], top[:, :], top[:, 0:1], None, ALU.subtract).then_inc(s["dl_done"], 1)
                    dve.wait_ge(s["pr_done"], v(1, 1))
                    link(4, dve.reciprocal(tot[:, 1:2], tot[:, 0:1]))
                    link(5, dve.tensor_scalar(pr[:, :], pr[:, :], tot[:, 1:2], None, ALU.mult))
                    link(6, dve.tensor_tensor(tot[:, 2:3], pr[:, 0:1], pr[:, 1:2], ALU.add))
                    link(7, dve.reciprocal(tot[:, 3:4], tot[:, 2:3]))
                    link(8, dve.tensor_scalar(pr[:, 0:2], pr[:, 0:2], tot[:, 3:4], None, ALU.mult))
                    wait(dve, s["b2_done"], v(1, 0))
                    dve.tensor_copy(wrow[:], pr[:, 0:2].unsqueeze(2).to_broadcast([1, 2, P])).then_inc(s["wr_done"], 1)
                    dve.wait_ge(s["wc_done"], v(1, 1))
                    link(9, dve.tensor_copy(wcol[:, :], bank[7][:, 8:10]))
                    dve.nop().then_inc(s["wcol_done"], 1)

                def Y1(m, v):
                    for j in range(2 * len(FT)):
                        k, f = divmod(j, len(FT))
                        n = FT[f][1]
                        dve.wait_ge(s["gelu_done"], v(2 * len(FT), j + 1))
                        dve.tensor_scalar(hT[0:n, k, f, :], hT[0:n, k, f, :], wcol[0:n, k:k + 1], None, ALU.mult)\
                            .then_inc(s["hs_done"], 1)

                def Y2(m, v):
                    for t in range(NT):
                        dve.wait_ge(s["o_done"], v(NT, t + 1))
                        dve.wait_ge(s["x2b_done"], v(NT, t + 1))
                        wait(dve, res_dma[t % 2], v(32, 16 * (t // 2)))
                        dve.tensor_tensor(res[:, t % 2], bank[4 + t % 2][:, :], pick(x2, half(m) + t), ALU.add)\
                            .then_inc(s["res_done"], 1)

                dve.memset(lg[:, :], -1e30).then_inc(s["pad_done"], 1)
                dve.wait_ge(s["pad_done"], 1)
                run(dve, [(X1, 1), (Y1, 0), (X2, 1), (Y2, 0), (G, 1)], X1, X2, None, G)


class Shared:

    def __init__(self, inputs):
        self.inputs = inputs


def build(nc, arrays, out):
    g = Shared(arrays)
    g.log1p = log1p_coefficients()
    g.log1p_factors = log1p_factors()
    g.ln2 = 0.6931471805599453
    g.out = out
    internal = lambda name, shape: nc.dram_tensor(name, shape, F32, kind="Internal").ap()
    g.dts_dram = internal("dts_scratch", (B, DT, 2, P, L))
    g.ud_dram = internal("ud_scratch", (B, DT, P, L))
    g.bc_dram = internal("bc_scratch", (B, 2 * DS, L))
    g.y_dram = internal("y_scratch", (B, DT, P, L))
    g.o_dram = nc.dram_tensor("o_scratch", (H, DH, B, L), F32, kind="Internal").ap()
    with ExitStack() as ctx:
        sb = lambda name, shape, dt=F32: ctx.enter_context(nc.sbuf_tensor(name, shape, dt))
        g.ident = sb("ident", [P, P])
        g.identb = sb("identb", [P, P], BF16)
        g.ones = sb("ones", [P, P])
        g.mhalf = sb("mhalf", [P, NTT])
        with ExitStack() as inner:
            sb = lambda name, shape, dt=F32: inner.enter_context(nc.sbuf_tensor(name, shape, dt))
            g.upto = sb("upto", [P, CM])
            g.after = sb("after", [P, CM])
            g.neg = sb("neg", [P, B * CM], BF16)
            g.negq = sb("negq", [P, B * CT], BF16)
            g.levels = sb("levels", [P, LV, CT], U32)
            g.normw = sb("normw", [P, 1])
            g.xT = sb("xT", [P, KT, B, TW])
            g.tab = sb("tab", [P, NIT, 27])
            g.a_neg = sb("a_neg", [P, DT * DS])
            g.Xm = sb("Xm", [P, LV, B, CM])
            g.S = sb("S", [P, B, DH])
            g.W = sb("W", [P, NO, KT, P])
            g.cw = sb("cw", [P, NO - 1, TAPS])
            sem = lambda name: inner.enter_context(nc.semaphore(name))
            g.w_in, g.cw_in = [sem(f"w_in{o}") for o in range(NO)], sem("cw_in")
            g.proj_done, g.conv_done = sem("proj_done"), sem("conv_done")
            with ExitStack() as loaded:
                weights = StateWeights(loaded, nc)
                prepare(nc, g, weights)
                state_inputs(nc, g, weights)
            delta(nc, g)
        combine(nc, g)


def constants():
    import numpy as np
    i = np.arange(P)
    levels = np.zeros((P, LV, CT), np.uint32)
    for l in range(LV):
        s = 1 << l
        levels[:, l, :] = (i[:, None] // (2 * s) == i[None, :CT] // s) & (i[:, None] // s % 2 == 1)
    neg = np.where(i[:, None] >= i[None, :], -30000.0, 0.0)
    negq = np.where(i[:, None] > 2 * np.arange(CT)[None, :] + 1, -30000.0, 0.0)
    first = np.ones((P, NIT), np.float32)
    first[:, ::NC] = 0
    flag = np.tile((np.arange(NIT) // 4 % 4 != 0).astype(np.float32), (P, 1))
    return dict(
        c_ident=np.eye(P, dtype=np.float32),
        c_ones=np.ones((P, P), np.float32),
        c_upto=(i[:, None] <= i[None, :]).astype(np.float32), c_after=(i[:, None] > i[None, :]).astype(np.float32),
        c_neg=neg.astype(np.float32), c_negq=negq.astype(np.float32),
        c_levels=levels, c_parity=np.stack([i % 2 == 0, i % 2 == 1], 1).astype(np.float32), c_first=first, c_flag=flag)


def laid_out(v):
    import numpy as np
    f = {k: np.asarray(a) for k, a in v.items()}
    per_head = lambda w: w.reshape(KT, P, -1, P).transpose(2, 1, 0, 3)
    a = "L0_attn_"
    q, k, vv, gg = (per_head(f[a + n]) for n in ("Wq", "Wk", "Wv", "Wg"))
    heads = np.stack([k[:H], k[H:], vv[:H], vv[H:], q, gg], 2)
    cq, ck, cvw = (f[a + n].reshape(-1, P, TAPS) for n in ("conv_q_w", "conv_k_w", "conv_v_w"))
    convs = np.stack([ck[:H], ck[H:], cvw[:H], cvw[H:], cq], 2)
    out = dict(
        x=f["x"].reshape(B * L, HID), w_heads=heads.reshape(H, P, -1), conv_heads=convs.reshape(H, P, -1),
        w_gates=np.concatenate([f[a + "Wb"], f[a + "Wa"]], 1).reshape(KT, P, NG).transpose(1, 0, 2),
        dt_bias=f[a + "dt_bias"], a_log=f[a + "A_log"], norm_w=f[a + "norm_w"].reshape(P, 1),
    )
    m = "L0_xattn_"
    tiles = lambda w: w.reshape(DT, P, -1).transpose(1, 0, 2)
    out.update(
        ctxT=f["ctx_1024"].reshape(B * L, CTXT, P).transpose(2, 1, 0),
        in_w=f[m + "in_proj_w"].T.reshape(CTXT, P, DI).transpose(1, 0, 2),
        s_conv=tiles(f[m + "conv_w"]), s_convb=f[m + "conv_b"].reshape(DT, P).T,
        x_w=tiles(f[m + "x_proj_w"].T), dt_w=f[m + "dt_proj_w"].T, dt_b=f[m + "dt_proj_b"].reshape(DT, P).T,
        s_d=f[m + "D"].reshape(DT, P).T, s_alog=tiles(f[m + "A_log"]).reshape(P, DT, 4, 4).transpose(0, 2, 1, 3).reshape(P, -1),
    )
    e = "L0_ffn_"
    pad = len(FT) * P - FF
    out.update(
        w_o=f[a + "Wo"].reshape(H, DH, HID).transpose(1, 0, 2), gate_w=f[e + "gate_W"].T.reshape(KT, P, NE).transpose(1, 0, 2),
        w1=f[e + "W1"].reshape(NE, KT, P, FF).transpose(0, 2, 1, 3),
        w2=np.pad(f[e + "W2"], ((0, 0), (0, pad), (0, 0))).reshape(NE, len(FT), P, HID).transpose(0, 2, 1, 3),
        b1=np.pad(f[e + "b1"], ((0, 0), (0, pad))).reshape(NE, len(FT), P).transpose(0, 2, 1), b2=f[e + "b2"],
    )
    out.update(constants())
    return {n: np.ascontiguousarray(x) for n, x in out.items()}


def kernel(**inputs):
    import concourse.bacc as bacc
    import numpy as np
    from concourse.bass_utils import run_bass_kernel_spmd

    nc = bacc.Bacc("TRN2", target_bir_lowering=False, num_devices=1)
    arrays = laid_out(inputs)
    aps = {n: nc.dram_tensor("in_" + n, x.shape, mybir.dt.from_np(x.dtype), kind="ExternalInput").ap()
           for n, x in arrays.items()}
    out = nc.dram_tensor("out", (B, L, HID), F32, kind="ExternalOutput").ap()
    build(nc, aps, out)
    r = run_bass_kernel_spmd(nc, [{"in_" + n: x for n, x in arrays.items()}], core_ids=[0])
    return r.results[0]["out"]
```
